# Optimizing a Trainium2 kernel written in Bass

```python
import numpy as np
import jax
import jax.numpy as jnp

def _softmax(x, axis=-1):
    return jax.nn.softmax(x, axis=axis)

def _gelu(x):
    return jax.nn.gelu(x, approximate=True)

def _silu(x):
    return jax.nn.silu(x)

def _sigmoid(x):
    return jax.nn.sigmoid(x)

def _layernorm(x, axis=-1, eps=1e-05):
    m = jnp.mean(x, axis=axis, keepdims=True)
    v = jnp.var(x, axis=axis, keepdims=True)
    return (x - m) / jnp.sqrt(v + eps)

def _scatter_add(tgt, idx, src, axis=0):
    return tgt.at[idx].add(src)

def _segment_sum(src, seg, n):
    return jax.ops.segment_sum(src, seg, n)
kernel_name = 'mk_seq_preln_d2_jaxref_r8_aef635'

def setup_inputs(seed: int=0):
    np.random.seed(seed)
    _w = jnp.asarray

    def _L0_attn_setup():
        import jax, jax.numpy as jnp
        import numpy as np
        BH = 32
        BW = 32
        key = jax.random.key(seed)
        k1, k2, k3, k4 = jax.random.split(key, 4)
        B, S, K, N = (2, 256, 512, 512)
        data = jax.random.normal(k1, (B, S, K), dtype=jnp.float32)
        weight = jax.random.normal(k2, (N, K), dtype=jnp.float32) * 0.02
        bias = jax.random.normal(k3, (N,), dtype=jnp.float32) * 0.02
        Nb, Kb = (N // BH, K // BW)
        block_on = jax.random.uniform(k4, (Nb, Kb)) < 0.3
        mask = jnp.repeat(jnp.repeat(block_on, BH, axis=0), BW, axis=1).astype(jnp.int32)
        return {'data': data, 'mask': mask, 'weight': weight, 'bias': bias}
    _L0_attn_in = _L0_attn_setup()

    def _L0_ffn_setup():
        import jax, jax.numpy as jnp
        import numpy as np
        K_TOP = 8
        key = jax.random.key(seed)
        k1, k2, k3 = jax.random.split(key, 3)
        B, S, H, E = (4, 512, 512, 64)
        hidden_states = jax.random.normal(k1, (B, S, H), dtype=jnp.float32)
        router_weight = jax.random.normal(k2, (E, H), dtype=jnp.float32)
        router_bias = jnp.zeros((E,), dtype=jnp.float32)
        expert_bias = jax.random.normal(k3, (E, H), dtype=jnp.float32) * 0.1
        return {'hidden_states': hidden_states, 'router_weight': router_weight, 'router_bias': router_bias, 'expert_bias': expert_bias}
    _L0_ffn_in = _L0_ffn_setup()

    def _L1_attn_setup():
        import jax, jax.numpy as jnp
        import numpy as np
        B, S, HID = (1, 256, 512)
        H, HK, D = (32, 8, 128)
        L = D // 4
        key = jax.random.key(seed)
        ks = jax.random.split(key, 7)
        s = 0.02
        return {'hidden_states': jax.random.normal(ks[0], (B, S, HID), jnp.float32), 'Wq': jax.random.normal(ks[1], (H * D, HID), jnp.float32) * s, 'Wk_down': jax.random.normal(ks[2], (HK * L, HID), jnp.float32) * s, 'Wv_down': jax.random.normal(ks[3], (HK * L, HID), jnp.float32) * s, 'Wk_up': jax.random.normal(ks[4], (HK * D, HK * L), jnp.float32) * s, 'Wv_up': jax.random.normal(ks[5], (HK * D, HK * L), jnp.float32) * s, 'Wo': jax.random.normal(ks[6], (HID, H * D), jnp.float32) * s}
    _L1_attn_in = _L1_attn_setup()

    def _L1_ffn_setup():
        import jax, jax.numpy as jnp
        import numpy as np
        HIDDEN = 512
        INTER = 1376
        BATCH, SEQ = (2, 256)

        def _ternary(key, shape):
            return jax.random.randint(key, shape, -1, 2).astype(jnp.float32)
        key = jax.random.key(seed)
        kx, kg, ku, kd = jax.random.split(key, 4)
        x = jax.random.normal(kx, (BATCH, SEQ, HIDDEN), dtype=jnp.float32)
        gate_w = _ternary(kg, (INTER, HIDDEN))
        up_w = _ternary(ku, (INTER, HIDDEN))
        down_w = _ternary(kd, (HIDDEN, INTER))
        gate_scale = jnp.float32(0.02)
        up_scale = jnp.float32(0.02)
        down_scale = jnp.float32(0.02)
        return {'x': x, 'gate_w': gate_w, 'up_w': up_w, 'down_w': down_w, 'gate_scale': gate_scale, 'up_scale': up_scale, 'down_scale': down_scale}
    _L1_ffn_in = _L1_ffn_setup()
    _d = {'L0_attn_data': _L0_attn_in['data'], 'L0_attn_mask': _L0_attn_in['mask'], 'L0_attn_weight': _L0_attn_in['weight'], 'L0_attn_bias': _L0_attn_in['bias'], 'L0_ffn_router_weight': _L0_ffn_in['router_weight'], 'L0_ffn_router_bias': _L0_ffn_in['router_bias'], 'L0_ffn_expert_bias': _L0_ffn_in['expert_bias'], 'L1_attn_Wq': _L1_attn_in['Wq'], 'L1_attn_Wk_down': _L1_attn_in['Wk_down'], 'L1_attn_Wv_down': _L1_attn_in['Wv_down'], 'L1_attn_Wk_up': _L1_attn_in['Wk_up'], 'L1_attn_Wv_up': _L1_attn_in['Wv_up'], 'L1_attn_Wo': _L1_attn_in['Wo'], 'L1_ffn_gate_w': _L1_ffn_in['gate_w'], 'L1_ffn_up_w': _L1_ffn_in['up_w'], 'L1_ffn_down_w': _L1_ffn_in['down_w'], 'L1_ffn_gate_scale': _L1_ffn_in['gate_scale'], 'L1_ffn_up_scale': _L1_ffn_in['up_scale'], 'L1_ffn_down_scale': _L1_ffn_in['down_scale']}
    _x0 = _d['L0_attn_data']
    _d['L0_attn_data'] = jax.random.normal(jax.random.fold_in(jax.random.key(seed), 1), (8, 256, 512), dtype=_x0.dtype)
    del _x0
    return _d

def reference(L0_attn_data, L0_attn_mask, L0_attn_weight, L0_attn_bias, L0_ffn_router_weight, L0_ffn_router_bias, L0_ffn_expert_bias, L1_attn_Wq, L1_attn_Wk_down, L1_attn_Wv_down, L1_attn_Wk_up, L1_attn_Wv_up, L1_attn_Wo, L1_ffn_gate_w, L1_ffn_up_w, L1_ffn_down_w, L1_ffn_gate_scale, L1_ffn_up_scale, L1_ffn_down_scale):

    def _L0_attn_ref(data, mask, weight, bias):
        import jax, jax.numpy as jnp
        import numpy as np
        BH = 32
        BW = 32
        N, K = weight.shape
        Nb, Kb = (N // BH, K // BW)
        bm = mask.reshape(Nb, BH, Kb, BW).sum(axis=(1, 3)) > 0
        wb = weight.reshape(Nb, BH, Kb, BW) * bm[:, None, :, None].astype(weight.dtype)
        w = wb.reshape(N, K)
        out = jnp.einsum('bsk,nk->bsn', data, w) + bias
        return out

    def _L0_ffn_ref(hidden_states, router_weight, router_bias, expert_bias):
        import jax, jax.numpy as jnp
        import numpy as np
        K_TOP = 8
        B, S, H = hidden_states.shape
        E = router_weight.shape[0]
        T = B * S
        flat = hidden_states.reshape(T, H)
        logits = jnp.einsum('th,eh->te', flat, router_weight) + router_bias
        scores = jax.nn.softmax(logits, axis=-1)
        topk_w, topk_idx = jax.lax.top_k(scores, K_TOP)
        w_sum = topk_w.sum(axis=-1, keepdims=True)
        w_dense = jnp.zeros((T, E), dtype=scores.dtype).at[jnp.arange(T)[:, None], topk_idx].add(topk_w)
        bias_mix = jnp.einsum('te,eh->th', w_dense, expert_bias)
        out = flat * w_sum + bias_mix
        return out.reshape(B, S, H)

    def _L1_attn_ref(hidden_states, Wq, Wk_down, Wv_down, Wk_up, Wv_up, Wo):
        import jax, jax.numpy as jnp
        import numpy as np
        B, S, HID = (1, 256, 512)
        H, HK, D = (32, 8, 128)
        L = D // 4
        b, s, _ = hidden_states.shape
        q = (hidden_states @ Wq.T).reshape(b, s, H, D).transpose(0, 2, 1, 3)
        kc = (hidden_states @ Wk_down.T).reshape(b, s, HK, L).transpose(0, 2, 1, 3)
        vc = (hidden_states @ Wv_down.T).reshape(b, s, HK, L).transpose(0, 2, 1, 3)
        lat = jnp.concatenate([kc, vc], axis=-1).reshape(b, s, HK * 2 * L)
        k_cmp, v_cmp = jnp.split(lat, 2, axis=-1)
        k = (k_cmp @ Wk_up.T).reshape(b, s, HK, D).transpose(0, 2, 1, 3)
        v = (v_cmp @ Wv_up.T).reshape(b, s, HK, D).transpose(0, 2, 1, 3)
        n_rep = H // HK
        k = jnp.repeat(k, n_rep, axis=1)
        v = jnp.repeat(v, n_rep, axis=1)
        scale = 1.0 / jnp.sqrt(jnp.asarray(D, hidden_states.dtype))
        scores = jnp.einsum('bhqd,bhkd->bhqk', q, k) * scale
        causal = jnp.tril(jnp.ones((s, s), dtype=bool))
        scores = jnp.where(causal, scores, jnp.asarray(-1000000000.0, scores.dtype))
        attn = jax.nn.softmax(scores, axis=-1)
        out = jnp.einsum('bhqk,bhkd->bhqd', attn, v)
        out = out.transpose(0, 2, 1, 3).reshape(b, s, H * D)
        return out @ Wo.T

    def _L1_ffn_ref(x, gate_w, up_w, down_w, gate_scale, up_scale, down_scale):
        import jax, jax.numpy as jnp
        import numpy as np
        HIDDEN = 512
        INTER = 1376
        BATCH, SEQ = (2, 256)

        def _ternary(key, shape):
            return jax.random.randint(key, shape, -1, 2).astype(jnp.float32)
        gate = jnp.einsum('bsh,ih->bsi', x, gate_w) * gate_scale
        up = jnp.einsum('bsh,ih->bsi', x, up_w) * up_scale
        inter = jax.nn.silu(gate) * up
        out = jnp.einsum('bsi,hi->bsh', inter, down_w) * down_scale
        return out
    x = L0_attn_data
    x = x + _L0_attn_ref(_layernorm(x, axis=-1), L0_attn_mask, L0_attn_weight, L0_attn_bias)
    x = x + _L0_ffn_ref(_layernorm(x, axis=-1), L0_ffn_router_weight, L0_ffn_router_bias, L0_ffn_expert_bias)
    x = x + _L1_attn_ref(_layernorm(x, axis=-1), L1_attn_Wq, L1_attn_Wk_down, L1_attn_Wv_down, L1_attn_Wk_up, L1_attn_Wv_up, L1_attn_Wo)
    x = x + _L1_ffn_ref(_layernorm(x, axis=-1), L1_ffn_gate_w, L1_ffn_up_w, L1_ffn_down_w, L1_ffn_gate_scale, L1_ffn_up_scale, L1_ffn_down_scale)
    return x

_drawn_inputs = setup_inputs


def setup_inputs(seed=0):
    import zlib

    import numpy as np

    out = dict(_drawn_inputs(seed))
    spreads = {'L0_ffn_router_bias': (0.0, 0.8)}
    factors = {'L0_attn_bias': 2.882,
     'L1_attn_Wq': 8.0,
     'L1_attn_Wk_down': 5.614,
     'L1_attn_Wv_down': 5.745,
     'L1_attn_Wk_up': 8.0,
     'L1_attn_Wv_up': 3.996,
     'L1_attn_Wo': 3.992,
     'L1_ffn_gate_w': 19.719,
     'L1_ffn_up_w': 6.836,
     'L1_ffn_down_w': 6.833}
    for name, (base, spread) in spreads.items():
        noise = np.random.default_rng([zlib.crc32(name.encode()), seed]).standard_normal(out[name].shape)
        drawn = base * np.exp(spread * noise) if base else spread * noise
        out[name] = jnp.asarray(drawn.astype(out[name].dtype))
    for name, factor in factors.items():
        out[name] = (out[name] * factor).astype(out[name].dtype)
    return out
```

```python
from contextlib import ExitStack

import concourse.bass as bass
from concourse import mybir

F32 = mybir.dt.float32
F32R = mybir.dt.float32r
I32 = mybir.dt.int32
ALU = mybir.AluOpType
ACT = mybir.ActivationFunctionType
AX_X = mybir.AxisListType.X

P = 128
HID = 512
KC = HID // P
BATCH, SEQ = 8, 256
TOKENS = BATCH * SEQ
TILES = TOKENS // P
EXPERTS = 64
BLOCK = 32
EPS = 1e-5

KV_HEADS = 8
GROUP = 4
HEAD = 128
LATENT = 32
PAIRS = BATCH // 2
PAIR = 2 * SEQ
KV_DOWN, KV_UP = KC * 2 * KV_HEADS * LATENT, 2 * KV_HEADS * HEAD
KV_PIECE = (KV_DOWN + 2 * KV_UP) // TILES
SCALE = float(HEAD) ** -0.5
MASKED = -1.0e30

INTER = 1376
CHUNKS = -(-INTER // P)
GROUPS = TILES // 4

HI, LO = 0, 1
PASSES = ((HI, HI), (LO, HI), (HI, LO))


def known(t):
    return isinstance(t, int)


def skewed(eng, depth, body):
    first = depth + depth % 2 + 2
    for i in range(first):
        body(i, i % 2, lambda k, i=i: i - k >= 0)
    with eng.Fori(first // 2, TILES // 2) as j:
        for par in range(2):
            body(2 * j + par, par, lambda k: True)
    for i in range(TILES, TILES + depth):
        body(i, i % 2, lambda k, i=i: i - k < TILES)


class LayerNorm:

    def __init__(self, sb, sem, name, half, ready):
        self.bn = sb(f"bn_{name}", [P, 2, 6])
        self.mv = sb(f"mv_{name}", [P, 2, 2])
        self.neg_mean = sb(f"neg_mean_{name}", [P, TILES])
        self.ve = sb(f"ve_{name}", [P, TILES])
        self.factors = sb(f"factors_{name}", [P, TILES, 2])
        self.half = half
        self.ready = ready
        self.bn_done = sem(f"bn_done_{name}")
        self.mv_done = sem(f"mv_done_{name}")
        self.ve_done = sem(f"ve_done_{name}")
        self.rstd_done = sem(f"rstd_done_{name}")
        self.shift_done = sem(f"shift_done_{name}")

    def stats(self, dve, src, t, par):
        dve.bn_stats(self.bn[:, par, :], src).then_inc(self.bn_done, 1)

    def aggregate(self, dve, t, par):
        wait_alone(dve, self.bn_done, t + 1, self.ready)
        dve.bn_aggr(self.mv[:, par, :], self.bn[:, par, :]).then_inc(self.mv_done, 1)

    def variance(self, dve, t, par):
        dve.wait_ge(self.mv_done, t + 1)
        dve.tensor_scalar(self.neg_mean[:, bass.ds(t, 1)], self.mv[:, par, 0:1], -1.0, None, ALU.mult)
        dve.tensor_scalar(self.ve[:, bass.ds(t, 1)], self.mv[:, par, 1:2], EPS, None, ALU.add).then_inc(self.ve_done, 1)

    def power(self, pool, t):
        pool.wait_ge(self.ve_done, t + 1)
        pool.tensor_tensor(self.factor(t, 0), self.ve[:, bass.ds(t, 1)], self.half, ALU.pow).then_inc(self.rstd_done, 1)
        pool.wait_ge(self.rstd_done, t + 1)
        pool.tensor_tensor(self.factor(t, 1), self.neg_mean[:, bass.ds(t, 1)], self.factor(t, 0), ALU.mult).then_inc(self.shift_done, 1)

    def factor(self, t, n):
        return self.factors[:, bass.ds(t, 1), n:n + 1].rearrange("p t n -> p (t n)")

    def apply(self, dve, out, src, t):
        dve.wait_ge(self.shift_done, t + 1)
        return dve.tensor_scalar(out, src, self.factor(t, 0), self.factor(t, 1), ALU.mult, ALU.add)

    def activate(self, act, out, src, t):
        act.wait_ge(self.shift_done, t + 1)
        return act.activation(out, src, ACT.Identity, bias=self.factor(t, 1), scale=self.factor(t, 0))


def wait_alone(eng, done, value, ready):
    if not known(value):
        eng.lower_val(value)
    eng.wait_ge(ready, 1)
    eng.wait_ge(done, value)


def tile_of(x, t):
    return x[:, bass.ds(t, 1), :].rearrange("p a f -> p (a f)")


def hi_part(act, parts, src):
    return act.activation(parts[HI], src, ACT.Copy)


def lo_part(dve, parts, src):
    return dve.tensor_tensor(parts[LO], src, parts[HI].bitcast(F32), ALU.subtract)


def build(nc, x_in, mask_t, w0_t, bias0, router_t, router_bias, expert_bias, kv_weights,
          wq_g, wo_g, gate_c, up_c, down_c, scales, out):
    whole = ExitStack()

    def sem(name):
        return whole.enter_context(nc.semaphore(name))

    def sb(name, shape, dt=F32, stack=whole):
        return stack.enter_context(nc.sbuf_tensor(name, shape, dt))

    def ps(name, shape, stack):
        return stack.enter_context(nc.psum_tensor(name, shape, F32))

    def split(name, shape, stack=whole):
        return [sb(name + "_hi", shape, F32R, stack), sb(name + "_lo", shape, F32R, stack)]

    k_scr = nc.dram_tensor("k_scratch", [KV_HEADS, 2, P, TOKENS], F32, kind="Internal").ap()
    v_scr = nc.dram_tensor("v_scratch", [KV_HEADS, PAIRS, 2, P, 4, HEAD], F32, kind="Internal").ap()

    with whole:
        x = sb("x", [P, TILES, HID])
        ident = sb("ident", [P, P])
        half = sb("half", [P, 1])
        consts = sem("consts")
        ln = [LayerNorm(sb, sem, f"ln{n}", half[:, 0:1], consts) for n in range(4)]

        with ExitStack() as held:
            h3 = split("h3", [P, KC, TOKENS], held)
            with ExitStack() as held_weights:
                kv_w = split("kv_w", [P, TILES, KV_PIECE], held_weights)
                with ExitStack() as held_router:
                    router = RouterWeights(sb, sem, held_router)
                    block_sparse_linear(nc, sem, sb, ps, split, x, ident, half, consts, ln[0], x_in, mask_t, w0_t, bias0,
                                        lambda eng: router.load(eng, router_t, router_bias, expert_bias), kv_weights, kv_w)
                    routed_bias(nc, sem, sb, ps, split, x, ident, ln[1], router)
                normalize_for_attention(nc, sem, sb, ps, x, ident, ln[2], h3)
                keys_and_values(nc, sem, sb, ps, split, ident, h3, kv_w, k_scr, v_scr)
            attention(nc, sem, sb, ps, split, x, ident, h3, wq_g, wo_g, k_scr, v_scr)
        feed_forward(nc, sem, sb, ps, split, x, ident, ln[3], gate_c, up_c, down_c, scales, out)


def block_sparse_linear(nc, sem, sb, ps, split, x, ident, half, consts, ln, x_in, mask_t, w0_t, bias0, load_next, kv_weights, kv_w):
    with ExitStack() as st:
        mask = sb("mask", [P, KC, HID], I32, st)
        w_raw = sb("w0_raw", [P, KC, HID], F32, st)
        w0 = split("w0", [P, KC, HID], st)
        bias = sb("bias0", [P, HID], F32, st)
        same_block = sb("same_block", [P, P], F32, st)
        row_sums = sb("row_sums", [P, KC * HID // BLOCK], F32, st)
        block_on = sb("block_on", [P, KC * HID // BLOCK], F32, st)
        h = sb("h0", [P, 2, HID], F32, st)
        ht = [split(f"h0t{n}", [P, KC, P], st) for n in range(2)]
        kv_raw = sb("kv_raw", [P, 2, KV_PIECE], F32, st)
        ps_t = ps("a_ps_t", [P, 2, HID], st)
        ps_y = ps("a_ps_y", [P, 2, HID], st)
        ps_b = ps("a_ps_b", [P, HID], st)

        x_loaded = [sem(f"a_x_loaded{n}") for n in range(2)]
        mask_loaded, w_loaded, bias_loaded = sem("a_mask_loaded"), sem("a_w_loaded"), sem("a_bias_loaded")
        block_zeroed = sem("a_block_zeroed")
        zeroed, const_done = sem("a_zeroed"), sem("a_const_done")
        rows_done, blocks_done, on_done, masked = sem("a_rows_done"), sem("a_blocks_done"), sem("a_on_done"), sem("a_masked")
        w_hi_done, w_lo_done = sem("a_w_hi_done"), sem("a_w_lo_done")
        h_done, t_done, hi_done, lo_done = sem("a_h_done"), sem("a_t_done"), sem("a_hi_done"), sem("a_lo_done")
        y_done, xb_done, x_done = sem("a_y_done"), sem("a_xb_done"), sem("a_x_done")
        kv_loaded = [sem(f"a_kv_loaded{n}") for n in range(2)]
        kv_hi, kv_lo = sem("a_kv_hi"), sem("a_kv_lo")

        with nc.Block() as block:
            @block.sync
            def _(sp):
                def load(t, par):
                    if not known(t) or t >= 2:
                        sp.wait_ge(x_loaded[par], 8 * (t - par))
                    sp.dma_start(x[:, bass.ds(t, 1), :], x_in[bass.ds(t * P, P), :].rearrange("(a p) f -> p a f", a=1)).then_inc(x_loaded[par], 16)

                def load_kv(t, par):
                    if not known(t) or t >= 2:
                        sp.wait_ge(kv_lo, t - 1)
                    sp.dma_start(kv_raw[:, bass.ds(par, 1), :], kv_weights[bass.ds(t, 1), :, :].rearrange("a p n -> p a n")).then_inc(kv_loaded[par], 16)

                def body(i, par, live):
                    if live(0):
                        load(i, par)
                    if live(4):
                        load_kv(i - 4, par)

                skewed(sp, 4, body)

            @block.scalar
            def _(act):
                act.dma_start(mask[:, :, :], mask_t.rearrange("(c p) n -> p c n", p=P)).then_inc(mask_loaded, 16)
                act.dma_start(w_raw[:, :, :], w0_t.rearrange("(c p) n -> p c n", p=P)).then_inc(w_loaded, 16)
                act.dma_start(bias[:, :], bias0.partition_broadcast(P)).then_inc(bias_loaded, 16)
                load_next(act)
                act.wait_ge(masked, 1)
                hi_part(act, [w[:, :, :] for w in w0], w_raw[:, :, :]).then_inc(w_hi_done, 1)

                def body(i, par, live):
                    if live(2):
                        t, pt = i - 2, par
                        act.wait_ge(t_done, t + 1)
                        if not known(t) or t >= 2:
                            act.wait_ge(y_done, t - 1)
                        hi_part(act, [p[:, :, :] for p in ht[pt]], ps_t[:, pt, :].rearrange("p (c n) -> p c n", c=KC)).then_inc(hi_done, 1)
                    if live(1):
                        t, pt = i - 1, (par - 1) % 2
                        if not known(t) or t >= 2:
                            act.wait_ge(t_done, t - 1)
                        ln.activate(act, h[:, pt, :], tile_of(x, t), t).then_inc(h_done, 1)
                    if live(3):
                        t, pt = i - 3, (par - 3) % 2
                        act.wait_ge(kv_loaded[pt], 8 * (t - pt) + 16)
                        hi_part(act, [tile_of(w, t) for w in kv_w], kv_raw[:, pt, :]).then_inc(kv_hi, 1)

                skewed(act, 3, body)

            @block.gpsimd
            def _(pool):
                pool.memset(half[:, :], -0.5).then_inc(zeroed, 1)
                pool.memset(ident[:, :], 0.0).then_inc(zeroed, 1)
                pool.wait_ge(zeroed, 2)
                pool.affine_select(out=ident[:, :], in_=ident[:, :], compare_op=ALU.not_equal, fill=1.0, base=0,
                                   pattern=[[-1, P]], channel_multiplier=1).then_inc(consts, 1)
                pool.wait_ge(consts, 1)
                pool.wait_ge(bias_loaded, 16)

                def body(i, par, live):
                    if live(2):
                        t = i - 2
                        pool.wait_ge(h_done, t + 1)
                        pool.tensor_tensor(tile_of(x, t), tile_of(x, t), bias[:, :], ALU.add).then_inc(xb_done, 1)
                    if live(0):
                        ln.power(pool, i)

                skewed(pool, 2, body)

            @block.vector
            def _(dve):
                dve.memset(same_block[:, :], 0.0).then_inc(block_zeroed, 1)
                dve.wait_ge(block_zeroed, 1)
                for q in range(0, P, BLOCK):
                    last = dve.memset(same_block[q:q + BLOCK, q:q + BLOCK], 1.0)
                last.then_inc(const_done, 1)
                dve.wait_ge(mask_loaded, 16)
                dve.tensor_reduce(row_sums[:, :], mask[:, :, :].rearrange("p c (n b) -> p (c n) b", b=BLOCK), AX_X, ALU.add).then_inc(rows_done, 1)
                dve.wait_ge(blocks_done, 1)
                dve.tensor_scalar(block_on[:, :], ps_b[:, 0:KC * HID // BLOCK], 0.0, None, ALU.is_gt).then_inc(on_done, 1)
                dve.wait_ge(w_loaded, 16)
                dve.wait_ge(on_done, 1)
                w_blocks = w_raw[:, :, :].rearrange("p c (n b) -> p (c n) b", b=BLOCK)
                dve.tensor_tensor(w_blocks, w_blocks, block_on[:, :].unsqueeze(2).to_broadcast([P, KC * HID // BLOCK, BLOCK]), ALU.mult).then_inc(masked, 1)
                dve.wait_ge(w_hi_done, 1)
                lo_part(dve, [w[:, :, :] for w in w0], w_raw[:, :, :]).then_inc(w_lo_done, 1)

                def body(i, par, live):
                    if live(4):
                        t, pt = i - 4, par
                        dve.wait_ge(y_done, t + 1)
                        dve.wait_ge(xb_done, t + 1)
                        dve.tensor_tensor(tile_of(x, t), ps_y[:, pt, :], tile_of(x, t), ALU.add).then_inc(x_done, 1)
                    if live(0):
                        dve.wait_ge(x_loaded[par], 8 * (i - par) + 16)
                        ln.stats(dve, x[:, bass.ds(i, 1), :], i, par)
                    if live(2):
                        t, pt = i - 2, par
                        dve.wait_ge(hi_done, t + 1)
                        lo_part(dve, [p[:, :, :] for p in ht[pt]], ps_t[:, pt, :].rearrange("p (c n) -> p c n", c=KC)).then_inc(lo_done, 1)
                    if live(0):
                        ln.aggregate(dve, i, par)
                    if live(4):
                        dve.wait_ge(kv_hi, i - 4 + 1)
                        lo_part(dve, [tile_of(w, i - 4) for w in kv_w], kv_raw[:, par, :]).then_inc(kv_lo, 1)
                    if live(0):
                        ln.variance(dve, i, par)

                skewed(dve, 4, body)

            @block.tensor
            def _(pe):
                pe.wait_ge(rows_done, 1)
                pe.wait_ge(const_done, 1)
                pe.matmul(ps_b[:, 0:KC * HID // BLOCK], same_block[:, :], row_sums[:, :], start=True, stop=True).then_inc(blocks_done, 1)
                pe.wait_ge(consts, 1)

                def body(i, par, live):
                    if live(2):
                        t, pt = i - 2, par
                        pe.wait_ge(h_done, t + 1)
                        if not known(t) or t >= 2:
                            pe.wait_ge(lo_done, t - 1)
                        for c in range(KC):
                            last = pe.transpose(ps_t[:, pt, c * P:(c + 1) * P], h[:, pt, c * P:(c + 1) * P], ident[:, :])
                        last.then_inc(t_done, 1)
                    if live(3):
                        t, pt = i - 3, (par - 3) % 2
                        if known(t) and t == 0:
                            pe.wait_ge(w_lo_done, 1)
                        pe.wait_ge(lo_done, t + 1)
                        if not known(t) or t >= 2:
                            pe.wait_ge(x_done, t - 1)
                        for c in range(KC):
                            for n, (a, b) in enumerate(PASSES):
                                last = pe.matmul(ps_y[:, pt, :], ht[pt][a][:, c, :], w0[b][:, c, :],
                                                 start=(c == 0 and n == 0), stop=(c == KC - 1 and n == 2))
                        last.then_inc(y_done, 1)

                skewed(pe, 3, body)


class RouterWeights:

    def __init__(self, sb, sem, stack):
        self.router = sb("router", [P, KC, EXPERTS], F32, stack)
        self.logit_bias = sb("r_bias", [P, EXPERTS], F32, stack)
        self.expert_bias = sb("e_bias", [P, HID], F32, stack)
        self.loaded = sem("b_loaded")

    def load(self, eng, router_t, router_bias, expert_bias):
        eng.dma_start(self.router[:, :, :], router_t.rearrange("(c p) n -> p c n", p=P)).then_inc(self.loaded, 16)
        eng.dma_start(self.logit_bias[:, :], router_bias.partition_broadcast(P)).then_inc(self.loaded, 16)
        eng.dma_start(self.expert_bias[0:EXPERTS, :], expert_bias).then_inc(self.loaded, 16)


def routed_bias(nc, sem, sb, ps, split, x, ident, ln, weights):
    with ExitStack() as st:
        h = sb("h1", [P, 2, HID], F32, st)
        ht = sb("h1t", [P, 2, HID], F32, st)
        logits = sb("logits", [P, 2, EXPERTS], F32, st)
        neg_max = sb("r_neg_max", [P, 2], F32, st)
        e = sb("r_exp", [P, 2, EXPERTS], F32, st)
        total = sb("r_total", [P, 2], F32, st)
        top = sb("r_top", [P, 2, 8], F32, st)
        rest = sb("r_rest", [P, 2, EXPERTS], F32, st)
        top_sum = sb("r_top_sum", [P, 2], F32, st)
        inv_total = sb("r_inv_total", [P, TILES], F32, st)
        weight_sum = sb("r_weight_sum", [P, 2], F32, st)
        one_zero = sb("r_one_zero", [P, 2], F32, st)
        combined = sb("r_combined", [P, 2, 2], F32, st)
        chosen = sb("r_chosen", [P, 2, P], F32, st)
        chosen_t = sb("r_chosen_t", [P, 2, P], F32, st)
        scaled = sb("r_scaled", [P, 2, HID], F32, st)
        ps_t = ps("b_ps_t", [P, 2, HID], st)
        ps_l = ps("b_ps_l", [P, 2, HID], st)
        ps_c = ps("b_ps_c", [P, 2, HID], st)
        ps_m = ps("b_ps_m", [P, 2, HID], st)

        zeroed = sem("b_zeroed")
        h_done, t_done, ht_done = sem("b_h_done"), sem("b_t_done"), sem("b_ht_done")
        l_done, lb_done, max_done, exp_done = sem("b_l_done"), sem("b_lb_done"), sem("b_max_done"), sem("b_exp_done")
        top_done, rest_done, inv_done, chosen_done = sem("b_top_done"), sem("b_rest_done"), sem("b_inv_done"), sem("b_chosen_done")
        sum_done, combined_done, scaled_done = sem("b_sum_done"), sem("b_combined_done"), sem("b_scaled_done")
        ct_done, ctc_done, mix_done, x_done = sem("b_ct_done"), sem("b_ctc_done"), sem("b_mix_done"), sem("b_x_done")

        with nc.Block() as block:
            @block.gpsimd
            def _(pool):
                pool.memset(one_zero[:, 0:1], 1.0).then_inc(zeroed, 1)
                pool.wait_ge(zeroed, 1)
                pool.memset(one_zero[:, 1:2], 0.0).then_inc(zeroed, 1)
                pool.wait_ge(zeroed, 2)
                pool.memset(weights.expert_bias[EXPERTS:P, :], 0.0).then_inc(zeroed, 1)
                pool.wait_ge(zeroed, 3)
                pool.memset(chosen[:, :, EXPERTS:P], 0.0).then_inc(zeroed, 1)

                def body(i, par, live):
                    if live(0):
                        ln.power(pool, i)

                skewed(pool, 0, body)

            @block.scalar
            def _(act):
                def body(i, par, live):
                    if live(4):
                        t, pt = i - 4, par
                        act.wait_ge(max_done, t + 1)
                        if not known(t) or t >= 2:
                            act.wait_ge(chosen_done, t - 1)
                        act.activation(e[:, pt, :], logits[:, pt, :], ACT.Exp, bias=neg_max[:, pt:pt + 1],
                                       accum_out=total[:, pt:pt + 1]).then_inc(exp_done, 1)
                    if live(1):
                        t, pt = i - 1, (par - 1) % 2
                        if not known(t) or t >= 2:
                            act.wait_ge(t_done, t - 1)
                        ln.activate(act, h[:, pt, :], tile_of(x, t), t).then_inc(h_done, 1)
                    if live(2):
                        t, pt = i - 2, par
                        act.wait_ge(t_done, t + 1)
                        if not known(t) or t >= 2:
                            act.wait_ge(l_done, t - 1)
                        act.activation(ht[:, pt, :], ps_t[:, pt, :], ACT.Copy).then_inc(ht_done, 1)
                    if live(5):
                        t, pt = i - 5, (par - 5) % 2
                        act.wait_ge(ct_done, t + 1)
                        if not known(t) or t >= 2:
                            act.wait_ge(mix_done, t - 1)
                        act.activation(chosen_t[:, pt, :], ps_c[:, pt, 0:P], ACT.Copy).then_inc(ctc_done, 1)
                        act.wait_ge(combined_done, t + 1)
                        if not known(t) or t >= 2:
                            act.wait_ge(x_done, t - 1)
                        act.activation(scaled[:, pt, :], tile_of(x, t), ACT.Identity, bias=combined[:, pt, 1:2],
                                       scale=combined[:, pt, 0:1]).then_inc(scaled_done, 1)

                skewed(act, 5, body)

            @block.vector
            def _(dve):
                dve.wait_ge(zeroed, 4)
                dve.wait_ge(weights.loaded, 48)

                def body(i, par, live):
                    p4, p3 = par, (par - 3) % 2
                    if live(6):
                        t = i - 6
                        dve.wait_ge(mix_done, t + 1)
                        dve.wait_ge(scaled_done, t + 1)
                        dve.scalar_tensor_tensor(tile_of(x, t), ps_m[:, par, :], inv_total[:, bass.ds(t, 1)], scaled[:, par, :],
                                                 ALU.mult, ALU.add).then_inc(x_done, 1)
                    if live(4):
                        t4 = i - 4
                        wait_alone(dve, exp_done, t4 + 1, ln.ready)
                        dve.max(top[:, p4, :], e[:, p4, :]).then_inc(top_done, 1)
                    if live(0):
                        ln.stats(dve, x[:, bass.ds(i, 1), :], i, par)
                    if live(4):
                        wait_alone(dve, top_done, t4 + 1, ln.ready)
                        dve.match_replace(rest[:, p4, :], top[:, p4, :], e[:, p4, :], 0.0).then_inc(rest_done, 1)
                    if live(0):
                        ln.aggregate(dve, i, par)
                    if live(4):
                        dve.reduce_sum(top_sum[:, p4:p4 + 1], top[:, p4, :], AX_X)
                        dve.reciprocal(inv_total[:, bass.ds(t4, 1)], total[:, p4:p4 + 1]).then_inc(inv_done, 1)
                        dve.wait_ge(rest_done, t4 + 1)
                        if not known(t4) or t4 >= 2:
                            dve.wait_ge(ct_done, t4 - 1)
                        dve.tensor_tensor(chosen[:, p4, 0:EXPERTS], e[:, p4, :], rest[:, p4, :], ALU.subtract).then_inc(chosen_done, 1)
                    if live(0):
                        ln.variance(dve, i, par)
                    if live(4):
                        dve.wait_ge(inv_done, t4 + 1)
                        dve.tensor_tensor(weight_sum[:, p4:p4 + 1], top_sum[:, p4:p4 + 1], inv_total[:, bass.ds(t4, 1)], ALU.mult).then_inc(sum_done, 1)
                    if live(3):
                        t3 = i - 3
                        dve.wait_ge(l_done, t3 + 1)
                        if not known(t3) or t3 >= 2:
                            dve.wait_ge(exp_done, t3 - 1)
                        dve.tensor_tensor(logits[:, p3, :], ps_l[:, p3, 0:EXPERTS], weights.logit_bias[:, :], ALU.add).then_inc(lb_done, 1)
                    if live(4):
                        dve.wait_ge(sum_done, t4 + 1)
                        if not known(t4) or t4 >= 2:
                            dve.wait_ge(scaled_done, t4 - 1)
                        dve.scalar_tensor_tensor(combined[:, p4, :], ln.factors[:, bass.ds(t4, 1), :].rearrange("p t n -> p (t n)"),
                                                 weight_sum[:, p4:p4 + 1], one_zero[:, :], ALU.mult, ALU.add).then_inc(combined_done, 1)
                    if live(3):
                        dve.wait_ge(lb_done, t3 + 1)
                        dve.tensor_reduce(neg_max[:, p3:p3 + 1], logits[:, p3, :], AX_X, ALU.max, negate=True).then_inc(max_done, 1)

                skewed(dve, 6, body)

            @block.tensor
            def _(pe):
                pe.wait_ge(weights.loaded, 48)
                pe.wait_ge(zeroed, 4)

                def body(i, par, live):
                    if live(2):
                        t, pt = i - 2, par
                        pe.wait_ge(h_done, t + 1)
                        if not known(t) or t >= 2:
                            pe.wait_ge(ht_done, t - 1)
                        for c in range(KC):
                            last = pe.transpose(ps_t[:, pt, c * P:(c + 1) * P], h[:, pt, c * P:(c + 1) * P], ident[:, :])
                        last.then_inc(t_done, 1)
                    if live(5):
                        t, pt = i - 5, (par - 5) % 2
                        pe.wait_ge(chosen_done, t + 1)
                        if not known(t) or t >= 2:
                            pe.wait_ge(ctc_done, t - 1)
                        pe.transpose(ps_c[:, pt, 0:P], chosen[:, pt, :], ident[:, :]).then_inc(ct_done, 1)
                    if live(3):
                        t, pt = i - 3, (par - 3) % 2
                        pe.wait_ge(ht_done, t + 1)
                        if not known(t) or t >= 2:
                            pe.wait_ge(lb_done, t - 1)
                        for c in range(KC):
                            last = pe.matmul(ps_l[:, pt, 0:EXPERTS], ht[:, pt, c * P:(c + 1) * P], weights.router[:, c, :],
                                             start=(c == 0), stop=(c == KC - 1))
                        last.then_inc(l_done, 1)
                    if live(5):
                        pe.wait_ge(ctc_done, i - 5 + 1)
                        if not known(i) or i - 5 >= 2:
                            pe.wait_ge(x_done, i - 5 - 1)
                        pt = (par - 5) % 2
                        pe.matmul(ps_m[:, pt, :], chosen_t[:, pt, :], weights.expert_bias[:, :], start=True, stop=True).then_inc(mix_done, 1)

                skewed(pe, 5, body)


def normalize_for_attention(nc, sem, sb, ps, x, ident, ln, h3):
    with ExitStack() as st:
        h = sb("h2", [P, 2, HID], F32, st)
        ps_t = ps("c_ps_t", [P, 2, HID], st)
        h_done, t_done, hi_done, lo_done = sem("c_h_done"), sem("c_t_done"), sem("c_hi_done"), sem("c_lo_done")

        def transposed(pt):
            return ps_t[:, pt, :].rearrange("p (c n) -> p c n", c=KC)

        with nc.Block() as block:
            @block.gpsimd
            def _(pool):
                def body(i, par, live):
                    if live(0):
                        ln.power(pool, i)

                skewed(pool, 0, body)

            @block.scalar
            def _(act):
                def body(i, par, live):
                    if live(1):
                        t, pt = i - 1, (par - 1) % 2
                        if not known(t) or t >= 2:
                            act.wait_ge(t_done, t - 1)
                        ln.activate(act, h[:, pt, :], tile_of(x, t), t).then_inc(h_done, 1)
                    if live(2):
                        t, pt = i - 2, par
                        act.wait_ge(t_done, t + 1)
                        hi_part(act, [p[:, :, bass.ds(t * P, P)] for p in h3], transposed(pt)).then_inc(hi_done, 1)

                skewed(act, 2, body)

            @block.vector
            def _(dve):
                def body(i, par, live):
                    if live(0):
                        ln.stats(dve, x[:, bass.ds(i, 1), :], i, par)
                    if live(3):
                        t, pt = i - 3, (par - 3) % 2
                        dve.wait_ge(hi_done, t + 1)
                        lo_part(dve, [p[:, :, bass.ds(t * P, P)] for p in h3], transposed(pt)).then_inc(lo_done, 1)
                    if live(0):
                        ln.aggregate(dve, i, par)
                        ln.variance(dve, i, par)

                skewed(dve, 3, body)

            @block.tensor
            def _(pe):
                def body(i, par, live):
                    if live(2):
                        t, pt = i - 2, par
                        pe.wait_ge(h_done, t + 1)
                        if not known(t) or t >= 2:
                            pe.wait_ge(lo_done, t - 1)
                        for c in range(KC):
                            last = pe.transpose(ps_t[:, pt, c * P:(c + 1) * P], h[:, pt, c * P:(c + 1) * P], ident[:, :])
                        last.then_inc(t_done, 1)

                skewed(pe, 2, body)


def kv_tasks():
    tasks = []
    for quad in range(2):
        down = [("Z", quad, j, 0) for j in range(8)]
        flip = [("C", quad, jp, hg) for jp in range(4) for hg in range(2)]
        keys = [("K", quad, pair, g) for pair in range(2) for g in range(KV_HEADS)]
        values = [("V", quad, tile, part) for tile in range(8) for part in range(2)]
        tasks += down[0:4] + flip[0:2] + down[4:6] + flip[2:4] + down[6:8] + flip[4:6] + keys[0:2] + flip[6:8] + keys[2:] + values
    return tasks


def keys_and_values(nc, sem, sb, ps, split, ident, h3, kv_w, k_scr, v_scr):
    SPAN = 4 * SEQ
    BANKS, STAGES = 8, 4
    tasks = kv_tasks()
    at = {task: n for n, task in enumerate(tasks)}
    hi_order = [n for n, task in enumerate(tasks) if task[0] != "Z"]
    lo_count = {n: k + 1 for k, n in enumerate(hi_order)}
    down_order = [n for n, task in enumerate(tasks) if task[0] == "Z"]
    down_count = {n: k + 1 for k, n in enumerate(down_order)}
    stage_order = [n for n, task in enumerate(tasks) if task[0] in "KV"]
    stage_count = {n: k for k, n in enumerate(stage_order)}

    with ExitStack() as st:
        whole_w = [w[:, :, :].rearrange("p a n -> p (a n)") for w in kv_w]
        down_w = [w[:, 0:KV_DOWN].rearrange("p (c n) -> p c n", c=KC) for w in whole_w]
        up_w = [[w[:, KV_DOWN + n * KV_UP:KV_DOWN + (n + 1) * KV_UP].rearrange("p (c n) -> p c n", c=2) for w in whole_w] for n in range(2)]
        z = sb("kv_z", [P, 2, KV_HEADS, 2, 2 * LATENT], F32, st)
        latent = split("latent", [P, 4, 4, KV_HEADS, BLOCK], st)
        stage = [split(f"kv_stage{n}", [P, HID], st) for n in range(STAGES)]
        bank = ps("kv_banks", [P, BANKS, HID], st)

        task_done, z_done, hi_done, lo_done = sem("kv_task_done"), sem("kv_z_done"), sem("kv_hi_done"), sem("kv_lo_done")
        stored = [sem(f"kv_stored{n}") for n in range(STAGES)]

        def freed(eng, n):
            before = n - BANKS
            if before >= 0:
                if before in down_count:
                    eng.wait_ge(z_done, down_count[before])
                else:
                    eng.wait_ge(lo_done, lo_count[before])

        def outlet(n):
            kind, quad, a, b = tasks[n]
            src = bank[:, n % BANKS, :]
            if kind == "C":
                return ([p[:, a, :, 4 * b:4 * b + 4, :].rearrange("p b h m -> p h b m") for p in latent],
                        src.rearrange("p (h b m) -> p h b m", h=4, b=4))
            return [p[:, :] for p in stage[stage_count[n] % STAGES]], src

        with nc.Block() as block:
            @block.sync
            def _(sp):
                for k, n in enumerate(stage_order):
                    kind, quad, a, b = tasks[n]
                    sp.wait_ge(lo_done, lo_count[n])
                    if k >= STAGES:
                        sp.wait_ge(stored[k % STAGES], 32 * (k // STAGES))
                    for part in (HI, LO):
                        src = stage[k % STAGES][part][:, :].bitcast(F32)
                        if kind == "K":
                            pair = 2 * quad + a
                            sp.dma_start(k_scr[b, part, :, pair * PAIR:(pair + 1) * PAIR], src).then_inc(stored[k % STAGES], 16)
                        else:
                            pair = 2 * quad + a // 4
                            sp.dma_start(v_scr[4 * b:4 * b + 4, pair, part, :, a % 4, :].rearrange("g p d -> p g d"),
                                         src.rearrange("p (g d) -> p g d", g=4)).then_inc(stored[k % STAGES], 16)
                for k in range(STAGES):
                    sp.wait_ge(stored[k], 32 * (len(stage_order) // STAGES))

            @block.scalar
            def _(act):
                for n, (kind, quad, a, b) in enumerate(tasks):
                    act.wait_ge(task_done, n + 1)
                    if kind == "Z":
                        before = [at[("C", q, jp, 1)] for q, jp in [(quad, a // 2 - 2) if a >= 4 else (quad - 1, a // 2 + 2)] if q >= 0]
                        if before:
                            act.wait_ge(task_done, before[0] + 1)
                        act.activation(z[:, a // 2 % 2, :, a % 2, :].rearrange("p h (t l) -> p h t l", t=2),
                                       bank[:, n % BANKS, :].rearrange("p (t h l) -> p h t l", t=2, h=KV_HEADS), ACT.Copy).then_inc(z_done, 1)
                    else:
                        if kind == "C" and quad == 1:
                            act.wait_ge(task_done, at[("K", 0, 1, KV_HEADS - 1) if a < 2 else ("V", 0, 7, 1)] + 1)
                        k = stage_count.get(n, 0)
                        if k >= STAGES:
                            act.wait_ge(stored[k % STAGES], 32 * (k // STAGES))
                        parts, src = outlet(n)
                        hi_part(act, parts, src).then_inc(hi_done, 1)

            @block.vector
            def _(dve):
                for k, n in enumerate(hi_order):
                    dve.wait_ge(hi_done, k + 1)
                    parts, src = outlet(n)
                    lo_part(dve, parts, src).then_inc(lo_done, 1)

            @block.tensor
            def _(pe):
                for n, (kind, quad, a, b) in enumerate(tasks):
                    freed(pe, n)
                    out = bank[:, n % BANKS, :]
                    if kind == "Z":
                        for c in range(KC):
                            for m, (u, v) in enumerate(PASSES):
                                tokens = h3[u][:, c, quad * SPAN:(quad + 1) * SPAN].rearrange("p (n j) -> p n j", j=8)[:, :, a]
                                last = pe.matmul(out, tokens, down_w[v][:, c, :], start=(c == 0 and m == 0), stop=(c == KC - 1 and m == 2))
                    elif kind == "C":
                        pe.wait_ge(z_done, down_count[at[("Z", quad, 2 * a + 1, 0)]])
                        for h in range(4):
                            last = pe.transpose(out[:, h * P:(h + 1) * P], z[:, a % 2, 4 * b + h, :, :].rearrange("p j l -> p (j l)"), ident[:, :])
                    elif kind == "K":
                        if (a, b) == (0, 0):
                            pe.wait_ge(lo_done, lo_count[at[("C", quad, 1, 1)]])
                        for c in range(2):
                            for m, (u, v) in enumerate(PASSES):
                                last = pe.matmul(out, up_w[0][u][:, c, b * HEAD:(b + 1) * HEAD],
                                                 latent[v][:, c, 2 * a:2 * a + 2, :, :].rearrange("p b h m -> p (b h m)"),
                                                 start=(c == 0 and m == 0), stop=(c == 1 and m == 2))
                    else:
                        if (a, b) == (0, 0):
                            pe.wait_ge(lo_done, lo_count[at[("C", quad, 3, 1)]])
                        for c in range(2):
                            for m, (u, v) in enumerate(PASSES):
                                rows = latent[u][:, 2 + c, a // 2, 4 * (a % 2):4 * (a % 2) + 4, :].rearrange("p h m -> p (h m)")
                                last = pe.matmul(out, rows, up_w[1][v][:, c, b * HID:(b + 1) * HID],
                                                 start=(c == 0 and m == 0), stop=(c == 1 and m == 2))
                    last.then_inc(task_done, 1)


def attention(nc, sem, sb, ps, split, x, ident, h3, wq_g, wo_g, k_scr, v_scr):
    HEADS = 2 * GROUP
    with ExitStack() as st:
        wq = split("wq", [P, KC, GROUP * HEAD], st)
        wo = split("wo", [P, GROUP, HID], st)
        raw = sb("w_raw", [P, 4, HID], F32, st)
        q_first = sb("q_first", [P, GROUP, 2, P], F32, st)
        q_second = split("q_second", [P, GROUP, 2, P], st)
        k = split("k", [P, 2, SEQ], st)
        k_first = sb("k_first", [P, 2, P], F32, st)
        v = split("v", [P, 4, HEAD], st)
        prob = sb("prob", [P, 2, GROUP, 3 * P], F32, st)
        neg_max = sb("neg_max", [P, 2, GROUP, 2], F32, st)
        row_sum = sb("row_sum", [P, 2, GROUP, 2], F32, st)
        inv_sum = sb("inv_sum", [P, 2, GROUP, 2], F32, st)
        prob_t = split("prob_t", [P, 3, GROUP * P], st)
        o = [split(f"o{n}", [P, 2, GROUP, P], st) for n in range(2)]
        causal = sb("causal", [P, 2 * P], F32, st)
        ps_s = ps("ps_s", [P, GROUP, HID], st)
        ps_t = ps_s[:, 2:4, :]
        ps_q = ps("ps_q", [P, 2, HID], st)
        ps_o = ps("ps_o", [P, 2, HID], st)

        k_loaded, v_loaded, raw_loaded = sem("k_loaded"), sem("v_loaded"), sem("raw_loaded")
        mask_zero, mask_done = sem("mask_zero"), sem("mask_done")
        k_joined = sem("k_joined")
        w_hi, w_lo = sem("w_hi"), sem("w_lo")
        s_done = sem("s_done")
        scored = sem("scored")
        exped, inv_done, normed = sem("exped"), sem("inv_done"), sem("normed")
        q_done, q_hi, q_read = sem("q_done"), sem("q_hi"), sem("q_read")
        t_done, t_hi, t_lo = sem("pt_done"), sem("pt_hi"), sem("pt_lo")
        pv_done, o_hi, o_lo = sem("pv_done"), sem("o_hi"), sem("o_lo")
        y_done, y_read = sem("y_done"), sem("y_read")

        UNITS = PAIRS * KV_HEADS
        LAST = KV_HEADS - 1

        def groups(eng, group):
            group(0, True, False)
            with eng.Fori(1, LAST) as g:
                group(g, False, False)
            group(LAST, False, True)

        with nc.Block() as block:
            @block.sync
            def _(sp):
                def load_raw(src, sets):
                    if not known(sets) or sets >= 1:
                        sp.wait_ge(w_lo, 4 * sets)
                    sp.dma_start(raw[:, :, :], src).then_inc(raw_loaded, 16)

                def group(g, first, last):
                    for p in range(PAIRS):
                        u = PAIRS * g + p
                        if not (first and p == 0):
                            sp.wait_ge(s_done, HEADS * u)
                        for part in (HI, LO):
                            sp.dma_start(k[part][:, :, :].rearrange("p b n -> p (b n)").bitcast(F32), k_scr[bass.ds(g, 1), part, :, p * PAIR:(p + 1) * PAIR].rearrange("a p n -> p (a n)")).then_inc(k_loaded, 16)
                        if not (first and p == 0):
                            sp.wait_ge(pv_done, 4 * u)
                        for part in (HI, LO):
                            sp.dma_start(v[part][:, :, :].bitcast(F32), v_scr[bass.ds(g, 1), p, part, :, :, :].rearrange("a p t d -> p (a t) d")).then_inc(v_loaded, 16)
                        if p == 0:
                            load_raw(wo_g[bass.ds(g, 1), :, :, :].rearrange("a p h n -> p (a h) n"), 2 * g + 1)
                        if p == 1 and not last:
                            load_raw(wq_g[bass.ds(g + 1, 1), :, :, :].rearrange("a p c n -> p (a c) n"), 2 * g + 2)

                load_raw(wq_g[0, :, :, :], 0)
                groups(sp, group)

            @block.gpsimd
            def _(pool):
                pool.memset(causal[:, :], 0.0).then_inc(mask_zero, 1)
                pool.wait_ge(mask_zero, 1)
                pool.affine_select(out=causal[:, P:2 * P], in_=causal[:, P:2 * P], compare_op=ALU.is_ge, fill=MASKED, base=0,
                                   pattern=[[-1, P]], channel_multiplier=1).then_inc(mask_done, 1)

                def group(g, first, last):
                    for p in range(PAIRS):
                        u = PAIRS * g + p
                        pool.wait_ge(k_loaded, 32 * u + 32)
                        if not (first and p == 0):
                            pool.wait_ge(s_done, HEADS * u)
                        parts = [w[:, :, 0:P].bitcast(F32) for w in k]
                        pool.tensor_tensor(k_first[:, :, :], parts[HI], parts[LO], ALU.add).then_inc(k_joined, 1)
                        for b in range(2):
                            for h in range(GROUP):
                                wait_alone(pool, inv_done, HEADS * u + GROUP * b + h + 1, mask_done)
                                pool.tensor_scalar(prob[:, b, h, 0:P], prob[:, b, h, 0:P], inv_sum[:, b, h, 0:1], 1.0, ALU.mult, ALU.mult)
                                pool.tensor_scalar(prob[:, b, h, P:3 * P], prob[:, b, h, P:3 * P], inv_sum[:, b, h, 1:2], 1.0,
                                                   ALU.mult, ALU.mult).then_inc(normed, 1)

                groups(pool, group)

            @block.scalar
            def _(act):
                def query_hi(h, count):
                    act.wait_ge(q_done, count)
                    by_tile = ps_q[:, h % 2, :].rearrange("p (b t n) -> p b t n", b=2, t=2)
                    act.activation(q_first[:, h, :, :], by_tile[:, :, 0, :], ACT.Copy)
                    hi_part(act, [w[:, h, :, :] for w in q_second], by_tile[:, :, 1, :]).then_inc(q_hi, 1)

                def weight_hi(w, n, sets):
                    if n == 0:
                        act.wait_ge(raw_loaded, 16 * sets + 16)
                    hi_part(act, [part[:, n, :] for part in w], raw[:, n, :]).then_inc(w_hi, 1)

                def group(g, first, last):
                    for p in range(PAIRS):
                        u = PAIRS * g + p
                        start = first and p == 0
                        more = not (last and p == PAIRS - 1)
                        def exponentials(b, h):
                            act.wait_ge(scored, HEADS * u + GROUP * b + h + 1)
                            act.activation(prob[:, b, h, 0:P], prob[:, b, h, 0:P], ACT.Exp, scale=-1.0,
                                           bias=neg_max[:, b, h, 0:1], accum_out=row_sum[:, b, h, 0:1])
                            act.activation(prob[:, b, h, P:3 * P], prob[:, b, h, P:3 * P], ACT.Exp, scale=-1.0,
                                           bias=neg_max[:, b, h, 1:2], accum_out=row_sum[:, b, h, 1:2]).then_inc(exped, 1)

                        def query(h):
                            if more:
                                query_hi(h, GROUP * (u + 1) + h + 1)
                            if p == 0:
                                if h == 0 and not first:
                                    act.wait_ge(y_done, 4 * u)
                                weight_hi(wo, h, 2 * g + 1)

                        def prob_hi(b, blk):
                            act.wait_ge(t_done, 6 * u + 3 * b + blk + 1)
                            if not (start and b == 0):
                                act.wait_ge(pv_done, 4 * u + 2 * b - 1 + (blk > 0))
                            hi_part(act, [w[:, blk, :] for w in prob_t], ps_t[:, (b + blk) % 2, :]).then_inc(t_hi, 1)

                        def out_hi(b, half):
                            act.wait_ge(pv_done, 4 * u + 2 * b + half + 1)
                            if not start:
                                act.wait_ge(y_done, 4 * (u - 1) + 2 * b + half + 1)
                            hi_part(act, [w[:, half, :, :].rearrange("p h n -> p (h n)") for w in o[b]], ps_o[:, half, :]).then_inc(o_hi, 1)

                        split_next = p == 2 and not last
                        for h in range(GROUP):
                            exponentials(0, h)
                        exponentials(1, 0)
                        exponentials(1, 1)
                        query(0)
                        exponentials(1, 2)
                        exponentials(1, 3)
                        query(1)
                        prob_hi(0, 0)
                        prob_hi(0, 1)
                        query(2)
                        prob_hi(0, 2)
                        query(3)
                        out_hi(0, 0)
                        out_hi(0, 1)
                        prob_hi(1, 0)
                        prob_hi(1, 1)
                        if split_next:
                            act.wait_ge(q_done, GROUP * (u + 2))
                            weight_hi(wq, 0, 2 * g + 2)
                            weight_hi(wq, 1, 2 * g + 2)
                        prob_hi(1, 2)
                        out_hi(1, 0)
                        if split_next:
                            weight_hi(wq, 2, 2 * g + 2)
                            weight_hi(wq, 3, 2 * g + 2)
                        out_hi(1, 1)

                for n in range(4):
                    weight_hi(wq, n, 0)
                for h in range(GROUP):
                    query_hi(h, h + 1)
                groups(act, group)

            @block.vector
            def _(dve):
                def query_lo(h, count):
                    dve.wait_ge(q_hi, count)
                    by_tile = ps_q[:, h % 2, :].rearrange("p (b t n) -> p b t n", b=2, t=2)
                    lo_part(dve, [w[:, h, :, :] for w in q_second], by_tile[:, :, 1, :]).then_inc(q_read, 1)

                def add(u, p, b, half):
                    dve.wait_ge(y_done, 4 * u + 2 * b + half + 1)
                    t = 4 * p + 2 * b + half
                    dve.tensor_tensor(x[:, t, :], ps_q[:, half, :], x[:, t, :], ALU.add).then_inc(y_read, 1)

                def weight_lo(w, n, sets):
                    dve.wait_ge(w_hi, 4 * sets + n + 1)
                    lo_part(dve, [part[:, n, :] for part in w], raw[:, n, :]).then_inc(w_lo, 1)

                def group(g, first, last):
                    for p in range(PAIRS):
                        u = PAIRS * g + p
                        start = first and p == 0
                        more = not (last and p == PAIRS - 1)

                        def score(b, h):
                            if not start and h == 0:
                                dve.wait_ge(t_done, 6 * (u - 1) + 3 * b + 3)
                            wait_alone(dve, s_done, HEADS * u + GROUP * b + h + 1, mask_done)
                            dve.tensor_tensor_reduce(out=prob[:, b, h, 0:P], in0=ps_s[:, h, 0:P], in1=causal[:, P:2 * P], scale=-SCALE,
                                                     scalar=3.0e38, op0=ALU.add, op1=ALU.min, accum_out=neg_max[:, b, h, 0:1])
                            dve.tensor_tensor_reduce(out=prob[:, b, h, P:3 * P], in0=ps_s[:, h, 2 * P:4 * P], in1=causal[:, :], scale=-SCALE,
                                                     scalar=3.0e38, op0=ALU.add, op1=ALU.min, accum_out=neg_max[:, b, h, 1:2]).then_inc(scored, 1)

                        def inverse(b, h):
                            dve.wait_ge(exped, HEADS * u + GROUP * b + h + 1)
                            dve.reciprocal(inv_sum[:, b, h, :], row_sum[:, b, h, :]).then_inc(inv_done, 1)

                        def query(h):
                            if more:
                                query_lo(h, GROUP * (u + 1) + h + 1)
                            if p == 0:
                                weight_lo(wo, h, 2 * g + 1)

                        def prob_lo(b, blk):
                            dve.wait_ge(t_hi, 6 * u + 3 * b + blk + 1)
                            lo_part(dve, [w[:, blk, :] for w in prob_t], ps_t[:, (b + blk) % 2, :]).then_inc(t_lo, 1)

                        def out_lo(b, half):
                            dve.wait_ge(o_hi, 4 * u + 2 * b + half + 1)
                            lo_part(dve, [w[:, half, :, :].rearrange("p h n -> p (h n)") for w in o[b]], ps_o[:, half, :]).then_inc(o_lo, 1)

                        for h in range(GROUP):
                            score(0, h)
                        if not start:
                            add(u - 1, (p - 1) % PAIRS, 1, 1)
                        for h in range(GROUP):
                            inverse(0, h)
                        for h in range(GROUP):
                            score(1, h)
                        inverse(1, 0)
                        query(0)
                        for h in range(1, GROUP):
                            inverse(1, h)
                        split_next = p == 2 and not last
                        query(1)
                        prob_lo(0, 0)
                        prob_lo(0, 1)
                        query(2)
                        prob_lo(0, 2)
                        query(3)
                        out_lo(0, 0)
                        out_lo(0, 1)
                        prob_lo(1, 0)
                        prob_lo(1, 1)
                        if split_next:
                            weight_lo(wq, 0, 2 * g + 2)
                            weight_lo(wq, 1, 2 * g + 2)
                        add(u, p, 0, 0)
                        prob_lo(1, 2)
                        out_lo(1, 0)
                        if split_next:
                            weight_lo(wq, 2, 2 * g + 2)
                            weight_lo(wq, 3, 2 * g + 2)
                        add(u, p, 0, 1)
                        out_lo(1, 1)
                        add(u, p, 1, 0)

                for n in range(4):
                    weight_lo(wq, n, 0)
                for h in range(GROUP):
                    query_lo(h, h + 1)
                groups(dve, group)
                add(UNITS - 1, PAIRS - 1, 1, 1)

            @block.tensor
            def _(pe):
                def project_query(h, pair):
                    for c in range(KC):
                        for n, (a, b) in enumerate(PASSES):
                            last = pe.matmul(ps_q[:, h % 2, :], wq[a][:, c, h * HEAD:(h + 1) * HEAD], h3[b][:, c, pair * PAIR:(pair + 1) * PAIR],
                                             start=(c == 0 and n == 0), stop=(c == KC - 1 and n == 2))
                    last.then_inc(q_done, 1)

                def group(g, first, last):
                    for p in range(PAIRS):
                        u = PAIRS * g + p
                        start = first and p == 0
                        more = not (last and p == PAIRS - 1)

                        def scores(b):
                            for h in range(GROUP):
                                n = HEADS * u + GROUP * b + h
                                if b:
                                    pe.wait_ge(scored, n - GROUP + 1)
                                elif not start:
                                    if h < 2:
                                        pe.wait_ge(scored, n - GROUP + 1)
                                    else:
                                        pe.wait_ge(t_lo, 6 * u)
                                pe.matmul(ps_s[:, h, 0:P], q_first[:, h, b, :], k_first[:, b, :], start=True, stop=True)
                                for m, (i, j) in enumerate(PASSES):
                                    done = pe.matmul(ps_s[:, h, 2 * P:4 * P], q_second[i][:, h, b, :], k[j][:, b, :], start=(m == 0), stop=(m == 2))
                                done.then_inc(s_done, 1)

                        def query(h):
                            if not more:
                                return
                            if h == 0 and p == PAIRS - 1:
                                pe.wait_ge(w_lo, 4 * (2 * g + 2) + 4)
                            if h < 2:
                                if not start:
                                    pe.wait_ge(y_read, 4 * u - 1 + h)
                            else:
                                pe.wait_ge(q_read, GROUP * (u + 1) + h - 1)
                            project_query(h, (p + 1) % PAIRS)

                        def flip(b, blk):
                            n = 6 * u + 3 * b + blk
                            if blk == 0:
                                pe.wait_ge(normed, HEADS * u + GROUP * (b + 1))
                            if b == 0 and blk < 2:
                                pe.wait_ge(scored, HEADS * u + GROUP + 3 + blk)
                            else:
                                pe.wait_ge(t_lo, n - 1)
                            for h in range(GROUP):
                                done = pe.transpose(ps_t[:, (b + blk) % 2, h * P:(h + 1) * P], prob[:, b, h, blk * P:(blk + 1) * P], ident[:, :])
                            done.then_inc(t_done, 1)

                        def values(b, half):
                            if b == 0 and half == 0:
                                pe.wait_ge(v_loaded, 32 * u + 32)
                            if not (start and b == 0):
                                pe.wait_ge(o_lo, 4 * u + 2 * b - 1 + half)
                            blocks = (((0, 0),), ((1, 0), (2, 1)))[half]
                            for n, (blk, tile) in enumerate(blocks):
                                pe.wait_ge(t_lo, 6 * u + 3 * b + blk + 1)
                                for m, (i, j) in enumerate(PASSES):
                                    done = pe.matmul(ps_o[:, half, :], v[i][:, 2 * b + tile, :], prob_t[j][:, blk, :],
                                                     start=(n == 0 and m == 0), stop=(n == len(blocks) - 1 and m == 2))
                            done.then_inc(pv_done, 1)

                        def output(b, half):
                            if b == 0 and half == 0 and p == 0:
                                pe.wait_ge(w_lo, 4 * (2 * g + 1) + 4)
                            if b == 0:
                                if more:
                                    pe.wait_ge(q_read, GROUP * (u + 1) + 3 + half)
                                else:
                                    pe.wait_ge(y_read, 4 * u - 1 + half)
                            else:
                                pe.wait_ge(y_read, 4 * u + 1 + half)
                            pe.wait_ge(o_lo, 4 * u + 2 * b + half + 1)
                            for h in range(GROUP):
                                for m, (i, j) in enumerate(PASSES):
                                    done = pe.matmul(ps_q[:, half, :], o[b][i][:, half, h, :], wo[j][:, h, :],
                                                     start=(h == 0 and m == 0), stop=(h == GROUP - 1 and m == 2))
                            done.then_inc(y_done, 1)

                        pe.wait_ge(k_joined, u + 1)
                        pe.wait_ge(q_read, GROUP * (u + 1))
                        scores(0)
                        query(0)
                        scores(1)
                        query(1)
                        flip(0, 0)
                        flip(0, 1)
                        query(2)
                        flip(0, 2)
                        query(3)
                        values(0, 0)
                        values(0, 1)
                        flip(1, 0)
                        flip(1, 1)
                        output(0, 0)
                        flip(1, 2)
                        values(1, 0)
                        output(0, 1)
                        values(1, 1)
                        output(1, 0)
                        output(1, 1)

                pe.wait_ge(w_lo, 4)
                for h in range(GROUP):
                    if h >= 2:
                        pe.wait_ge(q_read, h - 1)
                    project_query(h, 0)
                groups(pe, group)


def feed_forward(nc, sem, sb, ps, split, x, ident, ln, gate_c, up_c, down_c, scales, out):
    with ExitStack() as st:
        gate = split("gate", [P, CHUNKS, KC, P], st)
        up = split("up", [P, CHUNKS, KC, P], st)
        down = split("down", [P, CHUNKS, HID], st)
        raw = [sb(f"f_raw{n}", [P, HID], F32, st) for n in range(3)]
        h = sb("h3n", [P, 4, HID], F32, st)
        ht = split("h3t", [P, KC, 4 * P], st)
        act_buf = sb("f_act", [P, 4 * P], F32, st)
        inner = [split(f"inner{n}", [P, 4 * P], st) for n in range(2)]
        scale = sb("f_scale", [P, 3], F32, st)
        ps_r = ps("f_ps_r", [P, 4, HID], st)
        ps_y = ps("f_ps_y", [P, 4, HID], st)

        raw_loaded = [sem(f"f_raw_loaded{n}") for n in range(3)]
        scale_loaded = sem("f_scale_loaded")
        w_hi, w_lo = sem("f_w_hi"), sem("f_w_lo")
        h_done, t_done, h_hi, h_lo = sem("f_h_done"), sem("f_t_done"), sem("f_h_hi"), sem("f_h_lo")
        gate_done, up_done, silu_done, prod_done = sem("f_gate_done"), sem("f_up_done"), sem("f_silu_done"), sem("f_prod_done")
        inner_hi, inner_lo = sem("f_inner_hi"), sem("f_inner_lo")
        down_used, y_done, x_done, stored = sem("f_down_used"), sem("f_y_done"), sem("f_x_done"), sem("f_stored")

        LAST = GROUPS - 1
        weights = (gate, up, down)
        FLIP = 2 * CHUNKS

        def groups(eng, group):
            group(0, True, False)
            with eng.Fori(1, LAST) as g:
                group(g, False, False)
            group(LAST, False, True)

        def piece(w, c):
            if w is down:
                return [part[:, c, :] for part in w]
            return [part[:, c, :, :].rearrange("p c n -> p (c n)") for part in w]

        with nc.Block() as block:
            @block.sync
            def _(sp):
                sp.dma_start(scale[:, :], scales.partition_broadcast(P)).then_inc(scale_loaded, 16)
                for c in range(CHUNKS):
                    for n, src in enumerate((gate_c, up_c, down_c)):
                        if c:
                            sp.wait_ge(w_lo, 3 * (c - 1) + n + 1)
                        sp.dma_start(raw[n][:, :], src[c, :, :]).then_inc(raw_loaded[n], 16)

                def group(g, first, last):
                    for tt in range(4):
                        t = 4 * g + tt
                        sp.wait_ge(x_done, t + 1)
                        sp.dma_start(out[bass.ds(t * P, P), :].rearrange("(a p) f -> p a f", a=1), x[:, bass.ds(t, 1), :]).then_inc(stored, 16)

                groups(sp, group)
                sp.wait_ge(stored, 16 * TILES)

            @block.gpsimd
            def _(pool):
                def group(g, first, last):
                    for tt in range(4):
                        ln.power(pool, 4 * g + tt)

                groups(pool, group)

            @block.scalar
            def _(act):
                def flipped(g):
                    for tt in range(4):
                        act.wait_ge(t_done, 4 * g + tt + 1)
                        ring = tt if known(g) and g == 0 else (FLIP + tt) % 4
                        hi_part(act, [w[:, :, tt * P:(tt + 1) * P] for w in ht], ps_r[:, ring, :].rearrange("p (c n) -> p c n", c=KC)).then_inc(h_hi, 1)

                def weight_hi(c):
                    for n, w in enumerate(weights):
                        act.wait_ge(raw_loaded[n], 16 * (c + 1))
                        hi_part(act, piece(w, c), raw[n][:, :]).then_inc(w_hi, 1)

                def group(g, first, last):
                    for c in range(CHUNKS):
                        at = CHUNKS * g + c
                        if first and c + 1 < CHUNKS:
                            weight_hi(c + 1)
                        act.wait_ge(gate_done, at + 1)
                        if not (first and c == 0):
                            act.wait_ge(inner_lo, at)
                        act.activation(act_buf[:, :], ps_r[:, 2 * c % 4, :], ACT.Silu, scale=scale[:, 0:1]).then_inc(silu_done, 1)
                        act.wait_ge(prod_done, at + 1)
                        if c >= 2:
                            act.wait_ge(down_used, (CHUNKS - 1) * g + c - 1)
                        elif not first:
                            act.wait_ge(y_done, 4 * g)
                        hi_part(act, [w[:, :] for w in inner[c % 2]], act_buf[:, :]).then_inc(inner_hi, 1)
                    if not last:
                        flipped(g + 1)

                act.wait_ge(scale_loaded, 16)
                weight_hi(0)
                flipped(0)
                groups(act, group)

            @block.vector
            def _(dve):
                def normalize(g, tt):
                    t = 4 * g + tt
                    par = tt % 2
                    tile = x[:, bass.ds(t, 1), :].rearrange("p a f -> p (a f)")
                    ln.stats(dve, tile, t, par)
                    ln.aggregate(dve, t, par)
                    ln.variance(dve, t, par)
                    if not known(g) or g >= 1:
                        dve.wait_ge(t_done, 4 * (g - 1) + tt + 1)
                    ln.apply(dve, h[:, tt, :], tile, t).then_inc(h_done, 1)

                def flipped(g):
                    for tt in range(4):
                        dve.wait_ge(h_hi, 4 * g + tt + 1)
                        ring = tt if known(g) and g == 0 else (FLIP + tt) % 4
                        lo_part(dve, [w[:, :, tt * P:(tt + 1) * P] for w in ht], ps_r[:, ring, :].rearrange("p (c n) -> p c n", c=KC)).then_inc(h_lo, 1)

                def weight_lo(c):
                    for n, w in enumerate(weights):
                        dve.wait_ge(w_hi, 3 * c + n + 1)
                        lo_part(dve, piece(w, c), raw[n][:, :]).then_inc(w_lo, 1)

                def group(g, first, last):
                    for c in range(CHUNKS):
                        at = CHUNKS * g + c
                        if first and c + 1 < CHUNKS:
                            weight_lo(c + 1)
                        if not last and 2 <= c < 6:
                            normalize(g + 1, c - 2)
                        dve.wait_ge(up_done, at + 1)
                        dve.wait_ge(silu_done, at + 1)
                        dve.scalar_tensor_tensor(act_buf[:, :], ps_r[:, (2 * c + 1) % 4, :], scale[:, 1:2], act_buf[:, :],
                                                 ALU.mult, ALU.mult).then_inc(prod_done, 1)
                        dve.wait_ge(inner_hi, at + 1)
                        lo_part(dve, [w[:, :] for w in inner[c % 2]], act_buf[:, :]).then_inc(inner_lo, 1)
                    if not last:
                        flipped(g + 1)
                    for tt in range(4):
                        t = 4 * g + tt
                        dve.wait_ge(y_done, t + 1)
                        tile = x[:, bass.ds(t, 1), :].rearrange("p a f -> p (a f)")
                        dve.scalar_tensor_tensor(tile, ps_y[:, tt, :], scale[:, 2:3], tile, ALU.mult, ALU.add).then_inc(x_done, 1)

                dve.wait_ge(scale_loaded, 16)
                for tt in range(4):
                    normalize(0, tt)
                weight_lo(0)
                flipped(0)
                groups(dve, group)

            @block.tensor
            def _(pe):
                def flip(g):
                    for tt in range(4):
                        pe.wait_ge(h_done, 4 * g + tt + 1)
                        ring = tt if known(g) and g == 0 else (FLIP + tt) % 4
                        if not known(g) or g >= 1:
                            pe.wait_ge((silu_done, prod_done)[tt % 2], CHUNKS * g - (1 if tt < 2 else 0))
                        for c in range(KC):
                            last = pe.transpose(ps_r[:, ring, c * P:(c + 1) * P], h[:, tt, c * P:(c + 1) * P], ident[:, :])
                        last.then_inc(t_done, 1)

                def project(w, c, bank, done):
                    for k in range(KC):
                        for n, (a, b) in enumerate(PASSES):
                            last = pe.matmul(ps_r[:, bank, :], w[a][:, c, k, :], ht[b][:, k, :], start=(k == 0 and n == 0), stop=(k == KC - 1 and n == 2))
                    last.then_inc(done, 1)

                def multiply_down(g, c, first):
                    pe.wait_ge(inner_lo, CHUNKS * g + c + 1)
                    if first:
                        pe.wait_ge(w_lo, 3 * c + 3)
                    for tt in range(4):
                        if c == 0 and not first:
                            pe.wait_ge(x_done, 4 * (g - 1) + tt + 1)
                        for n, (a, b) in enumerate(PASSES):
                            last = pe.matmul(ps_y[:, tt, :], inner[c % 2][a][:, tt * P:(tt + 1) * P], down[b][:, c, :],
                                             start=(c == 0 and n == 0), stop=(c == CHUNKS - 1 and n == 2))
                        if c == CHUNKS - 1:
                            last.then_inc(y_done, 1)
                    if c < CHUNKS - 1:
                        last.then_inc(down_used, 1)

                def group(g, first, last):
                    for c in range(CHUNKS):
                        if c == 0:
                            pe.wait_ge(h_lo, 4 * g + 4)
                        for n, (w, read, done) in enumerate(((gate, silu_done, gate_done), (up, prod_done, up_done))):
                            if first:
                                pe.wait_ge(w_lo, 3 * c + n + 1)
                            if c >= 2:
                                pe.wait_ge(read, CHUNKS * g + c - 1)
                            project(w, c, (2 * c + n) % 4, done)
                        if c >= 1:
                            multiply_down(g, c - 1, first)
                    if not last:
                        flip(g + 1)
                    multiply_down(g, CHUNKS - 1, first)

                flip(0)
                groups(pe, group)


def lay_out(inputs):
    import numpy as np

    def a(name):
        return np.asarray(inputs[name])

    def rows(w, n):
        return np.ascontiguousarray(w.T.reshape(-1, P, n, w.shape[0] // n).transpose(2, 1, 0, 3))

    def padded(w):
        return np.concatenate([w, np.zeros((CHUNKS * P - INTER, w.shape[1]), w.dtype)], axis=0)

    def kv_weights():
        down = np.concatenate([a("L1_attn_Wk_down").T, a("L1_attn_Wv_down").T], axis=1)
        by_row = [w.reshape(-1, P, w.shape[1]).transpose(1, 0, 2).reshape(P, -1) for w in (down, a("L1_attn_Wk_up").T, a("L1_attn_Wv_up").T)]
        return np.concatenate(by_row, axis=1).reshape(P, TILES, KV_PIECE).transpose(1, 0, 2)

    arrays = {
        "in_x": a("L0_attn_data").reshape(TOKENS, HID),
        "in_mask_t": a("L0_attn_mask").T,
        "in_w0_t": a("L0_attn_weight").T,
        "in_bias0": a("L0_attn_bias"),
        "in_router_t": a("L0_ffn_router_weight").T,
        "in_router_bias": a("L0_ffn_router_bias"),
        "in_expert_bias": a("L0_ffn_expert_bias"),
        "in_kv_weights": kv_weights(),
        "in_wq_g": rows(a("L1_attn_Wq"), KV_HEADS),
        "in_wo_g": a("L1_attn_Wo").T.reshape(KV_HEADS, GROUP, HEAD, HID).transpose(0, 2, 1, 3),
        "in_gate_c": rows(padded(a("L1_ffn_gate_w")), CHUNKS).reshape(CHUNKS, P, HID),
        "in_up_c": rows(padded(a("L1_ffn_up_w")), CHUNKS).reshape(CHUNKS, P, HID),
        "in_down_c": padded(a("L1_ffn_down_w").T).reshape(CHUNKS, P, HID),
        "in_scales": np.stack([a("L1_ffn_gate_scale"), a("L1_ffn_up_scale"), a("L1_ffn_down_scale")]),
    }
    return {name: np.ascontiguousarray(v) for name, v in arrays.items()}


def kernel(**inputs):
    import concourse.bacc as bacc
    from concourse.bass_utils import run_bass_kernel_spmd

    nc = bacc.Bacc("TRN2", target_bir_lowering=False, num_devices=1)
    arrays = lay_out(inputs)
    args = [nc.dram_tensor(name, a.shape, mybir.dt.from_np(a.dtype), kind="ExternalInput").ap() for name, a in arrays.items()]
    out = nc.dram_tensor("out", (TOKENS, HID), F32, kind="ExternalOutput").ap()
    build(nc, *args, out)
    result = run_bass_kernel_spmd(nc, [arrays], core_ids=[0])
    return result.results[0]["out"].reshape(BATCH, SEQ, HID)
```

```python
from contextlib import ExitStack

import concourse.bass as bass
from concourse import mybir

F32 = mybir.dt.float32
F32R = mybir.dt.float32r
I32 = mybir.dt.int32
ALU = mybir.AluOpType
ACT = mybir.ActivationFunctionType
AX_X = mybir.AxisListType.X

P = 128
HID = 512
KC = HID // P
BATCH, SEQ = 8, 256
TOKENS = BATCH * SEQ
TILES = TOKENS // P
EXPERTS = 64
BLOCK = 32
EPS = 1e-5

KV_HEADS = 8
GROUP = 4
HEAD = 128
LATENT = 32
PAIRS = BATCH // 2
PAIR = 2 * SEQ
KV_DOWN, KV_UP = KC * 2 * KV_HEADS * LATENT, 2 * KV_HEADS * HEAD
KV_PIECE = (KV_DOWN + 2 * KV_UP) // TILES
SCALE = float(HEAD) ** -0.5
MASKED = -1.0e30

INTER = 1376
CHUNKS = -(-INTER // P)
GROUPS = TILES // 4

HI, LO = 0, 1
PASSES = ((HI, HI), (LO, HI), (HI, LO))


def known(t):
    return isinstance(t, int)


def skewed(eng, depth, body, first=None, tail=None):
    if first is None:
        first = depth + depth % 2 + 2
    for i in range(first):
        body(i, i % 2, lambda k, i=i: i - k >= 0)
    with eng.Fori(first // 2, TILES // 2) as j:
        for par in range(2):
            body(2 * j + par, par, lambda k: True)
    for i in range(TILES, TILES + depth):
        body(i, i % 2, lambda k, i=i: i - k < TILES)
        if tail:
            tail(i - TILES)


class LayerNorm:

    def __init__(self, sb, sem, name, half, ready):
        self.bn = sb(f"bn_{name}", [P, 2, 6])
        self.mv = sb(f"mv_{name}", [P, 2, 2])
        self.neg_mean = sb(f"neg_mean_{name}", [P, TILES])
        self.ve = sb(f"ve_{name}", [P, TILES])
        self.factors = sb(f"factors_{name}", [P, TILES, 2])
        self.half = half
        self.ready = ready
        self.bn_done = sem(f"bn_done_{name}")
        self.mv_done = sem(f"mv_done_{name}")
        self.ve_done = sem(f"ve_done_{name}")
        self.rstd_done = sem(f"rstd_done_{name}")
        self.shift_done = sem(f"shift_done_{name}")

    def stats(self, dve, src, t, par):
        dve.bn_stats(self.bn[:, par, :], src).then_inc(self.bn_done, 1)

    def aggregate(self, dve, t, par):
        wait_alone(dve, self.bn_done, t + 1, self.ready)
        dve.bn_aggr(self.mv[:, par, :], self.bn[:, par, :]).then_inc(self.mv_done, 1)

    def variance(self, dve, t, par):
        dve.wait_ge(self.mv_done, t + 1)
        dve.tensor_scalar(self.neg_mean[:, bass.ds(t, 1)], self.mv[:, par, 0:1], -1.0, None, ALU.mult)
        dve.tensor_scalar(self.ve[:, bass.ds(t, 1)], self.mv[:, par, 1:2], EPS, None, ALU.add).then_inc(self.ve_done, 1)

    def power(self, pool, t):
        pool.wait_ge(self.ve_done, t + 1)
        pool.tensor_tensor(self.factor(t, 0), self.ve[:, bass.ds(t, 1)], self.half, ALU.pow).then_inc(self.rstd_done, 1)
        pool.wait_ge(self.rstd_done, t + 1)
        pool.tensor_tensor(self.factor(t, 1), self.neg_mean[:, bass.ds(t, 1)], self.factor(t, 0), ALU.mult).then_inc(self.shift_done, 1)

    def factor(self, t, n):
        return self.factors[:, bass.ds(t, 1), n:n + 1].rearrange("p t n -> p (t n)")

    def apply(self, dve, out, src, t):
        dve.wait_ge(self.shift_done, t + 1)
        return dve.tensor_scalar(out, src, self.factor(t, 0), self.factor(t, 1), ALU.mult, ALU.add)

    def activate(self, act, out, src, t):
        act.wait_ge(self.shift_done, t + 1)
        return act.activation(out, src, ACT.Identity, bias=self.factor(t, 1), scale=self.factor(t, 0))


def wait_alone(eng, done, value, ready):
    if not known(value):
        eng.lower_val(value)
    eng.wait_ge(ready, 1)
    eng.wait_ge(done, value)


def tile_of(x, t):
    return x[:, bass.ds(t, 1), :].rearrange("p a f -> p (a f)")


def hi_part(act, parts, src):
    return act.activation(parts[HI], src, ACT.Copy)


def lo_part(dve, parts, src):
    return dve.tensor_tensor(parts[LO], src, parts[HI].bitcast(F32), ALU.subtract)


def build(nc, x_in, mask_t, w0_t, bias0, router_t, router_bias, expert_bias, kv_weights,
          wq_g, wo_g, gate_c, up_c, down_c, scales, out):
    whole = ExitStack()

    def sem(name):
        return whole.enter_context(nc.semaphore(name))

    def sb(name, shape, dt=F32, stack=whole):
        return stack.enter_context(nc.sbuf_tensor(name, shape, dt))

    def ps(name, shape, stack):
        return stack.enter_context(nc.psum_tensor(name, shape, F32))

    def split(name, shape, stack=whole):
        return [sb(name + "_hi", shape, F32R, stack), sb(name + "_lo", shape, F32R, stack)]

    k_scr = nc.dram_tensor("k_scratch", [KV_HEADS, P, TOKENS], F32, kind="Internal").ap()
    v_scr = nc.dram_tensor("v_scratch", [PAIRS, P, 4, KV_HEADS * HEAD], F32, kind="Internal").ap()

    with whole:
        x = sb("x", [P, TILES, HID])
        ident = sb("ident", [P, P])
        half = sb("half", [P, 1])
        consts = sem("consts")
        ln = [LayerNorm(sb, sem, f"ln{n}", half[:, 0:1], consts) for n in range(4)]

        with ExitStack() as held:
            h3 = split("h3", [P, KC, TOKENS], held)
            kv_w = split("kv_w", [P, TILES, KV_PIECE], held)
            stream = WeightStream(sem, sb, held)
            with ExitStack() as held_router:
                router = RouterWeights(sb, sem, held_router)
                block_sparse_linear(nc, sem, sb, ps, split, x, ident, half, consts, ln[0], x_in, mask_t, w0_t, bias0,
                                    lambda eng: router.load(eng, router_t, router_bias, expert_bias), kv_weights, kv_w)
                stored = routed_bias_and_keys(nc, sem, sb, ps, split, x, ident, ln[1], ln[2], router, h3, kv_w, stream, wq_g, k_scr, v_scr)
            attention(nc, sem, sb, ps, split, x, ident, h3, kv_w, stream, stored, wq_g, wo_g, k_scr, v_scr)
        feed_forward(nc, sem, sb, ps, split, x, ident, ln[3], gate_c, up_c, down_c, scales, out)


def block_sparse_linear(nc, sem, sb, ps, split, x, ident, half, consts, ln, x_in, mask_t, w0_t, bias0, load_next, kv_weights, kv_w):
    with ExitStack() as st:
        mask = sb("mask", [P, KC, HID], I32, st)
        w_raw = sb("w0_raw", [P, KC, HID], F32, st)
        w0 = split("w0", [P, KC, HID], st)
        bias = sb("bias0", [P, HID], F32, st)
        same_block = sb("same_block", [P, P], F32, st)
        row_sums = sb("row_sums", [P, KC * HID // BLOCK], F32, st)
        block_on = sb("block_on", [P, KC * HID // BLOCK], F32, st)
        h = sb("h0", [P, 2, HID], F32, st)
        ht = [split(f"h0t{n}", [P, KC, P], st) for n in range(2)]
        kv_raw = sb("kv_raw", [P, 2, KV_PIECE], F32, st)
        ps_t = ps("a_ps_t", [P, 2, HID], st)
        ps_y = ps("a_ps_y", [P, 2, HID], st)
        ps_b = ps("a_ps_b", [P, HID], st)

        x_loaded = [sem(f"a_x_loaded{n}") for n in range(2)]
        mask_loaded, w_loaded, bias_loaded = sem("a_mask_loaded"), sem("a_w_loaded"), sem("a_bias_loaded")
        block_zeroed = sem("a_block_zeroed")
        zeroed, const_done = sem("a_zeroed"), sem("a_const_done")
        rows_done, blocks_done, on_done, masked = sem("a_rows_done"), sem("a_blocks_done"), sem("a_on_done"), sem("a_masked")
        w_hi_done, w_lo_done = sem("a_w_hi_done"), sem("a_w_lo_done")
        h_done, t_done, hi_done, lo_done = sem("a_h_done"), sem("a_t_done"), sem("a_hi_done"), sem("a_lo_done")
        y_done, xb_done, x_done = sem("a_y_done"), sem("a_xb_done"), sem("a_x_done")
        kv_loaded = [sem(f"a_kv_loaded{n}") for n in range(2)]
        kv_hi, kv_lo = sem("a_kv_hi"), sem("a_kv_lo")

        with nc.Block() as block:
            @block.sync
            def _(sp):
                def load(t, par):
                    if not known(t) or t >= 2:
                        sp.wait_ge(x_loaded[par], 8 * (t - par))
                    sp.dma_start(x[:, bass.ds(t, 1), :], x_in[bass.ds(t * P, P), :].rearrange("(a p) f -> p a f", a=1)).then_inc(x_loaded[par], 16)

                def load_kv(t, par):
                    if not known(t) or t >= 2:
                        sp.wait_ge(kv_lo, t - 1)
                    sp.dma_start(kv_raw[:, bass.ds(par, 1), :], kv_weights[bass.ds(t, 1), :, :].rearrange("a p n -> p a n")).then_inc(kv_loaded[par], 16)

                def body(i, par, live):
                    if live(0):
                        load(i, par)
                    if live(4):
                        load_kv(i - 4, par)

                skewed(sp, 4, body)

            @block.scalar
            def _(act):
                act.dma_start(mask[:, :, :], mask_t.rearrange("(c p) n -> p c n", p=P)).then_inc(mask_loaded, 16)
                act.dma_start(w_raw[:, :, :], w0_t.rearrange("(c p) n -> p c n", p=P)).then_inc(w_loaded, 16)
                act.dma_start(bias[:, :], bias0.partition_broadcast(P)).then_inc(bias_loaded, 16)
                load_next(act)
                act.wait_ge(masked, 1)
                hi_part(act, [w[:, :, :] for w in w0], w_raw[:, :, :]).then_inc(w_hi_done, 1)

                def body(i, par, live):
                    if live(2):
                        t, pt = i - 2, par
                        act.wait_ge(t_done, t + 1)
                        if not known(t) or t >= 2:
                            act.wait_ge(y_done, t - 1)
                        hi_part(act, [p[:, :, :] for p in ht[pt]], ps_t[:, pt, :].rearrange("p (c n) -> p c n", c=KC)).then_inc(hi_done, 1)
                    if live(1):
                        t, pt = i - 1, (par - 1) % 2
                        if not known(t) or t >= 2:
                            act.wait_ge(t_done, t - 1)
                        ln.activate(act, h[:, pt, :], tile_of(x, t), t).then_inc(h_done, 1)
                    if live(3):
                        t, pt = i - 3, (par - 3) % 2
                        act.wait_ge(kv_loaded[pt], 8 * (t - pt) + 16)
                        hi_part(act, [tile_of(w, t) for w in kv_w], kv_raw[:, pt, :]).then_inc(kv_hi, 1)

                skewed(act, 3, body)

            @block.gpsimd
            def _(pool):
                pool.memset(half[:, :], -0.5).then_inc(zeroed, 1)
                pool.memset(ident[:, :], 0.0).then_inc(zeroed, 1)
                pool.wait_ge(zeroed, 2)
                pool.affine_select(out=ident[:, :], in_=ident[:, :], compare_op=ALU.not_equal, fill=1.0, base=0,
                                   pattern=[[-1, P]], channel_multiplier=1).then_inc(consts, 1)
                pool.wait_ge(consts, 1)
                pool.wait_ge(bias_loaded, 16)

                def body(i, par, live):
                    if live(2):
                        t = i - 2
                        pool.wait_ge(h_done, t + 1)
                        pool.tensor_tensor(tile_of(x, t), tile_of(x, t), bias[:, :], ALU.add).then_inc(xb_done, 1)
                    if live(0):
                        ln.power(pool, i)

                skewed(pool, 2, body)

            @block.vector
            def _(dve):
                dve.memset(same_block[:, :], 0.0).then_inc(block_zeroed, 1)
                dve.wait_ge(block_zeroed, 1)
                for q in range(0, P, BLOCK):
                    last = dve.memset(same_block[q:q + BLOCK, q:q + BLOCK], 1.0)
                last.then_inc(const_done, 1)
                dve.wait_ge(mask_loaded, 16)
                dve.tensor_reduce(row_sums[:, :], mask[:, :, :].rearrange("p c (n b) -> p (c n) b", b=BLOCK), AX_X, ALU.add).then_inc(rows_done, 1)
                dve.wait_ge(blocks_done, 1)
                dve.tensor_scalar(block_on[:, :], ps_b[:, 0:KC * HID // BLOCK], 0.0, None, ALU.is_gt).then_inc(on_done, 1)
                dve.wait_ge(w_loaded, 16)
                dve.wait_ge(on_done, 1)
                w_blocks = w_raw[:, :, :].rearrange("p c (n b) -> p (c n) b", b=BLOCK)
                dve.tensor_tensor(w_blocks, w_blocks, block_on[:, :].unsqueeze(2).to_broadcast([P, KC * HID // BLOCK, BLOCK]), ALU.mult).then_inc(masked, 1)
                dve.wait_ge(w_hi_done, 1)
                lo_part(dve, [w[:, :, :] for w in w0], w_raw[:, :, :]).then_inc(w_lo_done, 1)

                def body(i, par, live):
                    if live(4):
                        t, pt = i - 4, par
                        dve.wait_ge(y_done, t + 1)
                        dve.wait_ge(xb_done, t + 1)
                        dve.tensor_tensor(tile_of(x, t), ps_y[:, pt, :], tile_of(x, t), ALU.add).then_inc(x_done, 1)
                    if live(0):
                        dve.wait_ge(x_loaded[par], 8 * (i - par) + 16)
                        ln.stats(dve, x[:, bass.ds(i, 1), :], i, par)
                    if live(2):
                        t, pt = i - 2, par
                        dve.wait_ge(hi_done, t + 1)
                        lo_part(dve, [p[:, :, :] for p in ht[pt]], ps_t[:, pt, :].rearrange("p (c n) -> p c n", c=KC)).then_inc(lo_done, 1)
                    if live(0):
                        ln.aggregate(dve, i, par)
                    if live(4):
                        dve.wait_ge(kv_hi, i - 4 + 1)
                        lo_part(dve, [tile_of(w, i - 4) for w in kv_w], kv_raw[:, par, :]).then_inc(kv_lo, 1)
                    if live(0):
                        ln.variance(dve, i, par)

                skewed(dve, 4, body)

            @block.tensor
            def _(pe):
                pe.wait_ge(rows_done, 1)
                pe.wait_ge(const_done, 1)
                pe.matmul(ps_b[:, 0:KC * HID // BLOCK], same_block[:, :], row_sums[:, :], start=True, stop=True).then_inc(blocks_done, 1)
                pe.wait_ge(consts, 1)

                def body(i, par, live):
                    if live(2):
                        t, pt = i - 2, par
                        pe.wait_ge(h_done, t + 1)
                        if not known(t) or t >= 2:
                            pe.wait_ge(lo_done, t - 1)
                        for c in range(KC):
                            last = pe.transpose(ps_t[:, pt, c * P:(c + 1) * P], h[:, pt, c * P:(c + 1) * P], ident[:, :])
                        last.then_inc(t_done, 1)
                    if live(3):
                        t, pt = i - 3, (par - 3) % 2
                        if known(t) and t == 0:
                            pe.wait_ge(w_lo_done, 1)
                        pe.wait_ge(lo_done, t + 1)
                        if not known(t) or t >= 2:
                            pe.wait_ge(x_done, t - 1)
                        for c in range(KC):
                            for n, (a, b) in enumerate(PASSES):
                                last = pe.matmul(ps_y[:, pt, :], ht[pt][a][:, c, :], w0[b][:, c, :],
                                                 start=(c == 0 and n == 0), stop=(c == KC - 1 and n == 2))
                        last.then_inc(y_done, 1)

                skewed(pe, 3, body)


class WeightStream:

    def __init__(self, sem, sb, stack):
        self.raw = sb("w_raw", [P, 4, HID], F32, stack)
        self.raw_loaded, self.w_hi, self.w_lo = sem("raw_loaded"), sem("w_hi"), sem("w_lo")

    def load(self, sp, src, sets):
        if not known(sets) or sets >= 1:
            sp.wait_ge(self.w_lo, 4 * sets)
        sp.dma_start(self.raw[:, :, :], src).then_inc(self.raw_loaded, 16)

    def hi(self, act, w, n, sets):
        if n == 0:
            act.wait_ge(self.raw_loaded, 16 * sets + 16)
        hi_part(act, [part[:, n, :] for part in w], self.raw[:, n, :]).then_inc(self.w_hi, 1)

    def lo(self, dve, w, n, sets):
        dve.wait_ge(self.w_hi, 4 * sets + n + 1)
        lo_part(dve, [part[:, n, :] for part in w], self.raw[:, n, :]).then_inc(self.w_lo, 1)


def attention_weights(kv_w):
    whole = [w[:, :, :].rearrange("p a n -> p (a n)") for w in kv_w]
    size = KC * GROUP * HEAD
    return [[w[:, n * size:(n + 1) * size].rearrange("p (c n) -> p c n", n=HID) for w in whole] for n in range(3)]


class RouterWeights:

    def __init__(self, sb, sem, stack):
        self.router = sb("router", [P, KC, EXPERTS], F32, stack)
        self.logit_bias = sb("r_bias", [P, EXPERTS], F32, stack)
        self.expert_bias = sb("e_bias", [P, HID], F32, stack)
        self.loaded = sem("b_loaded")

    def load(self, eng, router_t, router_bias, expert_bias):
        eng.dma_start(self.router[:, :, :], router_t.rearrange("(c p) n -> p c n", p=P)).then_inc(self.loaded, 16)
        eng.dma_start(self.logit_bias[:, :], router_bias.partition_broadcast(P)).then_inc(self.loaded, 16)
        eng.dma_start(self.expert_bias[0:EXPERTS, :], expert_bias).then_inc(self.loaded, 16)


class RoutedBias:

    DEPTH = 10

    def __init__(self, sem, sb, bank, x, ident, ln, ln_next, weights, h3, st):
        self.x, self.ident, self.ln, self.ln_next, self.weights, self.h3 = x, ident, ln, ln_next, weights, h3
        self.h = sb("h1", [P, 2, HID], F32, st)
        self.ht = sb("h1t", [P, 2, HID], F32, st)
        self.h_next = sb("h2", [P, 2, HID], F32, st)
        self.logits = sb("logits", [P, 2, EXPERTS], F32, st)
        self.neg_max = sb("r_neg_max", [P, 2], F32, st)
        self.e = sb("r_exp", [P, 2, EXPERTS], F32, st)
        self.total = sb("r_total", [P, 2], F32, st)
        self.top = sb("r_top", [P, 2, 8], F32, st)
        self.rest = sb("r_rest", [P, 2, EXPERTS], F32, st)
        self.top_sum = sb("r_top_sum", [P, 2], F32, st)
        self.inv_total = sb("r_inv_total", [P, TILES], F32, st)
        self.weight_sum = sb("r_weight_sum", [P, 2], F32, st)
        self.one_zero = sb("r_one_zero", [P, 2], F32, st)
        self.combined = sb("r_combined", [P, 2, 2], F32, st)
        self.chosen = sb("r_chosen", [P, 2, P], F32, st)
        self.chosen_t = sb("r_chosen_t", [P, 2, P], F32, st)
        self.ps_t, self.ps_l, self.ps_m, self.ps_n = [bank[:, n, :] for n in range(4)]
        self.ps_c = self.ps_t
        self.zeroed = sem("b_zeroed")
        self.h_done = sem("b_h_done")
        self.t_done = sem("b_t_done")
        self.ht_done = sem("b_ht_done")
        self.l_done = sem("b_l_done")
        self.lb_done = sem("b_lb_done")
        self.max_done = sem("b_max_done")
        self.exp_done = sem("b_exp_done")
        self.top_done = sem("b_top_done")
        self.rest_done = sem("b_rest_done")
        self.inv_done = sem("b_inv_done")
        self.chosen_done = sem("b_chosen_done")
        self.sum_done = sem("b_sum_done")
        self.combined_done = sem("b_combined_done")
        self.scaled_done = sem("b_scaled_done")
        self.ct_done = sem("b_ct_done")
        self.ctc_done = sem("b_ctc_done")
        self.mix_done = sem("b_mix_done")
        self.x_done = sem("b_x_done")
        self.h_next_done = sem("b_h_next_done")
        self.tn_done = sem("b_tn_done")
        self.hi_done = sem("b_hi_done")
        self.lo_done = sem("b_lo_done")

    def transposed(self):
        return self.ps_n.rearrange("p (c n) -> p c n", c=KC)

    def set_constants(self, pool):
        for n, (part, value) in enumerate(((self.one_zero[:, 0:1], 1.0), (self.one_zero[:, 1:2], 0.0),
                                           (self.weights.expert_bias[EXPERTS:P, :], 0.0), (self.chosen[:, :, EXPERTS:P], 0.0))):
            if n:
                pool.wait_ge(self.zeroed, n)
            pool.memset(part, value).then_inc(self.zeroed, 1)

    def await_constants(self, eng):
        eng.wait_ge(self.zeroed, 4)
        eng.wait_ge(self.weights.loaded, 48)

    def pool_body(self, pool, i, par, live):
        if live(7):
            self.ln_next.power(pool, i - 7)
        if live(0):
            self.ln.power(pool, i)

    def act_body(self, act, i, par, live):
        odd = (par - 1) % 2
        if live(4):
            t, pt = i - 4, par
            act.wait_ge(self.max_done, t + 1)
            if not known(t) or t >= 2:
                act.wait_ge(self.chosen_done, t - 1)
            act.activation(self.e[:, pt, :], self.logits[:, pt, :], ACT.Exp, bias=self.neg_max[:, pt:pt + 1],
                           accum_out=self.total[:, pt:pt + 1]).then_inc(self.exp_done, 1)
        if live(5):
            t, pt = i - 5, odd
            act.wait_ge(self.combined_done, t + 1)
            act.activation(tile_of(self.x, t), tile_of(self.x, t), ACT.Identity, bias=self.combined[:, pt, 1:2],
                           scale=self.combined[:, pt, 0:1]).then_inc(self.scaled_done, 1)
            act.wait_ge(self.ct_done, t + 1)
            if not known(t) or t >= 2:
                act.wait_ge(self.mix_done, t - 1)
            act.activation(self.chosen_t[:, pt, :], self.ps_c[:, 0:P], ACT.Copy).then_inc(self.ctc_done, 1)
        if live(10):
            t = i - 10
            act.wait_ge(self.tn_done, t + 1)
            hi_part(act, [p[:, :, bass.ds(t * P, P)] for p in self.h3], self.transposed()).then_inc(self.hi_done, 1)
        if live(8):
            t, pt = i - 8, par
            if not known(t) or t >= 2:
                act.wait_ge(self.tn_done, t - 1)
            self.ln_next.activate(act, self.h_next[:, pt, :], tile_of(self.x, t), t).then_inc(self.h_next_done, 1)
        if live(1):
            t, pt = i - 1, odd
            if not known(t) or t >= 2:
                act.wait_ge(self.t_done, t - 1)
            self.ln.activate(act, self.h[:, pt, :], tile_of(self.x, t), t).then_inc(self.h_done, 1)
        if live(2):
            t, pt = i - 2, par
            act.wait_ge(self.t_done, t + 1)
            if not known(t) or t >= 2:
                act.wait_ge(self.l_done, t - 1)
            act.activation(self.ht[:, pt, :], self.ps_t, ACT.Copy).then_inc(self.ht_done, 1)

    def dve_body(self, dve, i, par, live):
        odd = (par - 1) % 2
        t3, t4, t6, t7 = i - 3, i - 4, i - 6, i - 7
        if live(7):
            wait_alone(dve, self.x_done, t7 + 1, self.ln.ready)
            self.ln_next.stats(dve, self.x[:, bass.ds(t7, 1), :], t7, odd)
        if live(0):
            self.ln.stats(dve, self.x[:, bass.ds(i, 1), :], i, par)
        if live(7):
            self.ln_next.aggregate(dve, t7, odd)
        if live(4):
            wait_alone(dve, self.exp_done, t4 + 1, self.ln.ready)
            dve.max(self.top[:, par, :], self.e[:, par, :]).then_inc(self.top_done, 1)
        if live(0):
            self.ln.aggregate(dve, i, par)
        if live(7):
            self.ln_next.variance(dve, t7, odd)
        if live(4):
            wait_alone(dve, self.top_done, t4 + 1, self.ln.ready)
            dve.match_replace(self.rest[:, par, :], self.top[:, par, :], self.e[:, par, :], 0.0).then_inc(self.rest_done, 1)
        if live(0):
            self.ln.variance(dve, i, par)
        if live(4):
            dve.reduce_sum(self.top_sum[:, par:par + 1], self.top[:, par, :], AX_X)
            dve.reciprocal(self.inv_total[:, bass.ds(t4, 1)], self.total[:, par:par + 1]).then_inc(self.inv_done, 1)
            dve.wait_ge(self.rest_done, t4 + 1)
            if not known(t4) or t4 >= 2:
                dve.wait_ge(self.ct_done, t4 - 1)
            dve.tensor_tensor(self.chosen[:, par, 0:EXPERTS], self.e[:, par, :], self.rest[:, par, :], ALU.subtract).then_inc(self.chosen_done, 1)
            dve.wait_ge(self.inv_done, t4 + 1)
            dve.tensor_tensor(self.weight_sum[:, par:par + 1], self.top_sum[:, par:par + 1], self.inv_total[:, bass.ds(t4, 1)], ALU.mult).then_inc(self.sum_done, 1)
        if live(6):
            dve.wait_ge(self.mix_done, t6 + 1)
            dve.wait_ge(self.scaled_done, t6 + 1)
            dve.scalar_tensor_tensor(tile_of(self.x, t6), self.ps_m, self.inv_total[:, bass.ds(t6, 1)], tile_of(self.x, t6),
                                     ALU.mult, ALU.add).then_inc(self.x_done, 1)
        if live(4):
            dve.wait_ge(self.sum_done, t4 + 1)
            if not known(t4) or t4 >= 2:
                dve.wait_ge(self.scaled_done, t4 - 1)
            dve.scalar_tensor_tensor(self.combined[:, par, :], self.ln.factors[:, bass.ds(t4, 1), :].rearrange("p t n -> p (t n)"),
                                     self.weight_sum[:, par:par + 1], self.one_zero[:, :], ALU.mult, ALU.add).then_inc(self.combined_done, 1)
        if live(3):
            dve.wait_ge(self.l_done, t3 + 1)
            if not known(t3) or t3 >= 2:
                dve.wait_ge(self.exp_done, t3 - 1)
            dve.tensor_tensor(self.logits[:, odd, :], self.ps_l[:, 0:EXPERTS], self.weights.logit_bias[:, :], ALU.add).then_inc(self.lb_done, 1)
        if live(10):
            t = i - 10
            dve.wait_ge(self.hi_done, t + 1)
            lo_part(dve, [p[:, :, bass.ds(t * P, P)] for p in self.h3], self.transposed()).then_inc(self.lo_done, 1)
        if live(3):
            dve.wait_ge(self.lb_done, t3 + 1)
            dve.tensor_reduce(self.neg_max[:, odd:odd + 1], self.logits[:, odd, :], AX_X, ALU.max, negate=True).then_inc(self.max_done, 1)

    def pe_body(self, pe, i, par, live):
        odd = (par - 1) % 2
        if live(5):
            pe.wait_ge(self.chosen_done, i - 5 + 1)
            if live(3):
                pe.wait_ge(self.ht_done, i - 3 + 1)
            else:
                pe.wait_ge(self.ctc_done, i - 5)
            pe.transpose(self.ps_c[:, 0:P], self.chosen[:, odd, :], self.ident[:, :]).then_inc(self.ct_done, 1)
        if live(10):
            t = i - 10
            pe.wait_ge(self.h_next_done, t + 1)
            if not known(t) or t >= 1:
                pe.wait_ge(self.lo_done, t)
            for c in range(KC):
                last = pe.transpose(self.ps_n[:, c * P:(c + 1) * P], self.h_next[:, par, c * P:(c + 1) * P], self.ident[:, :])
            last.then_inc(self.tn_done, 1)
        if live(6):
            t = i - 6
            pe.wait_ge(self.ctc_done, t + 1)
            if not known(t) or t >= 1:
                pe.wait_ge(self.x_done, t)
            pe.matmul(self.ps_m, self.chosen_t[:, par, :], self.weights.expert_bias[:, :], start=True, stop=True).then_inc(self.mix_done, 1)
        if live(3):
            t = i - 3
            pe.wait_ge(self.ht_done, t + 1)
            if not known(t) or t >= 1:
                pe.wait_ge(self.lb_done, t)
            for c in range(KC):
                last = pe.matmul(self.ps_l[:, 0:EXPERTS], self.ht[:, odd, c * P:(c + 1) * P], self.weights.router[:, c, :],
                                 start=(c == 0), stop=(c == KC - 1))
            last.then_inc(self.l_done, 1)
        if live(2):
            t = i - 2
            pe.wait_ge(self.h_done, t + 1)
            if not known(i) or i - 5 >= 0:
                pe.wait_ge(self.ctc_done, i - 5 + 1)
            elif t >= 1:
                pe.wait_ge(self.ht_done, t)
            for c in range(KC):
                last = pe.transpose(self.ps_t[:, c * P:(c + 1) * P], self.h[:, par, c * P:(c + 1) * P], self.ident[:, :])
            last.then_inc(self.t_done, 1)




def kv_tasks():
    tasks = []
    for quad in range(2):
        down = [("Z", quad, j, 0) for j in range(8)]
        flip = [("C", quad, jp, hg) for jp in range(4) for hg in range(2)]
        keys = [("K", quad, pair, g) for pair in range(2) for g in range(KV_HEADS)]
        values = [("V", quad, tile, part) for tile in range(8) for part in range(2)]
        tasks += down[0:4] + flip[0:2] + down[4:6] + flip[2:4] + down[6:8] + flip[4:6] + keys[0:2] + flip[6:8] + keys[2:] + values
    return tasks


def routed_bias_and_keys(nc, sem, sb, ps, split, x, ident, ln, ln_next, weights, h3, kv_w, stream, wq_g, k_scr, v_scr):
    SPAN = 4 * SEQ
    STAGES = 4
    DEPTH = RoutedBias.DEPTH
    tasks = kv_tasks()
    at = {task: n for n, task in enumerate(tasks)}
    hi_order = [n for n, task in enumerate(tasks) if task[0] == "C"]
    lo_count = {n: k + 1 for k, n in enumerate(hi_order)}
    down_order = [n for n, task in enumerate(tasks) if task[0] == "Z"]
    down_count = {n: k + 1 for k, n in enumerate(down_order)}
    stage_order = [n for n, task in enumerate(tasks) if task[0] in "KV"]
    stage_count = {n: k for k, n in enumerate(stage_order)}

    with ExitStack() as st:
        whole_w = [w[:, :, :].rearrange("p a n -> p (a n)") for w in kv_w]
        down_w = [w[:, 0:KV_DOWN].rearrange("p (c n) -> p c n", c=KC) for w in whole_w]
        up_w = [[w[:, KV_DOWN + n * KV_UP:KV_DOWN + (n + 1) * KV_UP].rearrange("p (c n) -> p c n", c=2) for w in whole_w] for n in range(2)]
        z = stream.raw[:, :, :].rearrange("p (j h) (h2 t l) -> p j (h h2) t l", j=2, h2=4, t=2)
        latent = split("latent", [P, 4, 4, KV_HEADS, BLOCK], st)
        bank = ps("kv_banks", [P, 8, HID], st)
        with ExitStack() as shared:
            routed = RoutedBias(sem, sb, bank[:, 4:8, :], x, ident, ln, ln_next, weights, h3, shared)
        stage = [sb(f"kv_stage{n}", [P, HID], F32, st) for n in range(STAGES)]

        task_done, z_done, hi_done, lo_done = sem("kv_task_done"), sem("kv_z_done"), sem("kv_hi_done"), sem("kv_lo_done")
        staged = sem("kv_staged")
        stored = [sem(f"kv_stored{n}") for n in range(STAGES)]

        begin = DEPTH - TILES // 2 - 1
        paired = DEPTH - begin
        bank_of = [n % 4 if n < paired else (n - paired + 4) % 8 for n in range(len(tasks))]

        def freed(eng, n):
            before = [m for m in range(n) if bank_of[m] == bank_of[n]]
            if not before:
                if bank_of[n] >= 4:
                    eng.wait_ge(routed.lo_done, TILES)
            elif before[-1] in down_count:
                eng.wait_ge(z_done, down_count[before[-1]])
            elif before[-1] in stage_count:
                eng.wait_ge(staged, stage_count[before[-1]] + 1)
            else:
                eng.wait_ge(lo_done, lo_count[before[-1]])

        def outlet(n):
            kind, quad, a, b = tasks[n]
            return ([p[:, a, :, 4 * b:4 * b + 4, :].rearrange("p b h m -> p h b m") for p in latent],
                    bank[:, bank_of[n], :].rearrange("p (h b m) -> p h b m", h=4, b=4))

        wq = attention_weights(kv_w)[0]
        query_weights = {at[("V", 1, 2 * n, 0)]: n for n in range(4)}

        def interleaved(eng, body, task):
            skewed(eng, DEPTH, lambda i, par, live: body(eng, i, par, live), first=DEPTH + DEPTH % 2,
                   tail=lambda n: task(n - begin) if n >= begin else None)
            for n in range(paired, len(tasks)):
                task(n)

        with nc.Block() as block:
            @block.gpsimd
            def _(pool):
                routed.set_constants(pool)
                skewed(pool, DEPTH, lambda i, par, live: routed.pool_body(pool, i, par, live), first=DEPTH + DEPTH % 2)

            @block.sync
            def _(sp):
                for k, n in enumerate(stage_order):
                    kind, quad, a, b = tasks[n]
                    sp.wait_ge(staged, k + 1)
                    if k >= STAGES:
                        sp.wait_ge(stored[k % STAGES], 16 * (k // STAGES))
                    if kind == "K":
                        pair = 2 * quad + a
                        dst = k_scr[b, :, pair * PAIR:(pair + 1) * PAIR]
                    else:
                        pair = 2 * quad + a // 4
                        dst = v_scr[pair, :, a % 4, b * HID:(b + 1) * HID]
                    sp.dma_start(dst, stage[k % STAGES][:, :]).then_inc(stored[k % STAGES], 16)
                    if n == at[("K", 1, 0, 2)]:
                        sp.wait_ge(task_done, at[("C", 1, 3, 1)] + 1)
                        stream.load(sp, wq_g[0, :, :, :], 0)

            @block.scalar
            def _(act):
                def task(n):
                    kind, quad, a, b = tasks[n]
                    act.wait_ge(task_done, n + 1)
                    if kind == "Z":
                        before = [at[("C", q, jp, 1)] for q, jp in [(quad, a // 2 - 2) if a >= 4 else (quad - 1, a // 2 + 2)] if q >= 0]
                        if before:
                            act.wait_ge(task_done, before[0] + 1)
                        act.activation(z[:, a // 2 % 2, :, a % 2, :].rearrange("p h (t l) -> p h t l", t=2),
                                       bank[:, bank_of[n], :].rearrange("p (t h l) -> p h t l", t=2, h=KV_HEADS), ACT.Copy).then_inc(z_done, 1)
                    else:
                        if kind == "C" and quad == 1:
                            act.wait_ge(task_done, at[("K", 0, 1, KV_HEADS - 1) if a < 2 else ("V", 0, 7, 1)] + 1)
                        if kind == "C":
                            parts, src = outlet(n)
                            hi_part(act, parts, src).then_inc(hi_done, 1)
                        else:
                            k = stage_count[n]
                            if k >= STAGES:
                                act.wait_ge(stored[k % STAGES], 16 * (k // STAGES))
                            else:
                                act.wait_ge(routed.lo_done, TILES)
                            act.activation(stage[k % STAGES][:, :], bank[:, bank_of[n], :], ACT.Copy).then_inc(staged, 1)
                        if n in query_weights:
                            stream.hi(act, wq, query_weights[n], 0)

                interleaved(act, routed.act_body, task)

            @block.vector
            def _(dve):
                routed.await_constants(dve)

                def task(n):
                    if n in lo_count:
                        dve.wait_ge(hi_done, lo_count[n])
                        parts, src = outlet(n)
                        lo_part(dve, parts, src).then_inc(lo_done, 1)
                    if n in query_weights:
                        stream.lo(dve, wq, query_weights[n], 0)

                interleaved(dve, routed.dve_body, task)

            @block.tensor
            def _(pe):
                routed.await_constants(pe)

                def task(n):
                    kind, quad, a, b = tasks[n]
                    freed(pe, n)
                    out = bank[:, bank_of[n], :]
                    if kind == "Z":
                        pe.wait_ge(routed.lo_done, (quad + 1) * TILES // 2)
                        for c in range(KC):
                            for m, (u, v) in enumerate(PASSES):
                                tokens = h3[u][:, c, quad * SPAN:(quad + 1) * SPAN].rearrange("p (n j) -> p n j", j=8)[:, :, a]
                                last = pe.matmul(out, tokens, down_w[v][:, c, :], start=(c == 0 and m == 0), stop=(c == KC - 1 and m == 2))
                    elif kind == "C":
                        pe.wait_ge(z_done, down_count[at[("Z", quad, 2 * a + 1, 0)]])
                        for h in range(4):
                            last = pe.transpose(out[:, h * P:(h + 1) * P], z[:, a % 2, 4 * b + h, :, :].rearrange("p j l -> p (j l)"), ident[:, :])
                    elif kind == "K":
                        if (a, b) == (0, 0):
                            pe.wait_ge(lo_done, lo_count[at[("C", quad, 1, 1)]])
                        for c in range(2):
                            for m, (u, v) in enumerate(PASSES):
                                last = pe.matmul(out, up_w[0][u][:, c, b * HEAD:(b + 1) * HEAD],
                                                 latent[v][:, c, 2 * a:2 * a + 2, :, :].rearrange("p b h m -> p (b h m)"),
                                                 start=(c == 0 and m == 0), stop=(c == 1 and m == 2))
                    else:
                        if (a, b) == (0, 0):
                            pe.wait_ge(lo_done, lo_count[at[("C", quad, 3, 1)]])
                        for c in range(2):
                            for m, (u, v) in enumerate(PASSES):
                                rows = latent[u][:, 2 + c, a // 2, 4 * (a % 2):4 * (a % 2) + 4, :].rearrange("p h m -> p (h m)")
                                last = pe.matmul(out, rows, up_w[1][v][:, c, b * HID:(b + 1) * HID],
                                                 start=(c == 0 and m == 0), stop=(c == 1 and m == 2))
                    last.then_inc(task_done, 1)

                interleaved(pe, routed.pe_body, task)

    return [(stored[k], 16 * (len(stage_order) // STAGES)) for k in range(STAGES)]


def attention(nc, sem, sb, ps, split, x, ident, h3, kv_w, stream, stored, wq_g, wo_g, k_scr, v_scr):
    HEADS = 2 * GROUP
    with ExitStack() as st:
        wq, wo, spare = attention_weights(kv_w)
        w_lo = stream.w_lo
        q_first = sb("q_first", [P, GROUP, 2, P], F32, st)
        q_second = [w[:, 0:2, :].rearrange("p a (h b n) -> p (a h) b n", h=2, b=2) for w in spare]
        k_raw = sb("k_raw", [P, 2, SEQ], F32, st)
        k = split("k", [P, 2, SEQ], st)
        v_raw = sb("v_raw", [P, 4, HEAD], F32, st)
        v = split("v", [P, 4, HEAD], st)
        prob = sb("prob", [P, 2, GROUP, 3 * P], F32, st)
        neg_max = sb("neg_max", [P, 2, GROUP, 2], F32, st)
        row_sum = sb("row_sum", [P, 2, GROUP, 2], F32, st)
        inv_sum = sb("inv_sum", [P, 2, GROUP, 2], F32, st)
        prob_t = split("prob_t", [P, 3, GROUP * P], st)
        o = [split("o0", [P, 2, GROUP, P], st), [w[:, 2:4, :].rearrange("p t (h n) -> p t h n", h=GROUP) for w in spare]]
        causal = sb("causal", [P, 2 * P], F32, st)
        ps_s = ps("ps_s", [P, GROUP, HID], st)
        ps_t = ps_s[:, 2:4, :]
        ps_q = ps("ps_q", [P, 2, HID], st)
        ps_o = ps("ps_o", [P, 2, HID], st)

        k_loaded, v_loaded = sem("k_loaded"), sem("v_loaded")
        mask_zero, mask_done = sem("mask_zero"), sem("mask_done")
        k_hi, k_lo, v_hi, v_lo = sem("k_hi"), sem("k_lo"), sem("v_hi"), sem("v_lo")
        s_done = sem("s_done")
        scored = sem("scored")
        exped, inv_done, normed = sem("exped"), sem("inv_done"), sem("normed")
        q_done, q_hi, q_read = sem("q_done"), sem("q_hi"), sem("q_read")
        t_done, t_hi, t_lo = sem("pt_done"), sem("pt_hi"), sem("pt_lo")
        pv_done, o_hi, o_lo = sem("pv_done"), sem("o_hi"), sem("o_lo")
        y_done, y_read = sem("y_done"), sem("y_read")

        UNITS = PAIRS * KV_HEADS
        LAST = KV_HEADS - 1

        def scratch_written(eng):
            for done, count in stored:
                eng.wait_ge(done, count)

        def groups(eng, group):
            group(0, True, False)
            with eng.Fori(1, LAST) as g:
                group(g, False, False)
            group(LAST, False, True)

        with nc.Block() as block:
            @block.sync
            def _(sp):
                def group(g, first, last):
                    for p in range(PAIRS):
                        u = PAIRS * g + p
                        if not (first and p == 0):
                            sp.wait_ge(s_done, HEADS * u)
                        sp.dma_start(k_raw[:, :, :].rearrange("p b n -> p (b n)"),
                                     k_scr[bass.ds(g, 1), :, p * PAIR:(p + 1) * PAIR].rearrange("g p n -> p (g n)")).then_inc(k_loaded, 16)
                        if not (first and p == 0):
                            sp.wait_ge(v_lo, u)
                        sp.dma_start(v_raw[:, :, :], v_scr[p, :, :, bass.ds(g * HEAD, HEAD)]).then_inc(v_loaded, 16)
                        if p == 0:
                            stream.load(sp, wo_g[bass.ds(g, 1), :, :, :].rearrange("a p h n -> p (a h) n"), 2 * g + 1)
                        if p == 1 and not last:
                            stream.load(sp, wq_g[bass.ds(g + 1, 1), :, :, :].rearrange("a p c n -> p (a c) n"), 2 * g + 2)

                scratch_written(sp)
                groups(sp, group)

            @block.gpsimd
            def _(pool):
                scratch_written(pool)
                pool.memset(causal[:, :], 0.0).then_inc(mask_zero, 1)
                pool.wait_ge(mask_zero, 1)
                pool.affine_select(out=causal[:, P:2 * P], in_=causal[:, P:2 * P], compare_op=ALU.is_ge, fill=MASKED, base=0,
                                   pattern=[[-1, P]], channel_multiplier=1).then_inc(mask_done, 1)

                def group(g, first, last):
                    for p in range(PAIRS):
                        u = PAIRS * g + p
                        for b in range(2):
                            for h in range(GROUP):
                                wait_alone(pool, inv_done, HEADS * u + GROUP * b + h + 1, mask_done)
                                pool.tensor_scalar(prob[:, b, h, 0:P], prob[:, b, h, 0:P], inv_sum[:, b, h, 0:1], 1.0, ALU.mult, ALU.mult)
                                pool.tensor_scalar(prob[:, b, h, P:3 * P], prob[:, b, h, P:3 * P], inv_sum[:, b, h, 1:2], 1.0,
                                                   ALU.mult, ALU.mult).then_inc(normed, 1)

                groups(pool, group)

            @block.scalar
            def _(act):
                def keys_hi(u):
                    act.wait_ge(k_loaded, 16 * u + 16)
                    hi_part(act, [w[:, :, :] for w in k], k_raw[:, :, :]).then_inc(k_hi, 1)

                def query_hi(h, count):
                    act.wait_ge(q_done, count)
                    by_tile = ps_q[:, h % 2, :].rearrange("p (b t n) -> p b t n", b=2, t=2)
                    act.activation(q_first[:, h, :, :], by_tile[:, :, 0, :], ACT.Copy)
                    hi_part(act, [w[:, h, :, :] for w in q_second], by_tile[:, :, 1, :]).then_inc(q_hi, 1)

                def group(g, first, last):
                    for p in range(PAIRS):
                        u = PAIRS * g + p
                        start = first and p == 0
                        more = not (last and p == PAIRS - 1)
                        def exponentials(b, h):
                            act.wait_ge(scored, HEADS * u + GROUP * b + h + 1)
                            act.activation(prob[:, b, h, 0:P], prob[:, b, h, 0:P], ACT.Exp, scale=-1.0,
                                           bias=neg_max[:, b, h, 0:1], accum_out=row_sum[:, b, h, 0:1])
                            act.activation(prob[:, b, h, P:3 * P], prob[:, b, h, P:3 * P], ACT.Exp, scale=-1.0,
                                           bias=neg_max[:, b, h, 1:2], accum_out=row_sum[:, b, h, 1:2]).then_inc(exped, 1)

                        def query(h):
                            if more:
                                query_hi(h, GROUP * (u + 1) + h + 1)
                            if p == 0:
                                if h == 0 and not first:
                                    act.wait_ge(y_done, 4 * u)
                                stream.hi(act, wo, h, 2 * g + 1)

                        def prob_hi(b, blk):
                            act.wait_ge(t_done, 6 * u + 3 * b + blk + 1)
                            if not (start and b == 0):
                                act.wait_ge(pv_done, 4 * u + 2 * b - 1 + (blk > 0))
                            hi_part(act, [w[:, blk, :] for w in prob_t], ps_t[:, (b + blk) % 2, :]).then_inc(t_hi, 1)

                        def out_hi(b, half):
                            act.wait_ge(pv_done, 4 * u + 2 * b + half + 1)
                            if not start:
                                act.wait_ge(y_done, 4 * (u - 1) + 2 * b + half + 1)
                            hi_part(act, [w[:, half, :, :].rearrange("p h n -> p (h n)") for w in o[b]], ps_o[:, half, :]).then_inc(o_hi, 1)

                        split_next = p == 2 and not last
                        for h in range(GROUP):
                            exponentials(0, h)
                        if not start:
                            act.wait_ge(pv_done, 4 * u)
                        act.wait_ge(v_loaded, 16 * u + 16)
                        hi_part(act, [w[:, :, :] for w in v], v_raw[:, :, :]).then_inc(v_hi, 1)
                        exponentials(1, 0)
                        exponentials(1, 1)
                        query(0)
                        exponentials(1, 2)
                        exponentials(1, 3)
                        query(1)
                        prob_hi(0, 0)
                        prob_hi(0, 1)
                        query(2)
                        prob_hi(0, 2)
                        query(3)
                        out_hi(0, 0)
                        out_hi(0, 1)
                        prob_hi(1, 0)
                        prob_hi(1, 1)
                        if split_next:
                            act.wait_ge(q_done, GROUP * (u + 2))
                            stream.hi(act, wq, 0, 2 * g + 2)
                            stream.hi(act, wq, 1, 2 * g + 2)
                        prob_hi(1, 2)
                        out_hi(1, 0)
                        if split_next:
                            stream.hi(act, wq, 2, 2 * g + 2)
                            stream.hi(act, wq, 3, 2 * g + 2)
                        out_hi(1, 1)
                        if more:
                            keys_hi(u + 1)

                scratch_written(act)
                for h in range(GROUP):
                    query_hi(h, h + 1)
                keys_hi(0)
                groups(act, group)

            @block.vector
            def _(dve):
                def keys_lo(u):
                    dve.wait_ge(k_hi, u + 1)
                    lo_part(dve, [w[:, :, :] for w in k], k_raw[:, :, :]).then_inc(k_lo, 1)

                def query_lo(h, count):
                    dve.wait_ge(q_hi, count)
                    by_tile = ps_q[:, h % 2, :].rearrange("p (b t n) -> p b t n", b=2, t=2)
                    lo_part(dve, [w[:, h, :, :] for w in q_second], by_tile[:, :, 1, :]).then_inc(q_read, 1)

                def add(u, p, b, half):
                    dve.wait_ge(y_done, 4 * u + 2 * b + half + 1)
                    t = 4 * p + 2 * b + half
                    dve.tensor_tensor(x[:, t, :], ps_q[:, half, :], x[:, t, :], ALU.add).then_inc(y_read, 1)

                def group(g, first, last):
                    for p in range(PAIRS):
                        u = PAIRS * g + p
                        start = first and p == 0
                        more = not (last and p == PAIRS - 1)

                        def score(b, h):
                            if not start and h == 0:
                                dve.wait_ge(t_done, 6 * (u - 1) + 3 * b + 3)
                            wait_alone(dve, s_done, HEADS * u + GROUP * b + h + 1, mask_done)
                            dve.tensor_tensor_reduce(out=prob[:, b, h, 0:P], in0=ps_s[:, h, 0:P], in1=causal[:, P:2 * P], scale=-SCALE,
                                                     scalar=3.0e38, op0=ALU.add, op1=ALU.min, accum_out=neg_max[:, b, h, 0:1])
                            dve.tensor_tensor_reduce(out=prob[:, b, h, P:3 * P], in0=ps_s[:, h, 2 * P:4 * P], in1=causal[:, :], scale=-SCALE,
                                                     scalar=3.0e38, op0=ALU.add, op1=ALU.min, accum_out=neg_max[:, b, h, 1:2]).then_inc(scored, 1)

                        def inverse(b, h):
                            dve.wait_ge(exped, HEADS * u + GROUP * b + h + 1)
                            dve.reciprocal(inv_sum[:, b, h, :], row_sum[:, b, h, :]).then_inc(inv_done, 1)

                        def query(h):
                            if more:
                                query_lo(h, GROUP * (u + 1) + h + 1)
                            if p == 0:
                                stream.lo(dve, wo, h, 2 * g + 1)

                        def prob_lo(b, blk):
                            dve.wait_ge(t_hi, 6 * u + 3 * b + blk + 1)
                            lo_part(dve, [w[:, blk, :] for w in prob_t], ps_t[:, (b + blk) % 2, :]).then_inc(t_lo, 1)

                        def out_lo(b, half):
                            dve.wait_ge(o_hi, 4 * u + 2 * b + half + 1)
                            lo_part(dve, [w[:, half, :, :].rearrange("p h n -> p (h n)") for w in o[b]], ps_o[:, half, :]).then_inc(o_lo, 1)

                        for h in range(GROUP):
                            score(0, h)
                        if not start:
                            add(u - 1, (p - 1) % PAIRS, 1, 1)
                        for h in range(GROUP):
                            inverse(0, h)
                        dve.wait_ge(v_hi, u + 1)
                        lo_part(dve, [w[:, :, :] for w in v], v_raw[:, :, :]).then_inc(v_lo, 1)
                        for h in range(GROUP):
                            score(1, h)
                        inverse(1, 0)
                        query(0)
                        for h in range(1, GROUP):
                            inverse(1, h)
                        split_next = p == 2 and not last
                        query(1)
                        prob_lo(0, 0)
                        prob_lo(0, 1)
                        query(2)
                        prob_lo(0, 2)
                        query(3)
                        out_lo(0, 0)
                        out_lo(0, 1)
                        prob_lo(1, 0)
                        prob_lo(1, 1)
                        if split_next:
                            stream.lo(dve, wq, 0, 2 * g + 2)
                            stream.lo(dve, wq, 1, 2 * g + 2)
                        add(u, p, 0, 0)
                        prob_lo(1, 2)
                        out_lo(1, 0)
                        if split_next:
                            stream.lo(dve, wq, 2, 2 * g + 2)
                            stream.lo(dve, wq, 3, 2 * g + 2)
                        add(u, p, 0, 1)
                        out_lo(1, 1)
                        if more:
                            keys_lo(u + 1)
                        add(u, p, 1, 0)

                scratch_written(dve)
                for h in range(GROUP):
                    query_lo(h, h + 1)
                keys_lo(0)
                groups(dve, group)
                add(UNITS - 1, PAIRS - 1, 1, 1)

            @block.tensor
            def _(pe):
                def project_query(h, pair):
                    for c in range(KC):
                        for n, (a, b) in enumerate(PASSES):
                            last = pe.matmul(ps_q[:, h % 2, :], wq[a][:, c, h * HEAD:(h + 1) * HEAD], h3[b][:, c, pair * PAIR:(pair + 1) * PAIR],
                                             start=(c == 0 and n == 0), stop=(c == KC - 1 and n == 2))
                    last.then_inc(q_done, 1)

                def group(g, first, last):
                    for p in range(PAIRS):
                        u = PAIRS * g + p
                        start = first and p == 0
                        more = not (last and p == PAIRS - 1)

                        def scores(b):
                            for h in range(GROUP):
                                n = HEADS * u + GROUP * b + h
                                if b:
                                    pe.wait_ge(scored, n - GROUP + 1)
                                elif not start:
                                    if h < 2:
                                        pe.wait_ge(scored, n - GROUP + 1)
                                    else:
                                        pe.wait_ge(t_lo, 6 * u)
                                pe.matmul(ps_s[:, h, 0:P], q_first[:, h, b, :], k_raw[:, b, 0:P], start=True, stop=True)
                                for m, (i, j) in enumerate(PASSES):
                                    done = pe.matmul(ps_s[:, h, 2 * P:4 * P], q_second[i][:, h, b, :], k[j][:, b, :], start=(m == 0), stop=(m == 2))
                                done.then_inc(s_done, 1)

                        def query(h):
                            if not more:
                                return
                            if h == 0 and p == PAIRS - 1:
                                pe.wait_ge(w_lo, 4 * (2 * g + 2) + 4)
                            if h < 2:
                                if not start:
                                    pe.wait_ge(y_read, 4 * u - 1 + h)
                            else:
                                pe.wait_ge(q_read, GROUP * (u + 1) + h - 1)
                            project_query(h, (p + 1) % PAIRS)

                        def flip(b, blk):
                            n = 6 * u + 3 * b + blk
                            if blk == 0:
                                pe.wait_ge(normed, HEADS * u + GROUP * (b + 1))
                            if b == 0 and blk < 2:
                                pe.wait_ge(scored, HEADS * u + GROUP + 3 + blk)
                            else:
                                pe.wait_ge(t_lo, n - 1)
                            for h in range(GROUP):
                                done = pe.transpose(ps_t[:, (b + blk) % 2, h * P:(h + 1) * P], prob[:, b, h, blk * P:(blk + 1) * P], ident[:, :])
                            done.then_inc(t_done, 1)

                        def values(b, half):
                            if b == 0 and half == 0:
                                pe.wait_ge(v_lo, u + 1)
                            if not (start and b == 0):
                                pe.wait_ge(o_lo, 4 * u + 2 * b - 1 + half)
                            blocks = (((0, 0),), ((1, 0), (2, 1)))[half]
                            for n, (blk, tile) in enumerate(blocks):
                                pe.wait_ge(t_lo, 6 * u + 3 * b + blk + 1)
                                for m, (i, j) in enumerate(PASSES):
                                    done = pe.matmul(ps_o[:, half, :], v[i][:, 2 * b + tile, :], prob_t[j][:, blk, :],
                                                     start=(n == 0 and m == 0), stop=(n == len(blocks) - 1 and m == 2))
                            done.then_inc(pv_done, 1)

                        def output(b, half):
                            if b == 0 and half == 0 and p == 0:
                                pe.wait_ge(w_lo, 4 * (2 * g + 1) + 4)
                            if b == 0:
                                if more:
                                    pe.wait_ge(q_read, GROUP * (u + 1) + 3 + half)
                                else:
                                    pe.wait_ge(y_read, 4 * u - 1 + half)
                            else:
                                pe.wait_ge(y_read, 4 * u + 1 + half)
                            pe.wait_ge(o_lo, 4 * u + 2 * b + half + 1)
                            for h in range(GROUP):
                                for m, (i, j) in enumerate(PASSES):
                                    done = pe.matmul(ps_q[:, half, :], o[b][i][:, half, h, :], wo[j][:, h, :],
                                                     start=(h == 0 and m == 0), stop=(h == GROUP - 1 and m == 2))
                            done.then_inc(y_done, 1)

                        pe.wait_ge(k_lo, u + 1)
                        pe.wait_ge(q_read, GROUP * (u + 1))
                        scores(0)
                        query(0)
                        scores(1)
                        query(1)
                        flip(0, 0)
                        flip(0, 1)
                        query(2)
                        flip(0, 2)
                        query(3)
                        values(0, 0)
                        values(0, 1)
                        flip(1, 0)
                        flip(1, 1)
                        output(0, 0)
                        flip(1, 2)
                        values(1, 0)
                        output(0, 1)
                        values(1, 1)
                        output(1, 0)
                        output(1, 1)

                pe.wait_ge(w_lo, 4)
                for h in range(GROUP):
                    if h >= 2:
                        pe.wait_ge(q_read, h - 1)
                    project_query(h, 0)
                groups(pe, group)


def feed_forward(nc, sem, sb, ps, split, x, ident, ln, gate_c, up_c, down_c, scales, out):
    with ExitStack() as st:
        gate = split("gate", [P, CHUNKS, KC, P], st)
        up = split("up", [P, CHUNKS, KC, P], st)
        down = split("down", [P, CHUNKS, HID], st)
        raw = [sb(f"f_raw{n}", [P, HID], F32, st) for n in range(3)]
        h = sb("h3n", [P, 4, HID], F32, st)
        ht = split("h3t", [P, KC, 4 * P], st)
        act_buf = sb("f_act", [P, 4 * P], F32, st)
        inner = [split(f"inner{n}", [P, 4 * P], st) for n in range(2)]
        scale = sb("f_scale", [P, 3], F32, st)
        ps_r = ps("f_ps_r", [P, 4, HID], st)
        ps_y = ps("f_ps_y", [P, 4, HID], st)

        raw_loaded = [sem(f"f_raw_loaded{n}") for n in range(3)]
        scale_loaded = sem("f_scale_loaded")
        w_hi, w_lo = sem("f_w_hi"), sem("f_w_lo")
        h_done, t_done, h_hi, h_lo = sem("f_h_done"), sem("f_t_done"), sem("f_h_hi"), sem("f_h_lo")
        gate_done, up_done, silu_done, prod_done = sem("f_gate_done"), sem("f_up_done"), sem("f_silu_done"), sem("f_prod_done")
        inner_hi, inner_lo = sem("f_inner_hi"), sem("f_inner_lo")
        down_used, y_done, x_done, stored = sem("f_down_used"), sem("f_y_done"), sem("f_x_done"), sem("f_stored")

        LAST = GROUPS - 1
        weights = (gate, up, down)
        FLIP = 2 * CHUNKS

        def groups(eng, group):
            group(0, True, False)
            with eng.Fori(1, LAST) as g:
                group(g, False, False)
            group(LAST, False, True)

        def piece(w, c):
            if w is down:
                return [part[:, c, :] for part in w]
            return [part[:, c, :, :].rearrange("p c n -> p (c n)") for part in w]

        with nc.Block() as block:
            @block.sync
            def _(sp):
                sp.dma_start(scale[:, :], scales.partition_broadcast(P)).then_inc(scale_loaded, 16)
                for c in range(CHUNKS):
                    for n, src in enumerate((gate_c, up_c, down_c)):
                        if c:
                            sp.wait_ge(w_lo, 3 * (c - 1) + n + 1)
                        sp.dma_start(raw[n][:, :], src[c, :, :]).then_inc(raw_loaded[n], 16)

                def group(g, first, last):
                    for tt in range(4):
                        t = 4 * g + tt
                        sp.wait_ge(x_done, t + 1)
                        sp.dma_start(out[bass.ds(t * P, P), :].rearrange("(a p) f -> p a f", a=1), x[:, bass.ds(t, 1), :]).then_inc(stored, 16)

                groups(sp, group)
                sp.wait_ge(stored, 16 * TILES)

            @block.gpsimd
            def _(pool):
                def group(g, first, last):
                    for tt in range(4):
                        ln.power(pool, 4 * g + tt)

                groups(pool, group)

            @block.scalar
            def _(act):
                def flipped(g):
                    for tt in range(4):
                        act.wait_ge(t_done, 4 * g + tt + 1)
                        ring = tt if known(g) and g == 0 else (FLIP + tt) % 4
                        hi_part(act, [w[:, :, tt * P:(tt + 1) * P] for w in ht], ps_r[:, ring, :].rearrange("p (c n) -> p c n", c=KC)).then_inc(h_hi, 1)

                def weight_hi(c):
                    for n, w in enumerate(weights):
                        act.wait_ge(raw_loaded[n], 16 * (c + 1))
                        hi_part(act, piece(w, c), raw[n][:, :]).then_inc(w_hi, 1)

                def group(g, first, last):
                    for c in range(CHUNKS):
                        at = CHUNKS * g + c
                        if first and c + 1 < CHUNKS:
                            weight_hi(c + 1)
                        act.wait_ge(gate_done, at + 1)
                        if not (first and c == 0):
                            act.wait_ge(inner_lo, at)
                        act.activation(act_buf[:, :], ps_r[:, 2 * c % 4, :], ACT.Silu, scale=scale[:, 0:1]).then_inc(silu_done, 1)
                        act.wait_ge(prod_done, at + 1)
                        if c >= 2:
                            act.wait_ge(down_used, (CHUNKS - 1) * g + c - 1)
                        elif not first:
                            act.wait_ge(y_done, 4 * g)
                        hi_part(act, [w[:, :] for w in inner[c % 2]], act_buf[:, :]).then_inc(inner_hi, 1)
                    if not last:
                        flipped(g + 1)

                act.wait_ge(scale_loaded, 16)
                weight_hi(0)
                flipped(0)
                groups(act, group)

            @block.vector
            def _(dve):
                def normalize(g, tt):
                    t = 4 * g + tt
                    par = tt % 2
                    tile = x[:, bass.ds(t, 1), :].rearrange("p a f -> p (a f)")
                    ln.stats(dve, tile, t, par)
                    ln.aggregate(dve, t, par)
                    ln.variance(dve, t, par)
                    if not known(g) or g >= 1:
                        dve.wait_ge(t_done, 4 * (g - 1) + tt + 1)
                    ln.apply(dve, h[:, tt, :], tile, t).then_inc(h_done, 1)

                def flipped(g):
                    for tt in range(4):
                        dve.wait_ge(h_hi, 4 * g + tt + 1)
                        ring = tt if known(g) and g == 0 else (FLIP + tt) % 4
                        lo_part(dve, [w[:, :, tt * P:(tt + 1) * P] for w in ht], ps_r[:, ring, :].rearrange("p (c n) -> p c n", c=KC)).then_inc(h_lo, 1)

                def weight_lo(c):
                    for n, w in enumerate(weights):
                        dve.wait_ge(w_hi, 3 * c + n + 1)
                        lo_part(dve, piece(w, c), raw[n][:, :]).then_inc(w_lo, 1)

                def group(g, first, last):
                    for c in range(CHUNKS):
                        at = CHUNKS * g + c
                        if first and c + 1 < CHUNKS:
                            weight_lo(c + 1)
                        if not last and 2 <= c < 6:
                            normalize(g + 1, c - 2)
                        dve.wait_ge(up_done, at + 1)
                        dve.wait_ge(silu_done, at + 1)
                        dve.scalar_tensor_tensor(act_buf[:, :], ps_r[:, (2 * c + 1) % 4, :], scale[:, 1:2], act_buf[:, :],
                                                 ALU.mult, ALU.mult).then_inc(prod_done, 1)
                        dve.wait_ge(inner_hi, at + 1)
                        lo_part(dve, [w[:, :] for w in inner[c % 2]], act_buf[:, :]).then_inc(inner_lo, 1)
                    if not last:
                        flipped(g + 1)
                    for tt in range(4):
                        t = 4 * g + tt
                        dve.wait_ge(y_done, t + 1)
                        tile = x[:, bass.ds(t, 1), :].rearrange("p a f -> p (a f)")
                        dve.scalar_tensor_tensor(tile, ps_y[:, tt, :], scale[:, 2:3], tile, ALU.mult, ALU.add).then_inc(x_done, 1)

                dve.wait_ge(scale_loaded, 16)
                for tt in range(4):
                    normalize(0, tt)
                weight_lo(0)
                flipped(0)
                groups(dve, group)

            @block.tensor
            def _(pe):
                def flip(g):
                    for tt in range(4):
                        pe.wait_ge(h_done, 4 * g + tt + 1)
                        ring = tt if known(g) and g == 0 else (FLIP + tt) % 4
                        if not known(g) or g >= 1:
                            pe.wait_ge((silu_done, prod_done)[tt % 2], CHUNKS * g - (1 if tt < 2 else 0))
                        for c in range(KC):
                            last = pe.transpose(ps_r[:, ring, c * P:(c + 1) * P], h[:, tt, c * P:(c + 1) * P], ident[:, :])
                        last.then_inc(t_done, 1)

                def project(w, c, bank, done):
                    for k in range(KC):
                        for n, (a, b) in enumerate(PASSES):
                            last = pe.matmul(ps_r[:, bank, :], w[a][:, c, k, :], ht[b][:, k, :], start=(k == 0 and n == 0), stop=(k == KC - 1 and n == 2))
                    last.then_inc(done, 1)

                def multiply_down(g, c, first):
                    pe.wait_ge(inner_lo, CHUNKS * g + c + 1)
                    if first:
                        pe.wait_ge(w_lo, 3 * c + 3)
                    for tt in range(4):
                        if c == 0 and not first:
                            pe.wait_ge(x_done, 4 * (g - 1) + tt + 1)
                        for n, (a, b) in enumerate(PASSES):
                            last = pe.matmul(ps_y[:, tt, :], inner[c % 2][a][:, tt * P:(tt + 1) * P], down[b][:, c, :],
                                             start=(c == 0 and n == 0), stop=(c == CHUNKS - 1 and n == 2))
                        if c == CHUNKS - 1:
                            last.then_inc(y_done, 1)
                    if c < CHUNKS - 1:
                        last.then_inc(down_used, 1)

                def group(g, first, last):
                    for c in range(CHUNKS):
                        if c == 0:
                            pe.wait_ge(h_lo, 4 * g + 4)
                        for n, (w, read, done) in enumerate(((gate, silu_done, gate_done), (up, prod_done, up_done))):
                            if first:
                                pe.wait_ge(w_lo, 3 * c + n + 1)
                            if c >= 2:
                                pe.wait_ge(read, CHUNKS * g + c - 1)
                            project(w, c, (2 * c + n) % 4, done)
                        if c >= 1:
                            multiply_down(g, c - 1, first)
                    if not last:
                        flip(g + 1)
                    multiply_down(g, CHUNKS - 1, first)

                flip(0)
                groups(pe, group)


def lay_out(inputs):
    import numpy as np

    def a(name):
        return np.asarray(inputs[name])

    def rows(w, n):
        return np.ascontiguousarray(w.T.reshape(-1, P, n, w.shape[0] // n).transpose(2, 1, 0, 3))

    def padded(w):
        return np.concatenate([w, np.zeros((CHUNKS * P - INTER, w.shape[1]), w.dtype)], axis=0)

    def kv_weights():
        down = np.concatenate([a("L1_attn_Wk_down").T, a("L1_attn_Wv_down").T], axis=1)
        by_row = [w.reshape(-1, P, w.shape[1]).transpose(1, 0, 2).reshape(P, -1) for w in (down, a("L1_attn_Wk_up").T, a("L1_attn_Wv_up").T)]
        return np.concatenate(by_row, axis=1).reshape(P, TILES, KV_PIECE).transpose(1, 0, 2)

    arrays = {
        "in_x": a("L0_attn_data").reshape(TOKENS, HID),
        "in_mask_t": a("L0_attn_mask").T,
        "in_w0_t": a("L0_attn_weight").T,
        "in_bias0": a("L0_attn_bias"),
        "in_router_t": a("L0_ffn_router_weight").T,
        "in_router_bias": a("L0_ffn_router_bias"),
        "in_expert_bias": a("L0_ffn_expert_bias"),
        "in_kv_weights": kv_weights(),
        "in_wq_g": rows(a("L1_attn_Wq"), KV_HEADS),
        "in_wo_g": a("L1_attn_Wo").T.reshape(KV_HEADS, GROUP, HEAD, HID).transpose(0, 2, 1, 3),
        "in_gate_c": rows(padded(a("L1_ffn_gate_w")), CHUNKS).reshape(CHUNKS, P, HID),
        "in_up_c": rows(padded(a("L1_ffn_up_w")), CHUNKS).reshape(CHUNKS, P, HID),
        "in_down_c": padded(a("L1_ffn_down_w").T).reshape(CHUNKS, P, HID),
        "in_scales": np.stack([a("L1_ffn_gate_scale"), a("L1_ffn_up_scale"), a("L1_ffn_down_scale")]),
    }
    return {name: np.ascontiguousarray(v) for name, v in arrays.items()}


def kernel(**inputs):
    import concourse.bacc as bacc
    from concourse.bass_utils import run_bass_kernel_spmd

    nc = bacc.Bacc("TRN2", target_bir_lowering=False, num_devices=1)
    arrays = lay_out(inputs)
    args = [nc.dram_tensor(name, a.shape, mybir.dt.from_np(a.dtype), kind="ExternalInput").ap() for name, a in arrays.items()]
    out = nc.dram_tensor("out", (TOKENS, HID), F32, kind="ExternalOutput").ap()
    build(nc, *args, out)
    result = run_bass_kernel_spmd(nc, [arrays], core_ids=[0])
    return result.results[0]["out"].reshape(BATCH, SEQ, HID)
```

```python
from contextlib import ExitStack

import concourse.bass as bass
from concourse import mybir

F32 = mybir.dt.float32
F32R = mybir.dt.float32r
I32 = mybir.dt.int32
ALU = mybir.AluOpType
ACT = mybir.ActivationFunctionType
AX_X = mybir.AxisListType.X

P = 128
HID = 512
KC = HID // P
BATCH, SEQ = 8, 256
TOKENS = BATCH * SEQ
TILES = TOKENS // P
EXPERTS = 64
BLOCK = 32
EPS = 1e-5

KV_HEADS = 8
GROUP = 4
HEAD = 128
LATENT = 32
PAIRS = BATCH // 2
PAIR = 2 * SEQ
KV_DOWN, KV_UP = KC * 2 * KV_HEADS * LATENT, 2 * KV_HEADS * HEAD
KV_PIECE = (KV_DOWN + 2 * KV_UP) // TILES
SCALE = float(HEAD) ** -0.5
MASKED = -1.0e30

INTER = 1376
CHUNKS = -(-INTER // P)
GROUPS = TILES // 4

HI, LO = 0, 1
PASSES = ((HI, HI), (LO, HI), (HI, LO))


def known(t):
    return isinstance(t, int)


def skewed(eng, depth, body, first=None, tail=None):
    if first is None:
        first = depth + depth % 2 + 2
    for i in range(first):
        body(i, i % 2, lambda k, i=i: i - k >= 0)
    with eng.Fori(first // 2, TILES // 2) as j:
        for par in range(2):
            body(2 * j + par, par, lambda k: True)
    for i in range(TILES, TILES + depth):
        body(i, i % 2, lambda k, i=i: i - k < TILES)
        if tail:
            tail(i - TILES)


class LayerNorm:

    def __init__(self, sb, sem, name, half, ready):
        self.bn = sb(f"bn_{name}", [P, 2, 6])
        self.mv = sb(f"mv_{name}", [P, 2, 2])
        self.neg_mean = sb(f"neg_mean_{name}", [P, TILES])
        self.ve = sb(f"ve_{name}", [P, TILES])
        self.factors = sb(f"factors_{name}", [P, TILES, 2])
        self.half = half
        self.ready = ready
        self.bn_done = sem(f"bn_done_{name}")
        self.mv_done = sem(f"mv_done_{name}")
        self.ve_done = sem(f"ve_done_{name}")
        self.rstd_done = sem(f"rstd_done_{name}")
        self.shift_done = sem(f"shift_done_{name}")

    def stats(self, dve, src, par):
        dve.bn_stats(self.bn[:, par, :], src).then_inc(self.bn_done, 1)

    def aggregate(self, dve, t, par):
        wait_alone(dve, self.bn_done, t + 1, self.ready)
        dve.bn_aggr(self.mv[:, par, :], self.bn[:, par, :]).then_inc(self.mv_done, 1)

    def variance(self, dve, t, par):
        dve.wait_ge(self.mv_done, t + 1)
        dve.tensor_scalar(self.neg_mean[:, bass.ds(t, 1)], self.mv[:, par, 0:1], -1.0, None, ALU.mult)
        dve.tensor_scalar(self.ve[:, bass.ds(t, 1)], self.mv[:, par, 1:2], EPS, None, ALU.add).then_inc(self.ve_done, 1)

    def power(self, pool, t):
        pool.wait_ge(self.ve_done, t + 1)
        pool.tensor_tensor(self.factor(t, 0), self.ve[:, bass.ds(t, 1)], self.half, ALU.pow).then_inc(self.rstd_done, 1)
        pool.wait_ge(self.rstd_done, t + 1)
        pool.tensor_tensor(self.factor(t, 1), self.neg_mean[:, bass.ds(t, 1)], self.factor(t, 0), ALU.mult).then_inc(self.shift_done, 1)

    def factor(self, t, n):
        return self.factors[:, bass.ds(t, 1), n:n + 1].rearrange("p t n -> p (t n)")

    def apply(self, dve, out, src, t):
        dve.wait_ge(self.shift_done, t + 1)
        return dve.tensor_scalar(out, src, self.factor(t, 0), self.factor(t, 1), ALU.mult, ALU.add)

    def activate(self, act, out, src, t):
        act.wait_ge(self.shift_done, t + 1)
        return act.activation(out, src, ACT.Identity, bias=self.factor(t, 1), scale=self.factor(t, 0))


def wait_alone(eng, done, value, ready):
    if not known(value):
        eng.lower_val(value)
    eng.wait_ge(ready, 1)
    eng.wait_ge(done, value)


def tile_of(x, t):
    return x[:, bass.ds(t, 1), :].rearrange("p a f -> p (a f)")


def hi_part(act, parts, src):
    return act.activation(parts[HI], src, ACT.Copy)


def lo_part(dve, parts, src):
    return dve.tensor_tensor(parts[LO], src, parts[HI].bitcast(F32), ALU.subtract)


def build(nc, x_in, mask_t, w0_t, bias0, router_t, router_bias, expert_bias, kv_weights,
          wq_g, wo_g, gate_c, up_c, down_c, scales, out):
    whole = ExitStack()

    def sem(name):
        return whole.enter_context(nc.semaphore(name))

    def sb(name, shape, dt=F32, stack=whole):
        return stack.enter_context(nc.sbuf_tensor(name, shape, dt))

    def ps(name, shape, stack):
        return stack.enter_context(nc.psum_tensor(name, shape, F32))

    def split(name, shape, stack=whole):
        return [sb(name + "_hi", shape, F32R, stack), sb(name + "_lo", shape, F32R, stack)]

    k_scr = nc.dram_tensor("k_scratch", [KV_HEADS, P, TOKENS], F32, kind="Internal").ap()
    v_scr = nc.dram_tensor("v_scratch", [PAIRS, P, 4, KV_HEADS * HEAD], F32, kind="Internal").ap()

    with whole:
        x = sb("x", [P, TILES, HID])
        ident = sb("ident", [P, P])
        half = sb("half", [P, 1])
        consts = sem("consts")
        ln = [LayerNorm(sb, sem, f"ln{n}", half[:, 0:1], consts) for n in range(4)]

        h3 = split("h3", [P, KC, TOKENS])
        feed = FeedStart(sem, x, ident, h3, ln[3], gate_c)
        with ExitStack() as held:
            kv_w = split("kv_w", [P, TILES, KV_PIECE], held)
            stream = WeightStream(sem, sb, held)
            with ExitStack() as held_router:
                router = RouterWeights(sb, sem, held_router)
                block_sparse_linear(nc, sem, sb, ps, split, x, ident, half, consts, ln[0], ln[1], x_in, mask_t, w0_t, bias0,
                                    lambda eng: router.load(eng, router_t, router_bias, expert_bias), kv_weights, kv_w)
                stored = routed_bias_and_keys(nc, sem, sb, ps, split, x, ident, ln[1], ln[2], router, h3, kv_w, stream, wq_g, k_scr, v_scr)
            attention(nc, sem, sb, ps, split, x, ident, h3, kv_w, stream, stored, feed, wq_g, wo_g, k_scr, v_scr)
        feed_forward(nc, sem, sb, ps, split, x, ident, ln[3], feed, gate_c, up_c, down_c, scales, out)


def block_sparse_linear(nc, sem, sb, ps, split, x, ident, half, consts, ln, ln_next, x_in, mask_t, w0_t, bias0, load_next, kv_weights, kv_w):
    with ExitStack() as st:
        mask = sb("mask", [P, KC, HID], I32, st)
        w_raw = sb("w0_raw", [P, KC, HID], F32, st)
        w0 = split("w0", [P, KC, HID], st)
        bias = sb("bias0", [P, HID], F32, st)
        same_block = sb("same_block", [P, P], F32, st)
        row_sums = sb("row_sums", [P, KC * HID // BLOCK], F32, st)
        block_on = sb("block_on", [P, KC * HID // BLOCK], F32, st)
        h = sb("h0", [P, 2, HID], F32, st)
        ht = [split(f"h0t{n}", [P, KC, P], st) for n in range(2)]
        kv_raw = sb("kv_raw", [P, 2, KV_PIECE], F32, st)
        ps_t = ps("a_ps_t", [P, 2, HID], st)
        ps_y = ps("a_ps_y", [P, 2, HID], st)
        ps_b = ps("a_ps_b", [P, HID], st)

        x_loaded = [sem(f"a_x_loaded{n}") for n in range(2)]
        mask_loaded = [sem(f"a_mask_loaded{c}") for c in range(KC)]
        w_loaded = [sem(f"a_w_loaded{c}") for c in range(KC)]
        bias_loaded = sem("a_bias_loaded")
        block_zeroed = sem("a_block_zeroed")
        zeroed, const_done = sem("a_zeroed"), sem("a_const_done")
        rows_done, blocks_done, on_done, masked = sem("a_rows_done"), sem("a_blocks_done"), sem("a_on_done"), sem("a_masked")
        w_hi_done, w_lo_done = sem("a_w_hi_done"), sem("a_w_lo_done")
        h_done, t_done, hi_done, lo_done = sem("a_h_done"), sem("a_t_done"), sem("a_hi_done"), sem("a_lo_done")
        y_done, xb_done, x_done = sem("a_y_done"), sem("a_xb_done"), sem("a_x_done")
        kv_loaded = [sem(f"a_kv_loaded{n}") for n in range(2)]
        kv_hi, kv_lo = sem("a_kv_hi"), sem("a_kv_lo")

        with nc.Block() as block:
            @block.sync
            def _(sp):
                def load(t, par):
                    if not known(t) or t >= 2:
                        sp.wait_ge(x_loaded[par], 8 * (t - par))
                    sp.dma_start(x[:, bass.ds(t, 1), :], x_in[bass.ds(t * P, P), :].rearrange("(a p) f -> p a f", a=1)).then_inc(x_loaded[par], 16)

                def load_kv(t, par):
                    if not known(t) or t >= 2:
                        sp.wait_ge(kv_lo, t - 1)
                    sp.dma_start(kv_raw[:, bass.ds(par, 1), :], kv_weights[bass.ds(t, 1), :, :].rearrange("a p n -> p a n")).then_inc(kv_loaded[par], 16)

                def body(i, par, live):
                    if live(0):
                        load(i, par)
                        if known(i) and i == 1:
                            for src, dst, loaded in ((mask_t, mask, mask_loaded), (w0_t, w_raw, w_loaded)):
                                for c in range(KC):
                                    sp.dma_start(dst[:, c, :], src[c * P:(c + 1) * P, :]).then_inc(loaded[c], 16)
                    if live(4):
                        load_kv(i - 4, par)

                skewed(sp, 4, body)

            @block.scalar
            def _(act):
                act.dma_start(bias[:, :], bias0.partition_broadcast(P)).then_inc(bias_loaded, 16)
                load_next(act)
                def body(i, par, live):
                    if known(i) and i == 2:
                        for c in range(KC):
                            act.wait_ge(masked, c + 1)
                            hi_part(act, [w[:, c, :] for w in w0], w_raw[:, c, :]).then_inc(w_hi_done, 1)
                    if live(2):
                        t, pt = i - 2, par
                        act.wait_ge(t_done, t + 1)
                        if not known(t) or t >= 2:
                            act.wait_ge(y_done, t - 1)
                        hi_part(act, [p[:, :, :] for p in ht[pt]], ps_t[:, pt, :].rearrange("p (c n) -> p c n", c=KC)).then_inc(hi_done, 1)
                    if live(1):
                        t, pt = i - 1, (par - 1) % 2
                        if not known(t) or t >= 2:
                            act.wait_ge(t_done, t - 1)
                        ln.activate(act, h[:, pt, :], tile_of(x, t), t).then_inc(h_done, 1)
                    if live(3):
                        t, pt = i - 3, (par - 3) % 2
                        act.wait_ge(kv_loaded[pt], 8 * (t - pt) + 16)
                        hi_part(act, [tile_of(w, t) for w in kv_w], kv_raw[:, pt, :]).then_inc(kv_hi, 1)

                skewed(act, 3, body)

            @block.gpsimd
            def _(pool):
                pool.memset(half[:, :], -0.5).then_inc(zeroed, 1)
                pool.memset(ident[:, :], 0.0).then_inc(zeroed, 1)
                pool.wait_ge(zeroed, 2)
                pool.affine_select(out=ident[:, :], in_=ident[:, :], compare_op=ALU.not_equal, fill=1.0, base=0,
                                   pattern=[[-1, P]], channel_multiplier=1).then_inc(consts, 1)
                pool.wait_ge(consts, 1)
                pool.wait_ge(bias_loaded, 16)

                def body(i, par, live):
                    if live(2):
                        t = i - 2
                        pool.wait_ge(h_done, t + 1)
                        pool.tensor_tensor(tile_of(x, t), tile_of(x, t), bias[:, :], ALU.add).then_inc(xb_done, 1)
                    if live(5):
                        ln_next.power(pool, i - 5)
                    if live(0):
                        ln.power(pool, i)

                skewed(pool, 5, body)

            @block.vector
            def _(dve):
                dve.memset(same_block[:, :], 0.0).then_inc(block_zeroed, 1)
                dve.wait_ge(block_zeroed, 1)
                for q in range(0, P, BLOCK):
                    last = dve.memset(same_block[q:q + BLOCK, q:q + BLOCK], 1.0)
                last.then_inc(const_done, 1)
                def weight():
                    per_chunk = HID // BLOCK
                    for c in range(KC):
                        dve.wait_ge(mask_loaded[c], 16)
                        dve.tensor_reduce(row_sums[:, c * per_chunk:(c + 1) * per_chunk], mask[:, c, :].rearrange("p (n b) -> p n b", b=BLOCK),
                                          AX_X, ALU.add).then_inc(rows_done, 1)
                    dve.wait_ge(blocks_done, 1)
                    dve.tensor_scalar(block_on[:, :], ps_b[:, 0:KC * per_chunk], 0.0, None, ALU.is_gt).then_inc(on_done, 1)
                    dve.wait_ge(on_done, 1)

                    def lo(c):
                        dve.wait_ge(w_hi_done, c + 1)
                        lo_part(dve, [w[:, c, :] for w in w0], w_raw[:, c, :]).then_inc(w_lo_done, 1)

                    for c in range(KC):
                        dve.wait_ge(w_loaded[c], 16)
                        blocks = w_raw[:, c, :].rearrange("p (n b) -> p n b", b=BLOCK)
                        on = block_on[:, c * per_chunk:(c + 1) * per_chunk].unsqueeze(2).to_broadcast([P, per_chunk, BLOCK])
                        dve.tensor_tensor(blocks, blocks, on, ALU.mult).then_inc(masked, 1)
                        if c >= 1:
                            lo(c - 1)
                    lo(KC - 1)

                def body(i, par, live):
                    if known(i) and i == 2:
                        weight()
                    if live(4):
                        t, pt = i - 4, par
                        dve.wait_ge(y_done, t + 1)
                        dve.wait_ge(xb_done, t + 1)
                        dve.tensor_tensor(tile_of(x, t), ps_y[:, pt, :], tile_of(x, t), ALU.add).then_inc(x_done, 1)
                    if live(5):
                        wait_alone(dve, x_done, i - 5 + 1, ln.ready)
                        ln_next.stats(dve, x[:, bass.ds(i - 5, 1), :], (par - 5) % 2)
                    if live(0):
                        dve.wait_ge(x_loaded[par], 8 * (i - par) + 16)
                        ln.stats(dve, x[:, bass.ds(i, 1), :], par)
                    if live(5):
                        ln_next.aggregate(dve, i - 5, (par - 5) % 2)
                    if live(2):
                        t, pt = i - 2, par
                        dve.wait_ge(hi_done, t + 1)
                        lo_part(dve, [p[:, :, :] for p in ht[pt]], ps_t[:, pt, :].rearrange("p (c n) -> p c n", c=KC)).then_inc(lo_done, 1)
                    if live(5):
                        ln_next.variance(dve, i - 5, (par - 5) % 2)
                    if live(0):
                        ln.aggregate(dve, i, par)
                    if live(4):
                        dve.wait_ge(kv_hi, i - 4 + 1)
                        lo_part(dve, [tile_of(w, i - 4) for w in kv_w], kv_raw[:, par, :]).then_inc(kv_lo, 1)
                    if live(0):
                        ln.variance(dve, i, par)

                skewed(dve, 5, body)

            @block.tensor
            def _(pe):
                pe.wait_ge(rows_done, KC)
                pe.wait_ge(const_done, 1)
                pe.matmul(ps_b[:, 0:KC * HID // BLOCK], same_block[:, :], row_sums[:, :], start=True, stop=True).then_inc(blocks_done, 1)
                pe.wait_ge(consts, 1)

                def body(i, par, live):
                    if live(2):
                        t, pt = i - 2, par
                        pe.wait_ge(h_done, t + 1)
                        if not known(t) or t >= 2:
                            pe.wait_ge(lo_done, t - 1)
                        for c in range(KC):
                            last = pe.transpose(ps_t[:, pt, c * P:(c + 1) * P], h[:, pt, c * P:(c + 1) * P], ident[:, :])
                        last.then_inc(t_done, 1)
                    if live(3):
                        t, pt = i - 3, (par - 3) % 2
                        pe.wait_ge(lo_done, t + 1)
                        if not known(t) or t >= 2:
                            pe.wait_ge(x_done, t - 1)
                        for c in range(KC):
                            if known(t) and t == 0:
                                pe.wait_ge(w_lo_done, c + 1)
                            for n, (a, b) in enumerate(PASSES):
                                last = pe.matmul(ps_y[:, pt, :], ht[pt][a][:, c, :], w0[b][:, c, :],
                                                 start=(c == 0 and n == 0), stop=(c == KC - 1 and n == 2))
                        last.then_inc(y_done, 1)

                skewed(pe, 3, body)


class FeedStart:

    def __init__(self, sem, x, ident, h3, ln, gate_c):
        self.x, self.ident, self.ln, self.gate_c = x, ident, ln, gate_c
        self.ht = [w[:, 0, :].rearrange("p (c n) -> p c n", c=KC) for w in h3]
        rest = [w[:, 1:KC, :].rearrange("p a n -> p (a n)") for w in h3]
        size = CHUNKS * KC * P
        self.gate = [w[:, 0:size].rearrange("p (c k n) -> p c k n", c=CHUNKS, k=KC) for w in rest]
        self.spare = [w[:, size:size + 4 * P] for w in rest]
        self.h_done, self.t_done, self.h_hi, self.h_lo = sem("f_h_done"), sem("f_t_done"), sem("f_h_hi"), sem("f_h_lo")
        self.raw_loaded = [sem(f"f_raw_loaded{n}") for n in range(3)]
        self.w_hi, self.w_lo = sem("f_w_hi"), sem("f_w_lo")

    def statistics(self, dve, t):
        self.ln.stats(dve, self.x[:, t, :], t % 2)
        self.ln.aggregate(dve, t, t % 2)
        self.ln.variance(dve, t, t % 2)

    def flip(self, pe, h, bank, t):
        pe.wait_ge(self.h_done, t + 1)
        for c in range(KC):
            last = pe.transpose(bank[:, c * P:(c + 1) * P], h[:, t, c * P:(c + 1) * P], self.ident[:, :])
        last.then_inc(self.t_done, 1)

    def part(self, eng, bank, t, part):
        eng.wait_ge((self.t_done, self.h_hi)[part], t + 1)
        split_part = (hi_part, lo_part)[part]
        split_part(eng, [w[:, :, t * P:(t + 1) * P] for w in self.ht], bank.rearrange("p (c n) -> p c n", c=KC)).then_inc((self.h_hi, self.h_lo)[part], 1)

    def load_gate(self, sp, raw):
        sp.dma_start(raw, self.gate_c[0, :, :]).then_inc(self.raw_loaded[0], 16)

    def gate_part(self, eng, raw, part):
        eng.wait_ge((self.raw_loaded[0], self.w_hi)[part], (16, 1)[part])
        (hi_part, lo_part)[part](eng, [w[:, 0, :, :].rearrange("p k n -> p (k n)") for w in self.gate], raw).then_inc((self.w_hi, self.w_lo)[part], 1)


class WeightStream:

    def __init__(self, sem, sb, stack):
        self.raw = sb("w_raw", [P, 4, HID], F32, stack)
        self.raw_loaded, self.w_hi, self.w_lo = sem("raw_loaded"), sem("w_hi"), sem("w_lo")

    def load(self, sp, src, sets):
        if not known(sets) or sets >= 1:
            sp.wait_ge(self.w_lo, 4 * sets)
        sp.dma_start(self.raw[:, :, :], src).then_inc(self.raw_loaded, 16)

    def hi(self, act, w, n, sets):
        if n == 0:
            act.wait_ge(self.raw_loaded, 16 * sets + 16)
        hi_part(act, [part[:, n, :] for part in w], self.raw[:, n, :]).then_inc(self.w_hi, 1)

    def lo(self, dve, w, n, sets):
        dve.wait_ge(self.w_hi, 4 * sets + n + 1)
        lo_part(dve, [part[:, n, :] for part in w], self.raw[:, n, :]).then_inc(self.w_lo, 1)


def attention_weights(kv_w):
    whole = [w[:, :, :].rearrange("p a n -> p (a n)") for w in kv_w]
    size = KC * GROUP * HEAD
    return [[w[:, n * size:(n + 1) * size].rearrange("p (c n) -> p c n", n=HID) for w in whole] for n in range(3)]


class RouterWeights:

    def __init__(self, sb, sem, stack):
        self.router = sb("router", [P, KC, EXPERTS], F32, stack)
        self.logit_bias = sb("r_bias", [P, EXPERTS], F32, stack)
        self.expert_bias = sb("e_bias", [P, HID], F32, stack)
        self.loaded = sem("b_loaded")

    def load(self, eng, router_t, router_bias, expert_bias):
        eng.dma_start(self.router[:, :, :], router_t.rearrange("(c p) n -> p c n", p=P)).then_inc(self.loaded, 16)
        eng.dma_start(self.logit_bias[:, :], router_bias.partition_broadcast(P)).then_inc(self.loaded, 16)
        eng.dma_start(self.expert_bias[0:EXPERTS, :], expert_bias).then_inc(self.loaded, 16)


class RoutedBias:

    DEPTH = 9

    def __init__(self, sem, sb, bank, x, ident, ln, ln_next, weights, h3, st):
        self.x, self.ident, self.ln, self.ln_next, self.weights, self.h3 = x, ident, ln, ln_next, weights, h3
        self.h = sb("h1", [P, 2, HID], F32, st)
        self.ht = sb("h1t", [P, 2, HID], F32, st)
        self.h_next = sb("h2", [P, 2, HID], F32, st)
        self.logits = sb("logits", [P, 2, EXPERTS], F32, st)
        self.neg_max = sb("r_neg_max", [P, 2], F32, st)
        self.e = sb("r_exp", [P, 2, EXPERTS], F32, st)
        self.total = sb("r_total", [P, 2], F32, st)
        self.top = sb("r_top", [P, 2, 8], F32, st)
        self.rest = sb("r_rest", [P, 2, EXPERTS], F32, st)
        self.top_sum = sb("r_top_sum", [P, 2], F32, st)
        self.inv_total = sb("r_inv_total", [P, TILES], F32, st)
        self.weight_sum = sb("r_weight_sum", [P, 2], F32, st)
        self.one_zero = sb("r_one_zero", [P, 2], F32, st)
        self.combined = sb("r_combined", [P, 2, 2], F32, st)
        self.chosen = sb("r_chosen", [P, 2, P], F32, st)
        self.chosen_t = sb("r_chosen_t", [P, 2, P], F32, st)
        self.ps_t, self.ps_l, self.ps_m, self.ps_n = [bank[:, n, :] for n in range(4)]
        self.ps_c = self.ps_t
        self.zeroed = sem("b_zeroed")
        self.h_done = sem("b_h_done")
        self.t_done = sem("b_t_done")
        self.ht_done = sem("b_ht_done")
        self.l_done = sem("b_l_done")
        self.lb_done = sem("b_lb_done")
        self.max_done = sem("b_max_done")
        self.exp_done = sem("b_exp_done")
        self.top_done = sem("b_top_done")
        self.rest_done = sem("b_rest_done")
        self.inv_done = sem("b_inv_done")
        self.chosen_done = sem("b_chosen_done")
        self.sum_done = sem("b_sum_done")
        self.combined_done = sem("b_combined_done")
        self.scaled_done = sem("b_scaled_done")
        self.ct_done = sem("b_ct_done")
        self.ctc_done = sem("b_ctc_done")
        self.mix_done = sem("b_mix_done")
        self.x_done = sem("b_x_done")
        self.h_next_done = sem("b_h_next_done")
        self.tn_done = sem("b_tn_done")
        self.hi_done = sem("b_hi_done")
        self.lo_done = sem("b_lo_done")

    def transposed(self):
        return self.ps_n.rearrange("p (c n) -> p c n", c=KC)

    def set_constants(self, pool):
        for n, (part, value) in enumerate(((self.one_zero[:, 0:1], 1.0), (self.one_zero[:, 1:2], 0.0),
                                           (self.weights.expert_bias[EXPERTS:P, :], 0.0), (self.chosen[:, :, EXPERTS:P], 0.0))):
            if n:
                pool.wait_ge(self.zeroed, n)
            pool.memset(part, value).then_inc(self.zeroed, 1)

    def await_constants(self, eng):
        eng.wait_ge(self.zeroed, 4)
        eng.wait_ge(self.weights.loaded, 48)

    def pool_body(self, pool, i, par, live):
        if live(6):
            self.ln_next.power(pool, i - 6)

    def act_body(self, act, i, par, live):
        odd = (par - 1) % 2
        if live(3):
            t, pt = i - 3, odd
            act.wait_ge(self.max_done, t + 1)
            if not known(t) or t >= 2:
                act.wait_ge(self.chosen_done, t - 1)
            act.activation(self.e[:, pt, :], self.logits[:, pt, :], ACT.Exp, bias=self.neg_max[:, pt:pt + 1],
                           accum_out=self.total[:, pt:pt + 1]).then_inc(self.exp_done, 1)
        if live(4):
            t, pt = i - 4, par
            act.wait_ge(self.combined_done, t + 1)
            act.activation(tile_of(self.x, t), tile_of(self.x, t), ACT.Identity, bias=self.combined[:, pt, 1:2],
                           scale=self.combined[:, pt, 0:1]).then_inc(self.scaled_done, 1)
            act.wait_ge(self.ct_done, t + 1)
            if not known(t) or t >= 2:
                act.wait_ge(self.mix_done, t - 1)
            act.activation(self.chosen_t[:, pt, :], self.ps_c[:, 0:P], ACT.Copy).then_inc(self.ctc_done, 1)
        if live(9):
            t = i - 9
            act.wait_ge(self.tn_done, t + 1)
            hi_part(act, [p[:, :, bass.ds(t * P, P)] for p in self.h3], self.transposed()).then_inc(self.hi_done, 1)
        if live(7):
            t, pt = i - 7, odd
            if not known(t) or t >= 2:
                act.wait_ge(self.tn_done, t - 1)
            self.ln_next.activate(act, self.h_next[:, pt, :], tile_of(self.x, t), t).then_inc(self.h_next_done, 1)
        if live(0):
            t, pt = i, par
            if not known(t) or t >= 2:
                act.wait_ge(self.t_done, t - 1)
            self.ln.activate(act, self.h[:, pt, :], tile_of(self.x, t), t).then_inc(self.h_done, 1)
        if live(1):
            t, pt = i - 1, odd
            act.wait_ge(self.t_done, t + 1)
            if not known(t) or t >= 2:
                act.wait_ge(self.l_done, t - 1)
            act.activation(self.ht[:, pt, :], self.ps_t, ACT.Copy).then_inc(self.ht_done, 1)

    def dve_body(self, dve, i, par, live):
        odd = (par - 1) % 2
        t2, t3, t5, t6 = i - 2, i - 3, i - 5, i - 6
        if live(6):
            wait_alone(dve, self.x_done, t6 + 1, self.ln.ready)
            self.ln_next.stats(dve, self.x[:, bass.ds(t6, 1), :], par)
        if live(6):
            self.ln_next.aggregate(dve, t6, par)
        if live(3):
            wait_alone(dve, self.exp_done, t3 + 1, self.ln.ready)
            dve.max(self.top[:, odd, :], self.e[:, odd, :]).then_inc(self.top_done, 1)
        if live(6):
            self.ln_next.variance(dve, t6, par)
        if live(3):
            wait_alone(dve, self.top_done, t3 + 1, self.ln.ready)
            dve.match_replace(self.rest[:, odd, :], self.top[:, odd, :], self.e[:, odd, :], 0.0).then_inc(self.rest_done, 1)
        if live(3):
            dve.reduce_sum(self.top_sum[:, odd:odd + 1], self.top[:, odd, :], AX_X)
            dve.reciprocal(self.inv_total[:, bass.ds(t3, 1)], self.total[:, odd:odd + 1]).then_inc(self.inv_done, 1)
            dve.wait_ge(self.rest_done, t3 + 1)
            if not known(t3) or t3 >= 2:
                dve.wait_ge(self.ct_done, t3 - 1)
            dve.tensor_tensor(self.chosen[:, odd, 0:EXPERTS], self.e[:, odd, :], self.rest[:, odd, :], ALU.subtract).then_inc(self.chosen_done, 1)
            dve.wait_ge(self.inv_done, t3 + 1)
            dve.tensor_tensor(self.weight_sum[:, odd:odd + 1], self.top_sum[:, odd:odd + 1], self.inv_total[:, bass.ds(t3, 1)], ALU.mult).then_inc(self.sum_done, 1)
        if live(5):
            dve.wait_ge(self.mix_done, t5 + 1)
            dve.wait_ge(self.scaled_done, t5 + 1)
            dve.scalar_tensor_tensor(tile_of(self.x, t5), self.ps_m, self.inv_total[:, bass.ds(t5, 1)], tile_of(self.x, t5),
                                     ALU.mult, ALU.add).then_inc(self.x_done, 1)
        if live(3):
            dve.wait_ge(self.sum_done, t3 + 1)
            if not known(t3) or t3 >= 2:
                dve.wait_ge(self.scaled_done, t3 - 1)
            dve.scalar_tensor_tensor(self.combined[:, odd, :], self.ln.factors[:, bass.ds(t3, 1), :].rearrange("p t n -> p (t n)"),
                                     self.weight_sum[:, odd:odd + 1], self.one_zero[:, :], ALU.mult, ALU.add).then_inc(self.combined_done, 1)
        if live(2):
            dve.wait_ge(self.l_done, t2 + 1)
            if not known(t2) or t2 >= 2:
                dve.wait_ge(self.exp_done, t2 - 1)
            dve.tensor_tensor(self.logits[:, par, :], self.ps_l[:, 0:EXPERTS], self.weights.logit_bias[:, :], ALU.add).then_inc(self.lb_done, 1)
        if live(9):
            t = i - 9
            dve.wait_ge(self.hi_done, t + 1)
            lo_part(dve, [p[:, :, bass.ds(t * P, P)] for p in self.h3], self.transposed()).then_inc(self.lo_done, 1)
        if live(2):
            dve.wait_ge(self.lb_done, t2 + 1)
            dve.tensor_reduce(self.neg_max[:, par:par + 1], self.logits[:, par, :], AX_X, ALU.max, negate=True).then_inc(self.max_done, 1)

    def pe_body(self, pe, i, par, live):
        odd = (par - 1) % 2
        if live(4):
            pe.wait_ge(self.chosen_done, i - 4 + 1)
            if live(2):
                pe.wait_ge(self.ht_done, i - 2 + 1)
            else:
                pe.wait_ge(self.ctc_done, i - 4)
            pe.transpose(self.ps_c[:, 0:P], self.chosen[:, par, :], self.ident[:, :]).then_inc(self.ct_done, 1)
        if live(9):
            t = i - 9
            pe.wait_ge(self.h_next_done, t + 1)
            if not known(t) or t >= 1:
                pe.wait_ge(self.lo_done, t)
            for c in range(KC):
                last = pe.transpose(self.ps_n[:, c * P:(c + 1) * P], self.h_next[:, odd, c * P:(c + 1) * P], self.ident[:, :])
            last.then_inc(self.tn_done, 1)
        if live(5):
            t = i - 5
            pe.wait_ge(self.ctc_done, t + 1)
            if not known(t) or t >= 1:
                pe.wait_ge(self.x_done, t)
            pe.matmul(self.ps_m, self.chosen_t[:, odd, :], self.weights.expert_bias[:, :], start=True, stop=True).then_inc(self.mix_done, 1)
        if live(2):
            t = i - 2
            pe.wait_ge(self.ht_done, t + 1)
            if not known(t) or t >= 1:
                pe.wait_ge(self.lb_done, t)
            for c in range(KC):
                last = pe.matmul(self.ps_l[:, 0:EXPERTS], self.ht[:, par, c * P:(c + 1) * P], self.weights.router[:, c, :],
                                 start=(c == 0), stop=(c == KC - 1))
            last.then_inc(self.l_done, 1)
        if live(1):
            t = i - 1
            pe.wait_ge(self.h_done, t + 1)
            if not known(i) or i - 4 >= 0:
                pe.wait_ge(self.ctc_done, i - 4 + 1)
            elif t >= 1:
                pe.wait_ge(self.ht_done, t)
            for c in range(KC):
                last = pe.transpose(self.ps_t[:, c * P:(c + 1) * P], self.h[:, odd, c * P:(c + 1) * P], self.ident[:, :])
            last.then_inc(self.t_done, 1)




def kv_tasks():
    tasks = []
    for quad in range(2):
        down = [("Z", quad, j, 0) for j in range(8)]
        flip = [("C", quad, jp, hg) for jp in range(4) for hg in range(2)]
        keys = [("K", quad, pair, g) for pair in range(2) for g in range(KV_HEADS)]
        values = [("V", quad, tile, part) for tile in range(8) for part in range(2)]
        tasks += down[0:4] + flip[0:2] + down[4:6] + flip[2:4] + down[6:8] + flip[4:6] + keys[0:2] + flip[6:8] + keys[2:] + values
    return tasks


def routed_bias_and_keys(nc, sem, sb, ps, split, x, ident, ln, ln_next, weights, h3, kv_w, stream, wq_g, k_scr, v_scr):
    SPAN = 4 * SEQ
    STAGES = 4
    DEPTH = RoutedBias.DEPTH
    tasks = kv_tasks()
    at = {task: n for n, task in enumerate(tasks)}
    hi_order = [n for n, task in enumerate(tasks) if task[0] == "C"]
    lo_count = {n: k + 1 for k, n in enumerate(hi_order)}
    down_order = [n for n, task in enumerate(tasks) if task[0] == "Z"]
    down_count = {n: k + 1 for k, n in enumerate(down_order)}
    stage_order = [n for n, task in enumerate(tasks) if task[0] in "KV"]
    stage_count = {n: k for k, n in enumerate(stage_order)}

    with ExitStack() as st:
        whole_w = [w[:, :, :].rearrange("p a n -> p (a n)") for w in kv_w]
        down_w = [w[:, 0:KV_DOWN].rearrange("p (c n) -> p c n", c=KC) for w in whole_w]
        up_w = [[w[:, KV_DOWN + n * KV_UP:KV_DOWN + (n + 1) * KV_UP].rearrange("p (c n) -> p c n", c=2) for w in whole_w] for n in range(2)]
        z = stream.raw[:, :, :].rearrange("p (j h) (h2 t l) -> p j (h h2) t l", j=2, h2=4, t=2)
        latent = split("latent", [P, 4, 4, KV_HEADS, BLOCK], st)
        bank = ps("kv_banks", [P, 8, HID], st)
        with ExitStack() as shared:
            routed = RoutedBias(sem, sb, bank[:, 4:8, :], x, ident, ln, ln_next, weights, h3, shared)
        stage = [sb(f"kv_stage{n}", [P, HID], F32, st) for n in range(STAGES)]

        task_done, z_done, hi_done, lo_done = sem("kv_task_done"), sem("kv_z_done"), sem("kv_hi_done"), sem("kv_lo_done")
        staged = sem("kv_staged")
        stored = [sem(f"kv_stored{n}") for n in range(STAGES)]

        begin = DEPTH - TILES // 2 - 1
        paired = DEPTH - begin
        bank_of = [n % 4 if n < paired else (n - paired + 4) % 8 for n in range(len(tasks))]

        def freed(eng, n):
            before = [m for m in range(n) if bank_of[m] == bank_of[n]]
            if not before:
                if bank_of[n] >= 4:
                    eng.wait_ge(routed.lo_done, TILES)
            elif before[-1] in down_count:
                eng.wait_ge(z_done, down_count[before[-1]])
            elif before[-1] in stage_count:
                eng.wait_ge(staged, stage_count[before[-1]] + 1)
            else:
                eng.wait_ge(lo_done, lo_count[before[-1]])

        def outlet(n):
            _, _, a, b = tasks[n]
            return ([p[:, a, :, 4 * b:4 * b + 4, :].rearrange("p b h m -> p h b m") for p in latent],
                    bank[:, bank_of[n], :].rearrange("p (h b m) -> p h b m", h=4, b=4))

        wq = attention_weights(kv_w)[0]
        query_weights = {at[("V", 1, 2 * n, 0)]: n for n in range(4)}

        def interleaved(eng, body, task):
            skewed(eng, DEPTH, lambda i, par, live: body(eng, i, par, live), first=DEPTH + DEPTH % 2,
                   tail=lambda n: task(n - begin) if n >= begin else None)
            for n in range(paired, len(tasks)):
                task(n)

        with nc.Block() as block:
            @block.gpsimd
            def _(pool):
                routed.set_constants(pool)
                skewed(pool, DEPTH, lambda i, par, live: routed.pool_body(pool, i, par, live), first=DEPTH + DEPTH % 2)

            @block.sync
            def _(sp):
                for k, n in enumerate(stage_order):
                    kind, quad, a, b = tasks[n]
                    sp.wait_ge(staged, k + 1)
                    if k >= STAGES:
                        sp.wait_ge(stored[k % STAGES], 16 * (k // STAGES))
                    if kind == "K":
                        pair = 2 * quad + a
                        dst = k_scr[b, :, pair * PAIR:(pair + 1) * PAIR]
                    else:
                        pair = 2 * quad + a // 4
                        dst = v_scr[pair, :, a % 4, b * HID:(b + 1) * HID]
                    sp.dma_start(dst, stage[k % STAGES][:, :]).then_inc(stored[k % STAGES], 16)
                    if n == at[("K", 1, 0, 2)]:
                        sp.wait_ge(task_done, at[("C", 1, 3, 1)] + 1)
                        stream.load(sp, wq_g[0, :, :, :], 0)

            @block.scalar
            def _(act):
                def task(n):
                    kind, quad, a, b = tasks[n]
                    act.wait_ge(task_done, n + 1)
                    if kind == "Z":
                        before = [at[("C", q, jp, 1)] for q, jp in [(quad, a // 2 - 2) if a >= 4 else (quad - 1, a // 2 + 2)] if q >= 0]
                        if before:
                            act.wait_ge(task_done, before[0] + 1)
                        act.activation(z[:, a // 2 % 2, :, a % 2, :].rearrange("p h (t l) -> p h t l", t=2),
                                       bank[:, bank_of[n], :].rearrange("p (t h l) -> p h t l", t=2, h=KV_HEADS), ACT.Copy).then_inc(z_done, 1)
                    else:
                        if kind == "C" and quad == 1:
                            act.wait_ge(task_done, at[("K", 0, 1, KV_HEADS - 1) if a < 2 else ("V", 0, 7, 1)] + 1)
                        if kind == "C":
                            parts, src = outlet(n)
                            hi_part(act, parts, src).then_inc(hi_done, 1)
                        else:
                            k = stage_count[n]
                            if k >= STAGES:
                                act.wait_ge(stored[k % STAGES], 16 * (k // STAGES))
                            else:
                                act.wait_ge(routed.lo_done, TILES)
                            act.activation(stage[k % STAGES][:, :], bank[:, bank_of[n], :], ACT.Copy).then_inc(staged, 1)
                        if n in query_weights:
                            stream.hi(act, wq, query_weights[n], 0)

                interleaved(act, routed.act_body, task)

            @block.vector
            def _(dve):
                routed.await_constants(dve)

                def task(n):
                    if n in lo_count:
                        dve.wait_ge(hi_done, lo_count[n])
                        parts, src = outlet(n)
                        lo_part(dve, parts, src).then_inc(lo_done, 1)
                    if n in query_weights:
                        stream.lo(dve, wq, query_weights[n], 0)

                interleaved(dve, routed.dve_body, task)

            @block.tensor
            def _(pe):
                routed.await_constants(pe)

                def task(n):
                    kind, quad, a, b = tasks[n]
                    freed(pe, n)
                    out = bank[:, bank_of[n], :]
                    if kind == "Z":
                        pe.wait_ge(routed.lo_done, (quad + 1) * TILES // 2)
                        for c in range(KC):
                            for m, (u, v) in enumerate(PASSES):
                                tokens = h3[u][:, c, quad * SPAN:(quad + 1) * SPAN].rearrange("p (n j) -> p n j", j=8)[:, :, a]
                                last = pe.matmul(out, tokens, down_w[v][:, c, :], start=(c == 0 and m == 0), stop=(c == KC - 1 and m == 2))
                    elif kind == "C":
                        pe.wait_ge(z_done, down_count[at[("Z", quad, 2 * a + 1, 0)]])
                        for h in range(4):
                            last = pe.transpose(out[:, h * P:(h + 1) * P], z[:, a % 2, 4 * b + h, :, :].rearrange("p j l -> p (j l)"), ident[:, :])
                    elif kind == "K":
                        if (a, b) == (0, 0):
                            pe.wait_ge(lo_done, lo_count[at[("C", quad, 1, 1)]])
                        for c in range(2):
                            for m, (u, v) in enumerate(PASSES):
                                last = pe.matmul(out, up_w[0][u][:, c, b * HEAD:(b + 1) * HEAD],
                                                 latent[v][:, c, 2 * a:2 * a + 2, :, :].rearrange("p b h m -> p (b h m)"),
                                                 start=(c == 0 and m == 0), stop=(c == 1 and m == 2))
                    else:
                        if (a, b) == (0, 0):
                            pe.wait_ge(lo_done, lo_count[at[("C", quad, 3, 1)]])
                        for c in range(2):
                            for m, (u, v) in enumerate(PASSES):
                                rows = latent[u][:, 2 + c, a // 2, 4 * (a % 2):4 * (a % 2) + 4, :].rearrange("p h m -> p (h m)")
                                last = pe.matmul(out, rows, up_w[1][v][:, c, b * HID:(b + 1) * HID],
                                                 start=(c == 0 and m == 0), stop=(c == 1 and m == 2))
                    last.then_inc(task_done, 1)

                interleaved(pe, routed.pe_body, task)

    return [(stored[k], 16 * (len(stage_order) // STAGES)) for k in range(STAGES)]


def attention(nc, sem, sb, ps, split, x, ident, h3, kv_w, stream, stored, feed, wq_g, wo_g, k_scr, v_scr):
    HEADS = 2 * GROUP
    with ExitStack() as st:
        wq, wo, spare = attention_weights(kv_w)
        w_lo = stream.w_lo
        q_first = sb("q_first", [P, GROUP, 2, P], F32, st)
        q_second = [w[:, 0:2, :].rearrange("p a (h b n) -> p (a h) b n", h=2, b=2) for w in spare]
        k_raw = sb("k_raw", [P, 2, SEQ], F32, st)
        k = split("k", [P, 2, SEQ], st)
        v_raw = sb("v_raw", [P, 4, HEAD], F32, st)
        v = split("v", [P, 4, HEAD], st)
        prob = sb("prob", [P, 2, GROUP, 3 * P], F32, st)
        neg_max = sb("neg_max", [P, 2, GROUP, 2], F32, st)
        row_sum = sb("row_sum", [P, 2, GROUP, 2], F32, st)
        inv_sum = sb("inv_sum", [P, 2, GROUP, 2], F32, st)
        prob_t = split("prob_t", [P, 3, GROUP * P], st)
        o = [split("o0", [P, 2, GROUP, P], st), [w[:, 2:4, :].rearrange("p t (h n) -> p t h n", h=GROUP) for w in spare]]
        causal = sb("causal", [P, 2 * P], F32, st)
        ps_s = ps("ps_s", [P, GROUP, HID], st)
        ps_t = ps_s[:, 2:4, :]
        ps_q = ps("ps_q", [P, 2, HID], st)
        ps_o = ps("ps_o", [P, 2, HID], st)

        k_loaded, v_loaded = sem("k_loaded"), sem("v_loaded")
        mask_zero, mask_done = sem("mask_zero"), sem("mask_done")
        k_hi, k_lo, v_hi, v_lo = sem("k_hi"), sem("k_lo"), sem("v_hi"), sem("v_lo")
        s_done = sem("s_done")
        scored = sem("scored")
        exped, inv_done, normed = sem("exped"), sem("inv_done"), sem("normed")
        q_done, q_hi, q_read = sem("q_done"), sem("q_hi"), sem("q_read")
        t_done, t_hi, t_lo = sem("pt_done"), sem("pt_hi"), sem("pt_lo")
        pv_done, o_hi, o_lo = sem("pv_done"), sem("o_hi"), sem("o_lo")
        y_done, y_read = sem("y_done"), sem("y_read")

        UNITS = PAIRS * KV_HEADS
        LAST = KV_HEADS - 1

        def scratch_written(eng):
            for done, count in stored:
                eng.wait_ge(done, count)

        def groups(eng, group):
            group(0, True, False)
            with eng.Fori(1, LAST) as g:
                group(g, False, False)
            group(LAST, False, True)

        with nc.Block() as block:
            @block.sync
            def _(sp):
                def group(g, first, last):
                    for p in range(PAIRS):
                        u = PAIRS * g + p
                        if not (first and p == 0):
                            sp.wait_ge(s_done, HEADS * u)
                        sp.dma_start(k_raw[:, :, :].rearrange("p b n -> p (b n)"),
                                     k_scr[bass.ds(g, 1), :, p * PAIR:(p + 1) * PAIR].rearrange("g p n -> p (g n)")).then_inc(k_loaded, 16)
                        if not (first and p == 0):
                            sp.wait_ge(v_lo, u)
                        sp.dma_start(v_raw[:, :, :], v_scr[p, :, :, bass.ds(g * HEAD, HEAD)]).then_inc(v_loaded, 16)
                        if last and p == PAIRS - 1:
                            sp.wait_ge(v_lo, u + 1)
                            feed.load_gate(sp, v_raw[:, :, :].rearrange("p t d -> p (t d)"))
                        if p == 0:
                            stream.load(sp, wo_g[bass.ds(g, 1), :, :, :].rearrange("a p h n -> p (a h) n"), 2 * g + 1)
                        if p == 1 and not last:
                            stream.load(sp, wq_g[bass.ds(g + 1, 1), :, :, :].rearrange("a p c n -> p (a c) n"), 2 * g + 2)

                scratch_written(sp)
                groups(sp, group)

            @block.gpsimd
            def _(pool):
                scratch_written(pool)
                pool.memset(causal[:, :], 0.0).then_inc(mask_zero, 1)
                pool.wait_ge(mask_zero, 1)
                pool.affine_select(out=causal[:, P:2 * P], in_=causal[:, P:2 * P], compare_op=ALU.is_ge, fill=MASKED, base=0,
                                   pattern=[[-1, P]], channel_multiplier=1).then_inc(mask_done, 1)

                def group(g, first, last):
                    for p in range(PAIRS):
                        u = PAIRS * g + p
                        for b in range(2):
                            for h in range(GROUP):
                                wait_alone(pool, inv_done, HEADS * u + GROUP * b + h + 1, mask_done)
                                pool.tensor_scalar(prob[:, b, h, 0:P], prob[:, b, h, 0:P], inv_sum[:, b, h, 0:1], 1.0, ALU.mult, ALU.mult)
                                pool.tensor_scalar(prob[:, b, h, P:3 * P], prob[:, b, h, P:3 * P], inv_sum[:, b, h, 1:2], 1.0,
                                                   ALU.mult, ALU.mult).then_inc(normed, 1)
                        if last and p == 1:
                            for t in range(4):
                                feed.ln.power(pool, t)

                groups(pool, group)

            @block.scalar
            def _(act):
                def keys_hi(u):
                    act.wait_ge(k_loaded, 16 * u + 16)
                    hi_part(act, [w[:, :, :] for w in k], k_raw[:, :, :]).then_inc(k_hi, 1)

                def query_hi(h, count):
                    act.wait_ge(q_done, count)
                    by_tile = ps_q[:, h % 2, :].rearrange("p (b t n) -> p b t n", b=2, t=2)
                    act.activation(q_first[:, h, :, :], by_tile[:, :, 0, :], ACT.Copy)
                    hi_part(act, [w[:, h, :, :] for w in q_second], by_tile[:, :, 1, :]).then_inc(q_hi, 1)

                def group(g, first, last):
                    for p in range(PAIRS):
                        u = PAIRS * g + p
                        start = first and p == 0
                        more = not (last and p == PAIRS - 1)
                        def exponentials(b, h):
                            act.wait_ge(scored, HEADS * u + GROUP * b + h + 1)
                            act.activation(prob[:, b, h, 0:P], prob[:, b, h, 0:P], ACT.Exp, scale=-1.0,
                                           bias=neg_max[:, b, h, 0:1], accum_out=row_sum[:, b, h, 0:1])
                            act.activation(prob[:, b, h, P:3 * P], prob[:, b, h, P:3 * P], ACT.Exp, scale=-1.0,
                                           bias=neg_max[:, b, h, 1:2], accum_out=row_sum[:, b, h, 1:2]).then_inc(exped, 1)

                        def query(h):
                            if more:
                                query_hi(h, GROUP * (u + 1) + h + 1)
                            else:
                                feed.part(act, ps_q[:, h % 2, :], h, HI)
                                if h == GROUP - 1:
                                    feed.gate_part(act, v_raw[:, :, :].rearrange("p t d -> p (t d)"), HI)
                            if p == 0:
                                if h == 0 and not first:
                                    act.wait_ge(y_done, 4 * u)
                                stream.hi(act, wo, h, 2 * g + 1)

                        def prob_hi(b, blk):
                            act.wait_ge(t_done, 6 * u + 3 * b + blk + 1)
                            if not (start and b == 0):
                                act.wait_ge(pv_done, 4 * u + 2 * b - 1 + (blk > 0))
                            hi_part(act, [w[:, blk, :] for w in prob_t], ps_t[:, (b + blk) % 2, :]).then_inc(t_hi, 1)

                        def out_hi(b, half):
                            act.wait_ge(pv_done, 4 * u + 2 * b + half + 1)
                            if not start:
                                act.wait_ge(y_done, 4 * (u - 1) + 2 * b + half + 1)
                            hi_part(act, [w[:, half, :, :].rearrange("p h n -> p (h n)") for w in o[b]], ps_o[:, half, :]).then_inc(o_hi, 1)

                        split_next = p == 2 and not last
                        for h in range(GROUP):
                            exponentials(0, h)
                        if not start:
                            act.wait_ge(pv_done, 4 * u)
                        act.wait_ge(v_loaded, 16 * u + 16)
                        hi_part(act, [w[:, :, :] for w in v], v_raw[:, :, :]).then_inc(v_hi, 1)
                        exponentials(1, 0)
                        exponentials(1, 1)
                        query(0)
                        exponentials(1, 2)
                        exponentials(1, 3)
                        if more:
                            query(1)
                            prob_hi(0, 0)
                            prob_hi(0, 1)
                            query(2)
                            prob_hi(0, 2)
                            query(3)
                            out_hi(0, 0)
                            out_hi(0, 1)
                        else:
                            prob_hi(0, 0)
                            prob_hi(0, 1)
                            prob_hi(0, 2)
                            query(1)
                            out_hi(0, 0)
                            query(2)
                            out_hi(0, 1)
                            query(3)
                        prob_hi(1, 0)
                        prob_hi(1, 1)
                        if split_next:
                            act.wait_ge(q_done, GROUP * (u + 2))
                            stream.hi(act, wq, 0, 2 * g + 2)
                            stream.hi(act, wq, 1, 2 * g + 2)
                        prob_hi(1, 2)
                        if more:
                            keys_hi(u + 1)
                        out_hi(1, 0)
                        if split_next:
                            stream.hi(act, wq, 2, 2 * g + 2)
                            stream.hi(act, wq, 3, 2 * g + 2)
                        out_hi(1, 1)

                scratch_written(act)
                for h in range(GROUP):
                    query_hi(h, h + 1)
                keys_hi(0)
                groups(act, group)

            @block.vector
            def _(dve):
                def keys_lo(u):
                    dve.wait_ge(k_hi, u + 1)
                    lo_part(dve, [w[:, :, :] for w in k], k_raw[:, :, :]).then_inc(k_lo, 1)

                def query_lo(h, count):
                    dve.wait_ge(q_hi, count)
                    by_tile = ps_q[:, h % 2, :].rearrange("p (b t n) -> p b t n", b=2, t=2)
                    lo_part(dve, [w[:, h, :, :] for w in q_second], by_tile[:, :, 1, :]).then_inc(q_read, 1)

                def add(u, p, b, half):
                    dve.wait_ge(y_done, 4 * u + 2 * b + half + 1)
                    t = 4 * p + 2 * b + half
                    dve.tensor_tensor(x[:, t, :], ps_q[:, half, :], x[:, t, :], ALU.add).then_inc(y_read, 1)

                def group(g, first, last):
                    for p in range(PAIRS):
                        u = PAIRS * g + p
                        start = first and p == 0
                        more = not (last and p == PAIRS - 1)

                        def score(b, h):
                            if not start and h == 0:
                                dve.wait_ge(t_done, 6 * (u - 1) + 3 * b + 3)
                            wait_alone(dve, s_done, HEADS * u + GROUP * b + h + 1, mask_done)
                            dve.tensor_tensor_reduce(out=prob[:, b, h, 0:P], in0=ps_s[:, h, 0:P], in1=causal[:, P:2 * P], scale=-SCALE,
                                                     scalar=3.0e38, op0=ALU.add, op1=ALU.min, accum_out=neg_max[:, b, h, 0:1])
                            dve.tensor_tensor_reduce(out=prob[:, b, h, P:3 * P], in0=ps_s[:, h, 2 * P:4 * P], in1=causal[:, :], scale=-SCALE,
                                                     scalar=3.0e38, op0=ALU.add, op1=ALU.min, accum_out=neg_max[:, b, h, 1:2]).then_inc(scored, 1)

                        def inverse(b, h):
                            dve.wait_ge(exped, HEADS * u + GROUP * b + h + 1)
                            dve.reciprocal(inv_sum[:, b, h, :], row_sum[:, b, h, :]).then_inc(inv_done, 1)

                        def query(h):
                            if more:
                                query_lo(h, GROUP * (u + 1) + h + 1)
                            else:
                                feed.part(dve, ps_q[:, h % 2, :], h, LO)
                                if h == GROUP - 1:
                                    feed.gate_part(dve, v_raw[:, :, :].rearrange("p t d -> p (t d)"), LO)
                            if last and p == 1:
                                if h == 0:
                                    dve.wait_ge(y_read, 4 * u)
                                feed.statistics(dve, h)
                            if last and p == 2:
                                if h == 0:
                                    dve.wait_ge(w_lo, 4 * (2 * g + 2))
                                feed.ln.apply(dve, stream.raw[:, h, :], x[:, h, :], h).then_inc(feed.h_done, 1)
                            if p == 0:
                                stream.lo(dve, wo, h, 2 * g + 1)

                        def prob_lo(b, blk):
                            dve.wait_ge(t_hi, 6 * u + 3 * b + blk + 1)
                            lo_part(dve, [w[:, blk, :] for w in prob_t], ps_t[:, (b + blk) % 2, :]).then_inc(t_lo, 1)

                        def out_lo(b, half):
                            dve.wait_ge(o_hi, 4 * u + 2 * b + half + 1)
                            lo_part(dve, [w[:, half, :, :].rearrange("p h n -> p (h n)") for w in o[b]], ps_o[:, half, :]).then_inc(o_lo, 1)

                        for h in range(GROUP):
                            score(0, h)
                        if more and not start:
                            add(u - 1, (p - 1) % PAIRS, 1, 1)
                        for h in range(GROUP):
                            inverse(0, h)
                        dve.wait_ge(v_hi, u + 1)
                        lo_part(dve, [w[:, :, :] for w in v], v_raw[:, :, :]).then_inc(v_lo, 1)
                        if not more:
                            add(u - 1, p - 1, 1, 0)
                        for h in range(GROUP):
                            score(1, h)
                        inverse(1, 0)
                        query(0)
                        for h in range(1, GROUP):
                            inverse(1, h)
                        split_next = p == 2 and not last
                        if more:
                            query(1)
                            prob_lo(0, 0)
                            prob_lo(0, 1)
                            query(2)
                            prob_lo(0, 2)
                            query(3)
                            out_lo(0, 0)
                            out_lo(0, 1)
                        else:
                            prob_lo(0, 0)
                            prob_lo(0, 1)
                            add(u - 1, p - 1, 1, 1)
                            prob_lo(0, 2)
                            query(1)
                            out_lo(0, 0)
                            query(2)
                            out_lo(0, 1)
                            query(3)
                        prob_lo(1, 0)
                        prob_lo(1, 1)
                        if split_next:
                            stream.lo(dve, wq, 0, 2 * g + 2)
                            stream.lo(dve, wq, 1, 2 * g + 2)
                        add(u, p, 0, 0)
                        prob_lo(1, 2)
                        if more:
                            keys_lo(u + 1)
                        out_lo(1, 0)
                        if split_next:
                            stream.lo(dve, wq, 2, 2 * g + 2)
                            stream.lo(dve, wq, 3, 2 * g + 2)
                        add(u, p, 0, 1)
                        out_lo(1, 1)
                        if not (last and p == PAIRS - 2):
                            add(u, p, 1, 0)

                scratch_written(dve)
                for h in range(GROUP):
                    query_lo(h, h + 1)
                keys_lo(0)
                groups(dve, group)
                add(UNITS - 1, PAIRS - 1, 1, 1)

            @block.tensor
            def _(pe):
                def project_query(h, pair):
                    for c in range(KC):
                        for n, (a, b) in enumerate(PASSES):
                            last = pe.matmul(ps_q[:, h % 2, :], wq[a][:, c, h * HEAD:(h + 1) * HEAD], h3[b][:, c, pair * PAIR:(pair + 1) * PAIR],
                                             start=(c == 0 and n == 0), stop=(c == KC - 1 and n == 2))
                    last.then_inc(q_done, 1)

                def group(g, first, last):
                    for p in range(PAIRS):
                        u = PAIRS * g + p
                        start = first and p == 0
                        more = not (last and p == PAIRS - 1)

                        def scores(b):
                            for h in range(GROUP):
                                n = HEADS * u + GROUP * b + h
                                if b:
                                    pe.wait_ge(scored, n - GROUP + 1)
                                elif not start:
                                    if h < 2:
                                        pe.wait_ge(scored, n - GROUP + 1)
                                    else:
                                        pe.wait_ge(t_lo, 6 * u)
                                pe.matmul(ps_s[:, h, 0:P], q_first[:, h, b, :], k_raw[:, b, 0:P], start=True, stop=True)
                                for m, (i, j) in enumerate(PASSES):
                                    done = pe.matmul(ps_s[:, h, 2 * P:4 * P], q_second[i][:, h, b, :], k[j][:, b, :], start=(m == 0), stop=(m == 2))
                                done.then_inc(s_done, 1)

                        def query(h):
                            if h == 0 and p == PAIRS - 1 and more:
                                pe.wait_ge(w_lo, 4 * (2 * g + 2) + 4)
                            if h < 2:
                                if not start:
                                    pe.wait_ge(y_read, 4 * u - 1 + h)
                            elif not more:
                                pe.wait_ge(feed.h_lo, h - 1)
                            else:
                                pe.wait_ge(q_read, GROUP * (u + 1) + h - 1)
                            if more:
                                project_query(h, (p + 1) % PAIRS)
                            else:
                                feed.flip(pe, stream.raw, ps_q[:, h % 2, :], h)

                        def flip(b, blk):
                            n = 6 * u + 3 * b + blk
                            if blk == 0:
                                pe.wait_ge(normed, HEADS * u + GROUP * (b + 1))
                            if b == 0 and blk < 2:
                                pe.wait_ge(scored, HEADS * u + GROUP + 3 + blk)
                            else:
                                pe.wait_ge(t_lo, n - 1)
                            for h in range(GROUP):
                                done = pe.transpose(ps_t[:, (b + blk) % 2, h * P:(h + 1) * P], prob[:, b, h, blk * P:(blk + 1) * P], ident[:, :])
                            done.then_inc(t_done, 1)

                        def values(b, half):
                            if b == 0 and half == 0:
                                pe.wait_ge(v_lo, u + 1)
                            if not (start and b == 0):
                                pe.wait_ge(o_lo, 4 * u + 2 * b - 1 + half)
                            blocks = (((0, 0),), ((1, 0), (2, 1)))[half]
                            for n, (blk, tile) in enumerate(blocks):
                                pe.wait_ge(t_lo, 6 * u + 3 * b + blk + 1)
                                for m, (i, j) in enumerate(PASSES):
                                    done = pe.matmul(ps_o[:, half, :], v[i][:, 2 * b + tile, :], prob_t[j][:, blk, :],
                                                     start=(n == 0 and m == 0), stop=(n == len(blocks) - 1 and m == 2))
                            done.then_inc(pv_done, 1)

                        def output(b, half, u=u):
                            if b == 0 and half == 0 and p == 0:
                                pe.wait_ge(w_lo, 4 * (2 * g + 1) + 4)
                            if b == 0:
                                if more:
                                    pe.wait_ge(q_read, GROUP * (u + 1) + 3 + half)
                                else:
                                    pe.wait_ge(feed.h_lo, 3 + half)
                            else:
                                pe.wait_ge(y_read, 4 * u + 1 + half)
                            pe.wait_ge(o_lo, 4 * u + 2 * b + half + 1)
                            for h in range(GROUP):
                                for m, (i, j) in enumerate(PASSES):
                                    done = pe.matmul(ps_q[:, half, :], o[b][i][:, half, h, :], wo[j][:, h, :],
                                                     start=(h == 0 and m == 0), stop=(h == GROUP - 1 and m == 2))
                            done.then_inc(y_done, 1)

                        pe.wait_ge(k_lo, u + 1)
                        pe.wait_ge(q_read, GROUP * (u + 1))
                        scores(0)
                        if not more:
                            output(1, 0, u - 1)
                        else:
                            query(0)
                        scores(1)
                        query(1 if more else 0)
                        flip(0, 0)
                        flip(0, 1)
                        if more:
                            query(2)
                            flip(0, 2)
                            query(3)
                            values(0, 0)
                            values(0, 1)
                        else:
                            output(1, 1, u - 1)
                            flip(0, 2)
                            query(1)
                            values(0, 0)
                            query(2)
                            values(0, 1)
                            query(3)
                        flip(1, 0)
                        flip(1, 1)
                        output(0, 0)
                        flip(1, 2)
                        values(1, 0)
                        output(0, 1)
                        values(1, 1)
                        if not (last and p == PAIRS - 2):
                            output(1, 0)
                            output(1, 1)

                pe.wait_ge(w_lo, 4)
                for h in range(GROUP):
                    if h >= 2:
                        pe.wait_ge(q_read, h - 1)
                    project_query(h, 0)
                groups(pe, group)


def feed_forward(nc, sem, sb, ps, split, x, ident, ln, feed, gate_c, up_c, down_c, scales, out):
    with ExitStack() as st:
        gate, ht = feed.gate, feed.ht
        up = split("up", [P, CHUNKS, KC, P], st)
        down = split("down", [P, CHUNKS, HID], st)
        raw = [sb(f"f_raw{n}", [P, HID], F32, st) for n in range(3)]
        h = sb("h3n", [P, 4, HID], F32, st)
        act_buf = sb("f_act", [P, 4 * P], F32, st)
        inner = [feed.spare, split("inner1", [P, 4 * P], st)]
        scale = sb("f_scale", [P, 3], F32, st)
        ps_r = ps("f_ps_r", [P, 4, HID], st)
        ps_y = ps("f_ps_y", [P, 4, HID], st)

        scale_loaded = sem("f_scale_loaded")
        raw_loaded, w_hi, w_lo = feed.raw_loaded, feed.w_hi, feed.w_lo
        h_done, t_done, h_hi, h_lo = feed.h_done, feed.t_done, feed.h_hi, feed.h_lo
        gate_done, up_done, silu_done, prod_done = sem("f_gate_done"), sem("f_up_done"), sem("f_silu_done"), sem("f_prod_done")
        inner_hi, inner_lo = sem("f_inner_hi"), sem("f_inner_lo")
        down_used, y_done, x_done, stored = sem("f_down_used"), sem("f_y_done"), sem("f_x_done"), sem("f_stored")

        LAST = GROUPS - 1
        weights = (gate, up, down)
        FLIP = 2 * CHUNKS

        def groups(eng, group):
            group(0, True, False)
            with eng.Fori(1, LAST) as g:
                group(g, False, False)
            group(LAST, False, True)

        def piece(w, c):
            if w is down:
                return [part[:, c, :] for part in w]
            return [part[:, c, :, :].rearrange("p c n -> p (c n)") for part in w]

        with nc.Block() as block:
            @block.sync
            def _(sp):
                sp.dma_start(scale[:, :], scales.partition_broadcast(P)).then_inc(scale_loaded, 16)
                for c in range(CHUNKS):
                    for n, src in enumerate((gate_c, up_c, down_c)):
                        if (c, n) == (0, 0):
                            continue
                        if c:
                            sp.wait_ge(w_lo, 3 * (c - 1) + n + 1)
                        sp.dma_start(raw[n][:, :], src[c, :, :]).then_inc(raw_loaded[n], 16)

                def group(g, first, last):
                    for tt in range(4):
                        t = 4 * g + tt
                        sp.wait_ge(x_done, t + 1)
                        sp.dma_start(out[bass.ds(t * P, P), :].rearrange("(a p) f -> p a f", a=1), x[:, bass.ds(t, 1), :]).then_inc(stored, 16)

                groups(sp, group)
                sp.wait_ge(stored, 16 * TILES)

            @block.gpsimd
            def _(pool):
                def group(g, first, last):
                    if not last:
                        for tt in range(4):
                            ln.power(pool, 4 * (g + 1) + tt)

                groups(pool, group)

            @block.scalar
            def _(act):
                def flipped(g):
                    for tt in range(4):
                        act.wait_ge(t_done, 4 * g + tt + 1)
                        ring = (FLIP + tt) % 4
                        hi_part(act, [w[:, :, tt * P:(tt + 1) * P] for w in ht], ps_r[:, ring, :].rearrange("p (c n) -> p c n", c=KC)).then_inc(h_hi, 1)

                def weight_hi(c):
                    for n, w in enumerate(weights):
                        if (c, n) == (0, 0):
                            continue
                        act.wait_ge(raw_loaded[n], 16 * (c + 1))
                        hi_part(act, piece(w, c), raw[n][:, :]).then_inc(w_hi, 1)

                def group(g, first, last):
                    for c in range(CHUNKS):
                        at = CHUNKS * g + c
                        if first and c + 1 < CHUNKS:
                            weight_hi(c + 1)
                        act.wait_ge(gate_done, at + 1)
                        if not (first and c == 0):
                            act.wait_ge(inner_lo, at)
                        act.activation(act_buf[:, :], ps_r[:, 2 * c % 4, :], ACT.Silu, scale=scale[:, 0:1]).then_inc(silu_done, 1)
                        act.wait_ge(prod_done, at + 1)
                        if c >= 2:
                            act.wait_ge(down_used, (CHUNKS - 1) * g + c - 1)
                        elif not first:
                            act.wait_ge(y_done, 4 * g)
                        hi_part(act, [w[:, :] for w in inner[c % 2]], act_buf[:, :]).then_inc(inner_hi, 1)
                    if not last:
                        flipped(g + 1)

                act.wait_ge(scale_loaded, 16)
                weight_hi(0)
                groups(act, group)

            @block.vector
            def _(dve):
                def normalize(g, tt):
                    t = 4 * g + tt
                    par = tt % 2
                    tile = x[:, bass.ds(t, 1), :].rearrange("p a f -> p (a f)")
                    ln.stats(dve, tile, par)
                    ln.aggregate(dve, t, par)
                    ln.variance(dve, t, par)
                    if not known(g) or g >= 2:
                        dve.wait_ge(t_done, 4 * (g - 1) + tt + 1)
                    ln.apply(dve, h[:, tt, :], tile, t).then_inc(h_done, 1)

                def flipped(g):
                    for tt in range(4):
                        dve.wait_ge(h_hi, 4 * g + tt + 1)
                        ring = (FLIP + tt) % 4
                        lo_part(dve, [w[:, :, tt * P:(tt + 1) * P] for w in ht], ps_r[:, ring, :].rearrange("p (c n) -> p c n", c=KC)).then_inc(h_lo, 1)

                def weight_lo(c):
                    for n, w in enumerate(weights):
                        if (c, n) == (0, 0):
                            continue
                        dve.wait_ge(w_hi, 3 * c + n + 1)
                        lo_part(dve, piece(w, c), raw[n][:, :]).then_inc(w_lo, 1)

                def group(g, first, last):
                    for c in range(CHUNKS):
                        at = CHUNKS * g + c
                        if first and c + 1 < CHUNKS:
                            weight_lo(c + 1)
                        if not last and 2 <= c < 6:
                            normalize(g + 1, c - 2)
                        dve.wait_ge(up_done, at + 1)
                        dve.wait_ge(silu_done, at + 1)
                        dve.scalar_tensor_tensor(act_buf[:, :], ps_r[:, (2 * c + 1) % 4, :], scale[:, 1:2], act_buf[:, :],
                                                 ALU.mult, ALU.mult).then_inc(prod_done, 1)
                        dve.wait_ge(inner_hi, at + 1)
                        lo_part(dve, [w[:, :] for w in inner[c % 2]], act_buf[:, :]).then_inc(inner_lo, 1)
                    if not last:
                        flipped(g + 1)
                    for tt in range(4):
                        t = 4 * g + tt
                        dve.wait_ge(y_done, t + 1)
                        tile = x[:, bass.ds(t, 1), :].rearrange("p a f -> p (a f)")
                        dve.scalar_tensor_tensor(tile, ps_y[:, tt, :], scale[:, 2:3], tile, ALU.mult, ALU.add).then_inc(x_done, 1)

                dve.wait_ge(scale_loaded, 16)
                weight_lo(0)
                groups(dve, group)

            @block.tensor
            def _(pe):
                def flip(g):
                    for tt in range(4):
                        pe.wait_ge(h_done, 4 * g + tt + 1)
                        ring = (FLIP + tt) % 4
                        pe.wait_ge((silu_done, prod_done)[tt % 2], CHUNKS * g - (1 if tt < 2 else 0))
                        for c in range(KC):
                            last = pe.transpose(ps_r[:, ring, c * P:(c + 1) * P], h[:, tt, c * P:(c + 1) * P], ident[:, :])
                        last.then_inc(t_done, 1)

                def project(w, c, bank, done):
                    for k in range(KC):
                        for n, (a, b) in enumerate(PASSES):
                            last = pe.matmul(ps_r[:, bank, :], w[a][:, c, k, :], ht[b][:, k, :], start=(k == 0 and n == 0), stop=(k == KC - 1 and n == 2))
                    last.then_inc(done, 1)

                def multiply_down(g, c, first):
                    pe.wait_ge(inner_lo, CHUNKS * g + c + 1)
                    if first:
                        pe.wait_ge(w_lo, 3 * c + 3)
                    for tt in range(4):
                        if c == 0 and not first:
                            pe.wait_ge(x_done, 4 * (g - 1) + tt + 1)
                        for n, (a, b) in enumerate(PASSES):
                            last = pe.matmul(ps_y[:, tt, :], inner[c % 2][a][:, tt * P:(tt + 1) * P], down[b][:, c, :],
                                             start=(c == 0 and n == 0), stop=(c == CHUNKS - 1 and n == 2))
                        if c == CHUNKS - 1:
                            last.then_inc(y_done, 1)
                    if c < CHUNKS - 1:
                        last.then_inc(down_used, 1)

                def group(g, first, last):
                    for c in range(CHUNKS):
                        if c == 0:
                            pe.wait_ge(h_lo, 4 * g + 4)
                        for n, (w, read, done) in enumerate(((gate, silu_done, gate_done), (up, prod_done, up_done))):
                            if first:
                                pe.wait_ge(w_lo, 3 * c + n + 1)
                            if c >= 2:
                                pe.wait_ge(read, CHUNKS * g + c - 1)
                            project(w, c, (2 * c + n) % 4, done)
                        if c >= 1:
                            multiply_down(g, c - 1, first)
                    if not last:
                        flip(g + 1)
                    multiply_down(g, CHUNKS - 1, first)

                groups(pe, group)


def lay_out(inputs):
    import numpy as np

    def a(name):
        return np.asarray(inputs[name])

    def rows(w, n):
        return np.ascontiguousarray(w.T.reshape(-1, P, n, w.shape[0] // n).transpose(2, 1, 0, 3))

    def padded(w):
        return np.concatenate([w, np.zeros((CHUNKS * P - INTER, w.shape[1]), w.dtype)], axis=0)

    def kv_weights():
        down = np.concatenate([a("L1_attn_Wk_down").T, a("L1_attn_Wv_down").T], axis=1)
        by_row = [w.reshape(-1, P, w.shape[1]).transpose(1, 0, 2).reshape(P, -1) for w in (down, a("L1_attn_Wk_up").T, a("L1_attn_Wv_up").T)]
        return np.concatenate(by_row, axis=1).reshape(P, TILES, KV_PIECE).transpose(1, 0, 2)

    arrays = {
        "in_x": a("L0_attn_data").reshape(TOKENS, HID),
        "in_mask_t": a("L0_attn_mask").T,
        "in_w0_t": a("L0_attn_weight").T,
        "in_bias0": a("L0_attn_bias"),
        "in_router_t": a("L0_ffn_router_weight").T,
        "in_router_bias": a("L0_ffn_router_bias"),
        "in_expert_bias": a("L0_ffn_expert_bias"),
        "in_kv_weights": kv_weights(),
        "in_wq_g": rows(a("L1_attn_Wq"), KV_HEADS),
        "in_wo_g": a("L1_attn_Wo").T.reshape(KV_HEADS, GROUP, HEAD, HID).transpose(0, 2, 1, 3),
        "in_gate_c": rows(padded(a("L1_ffn_gate_w")), CHUNKS).reshape(CHUNKS, P, HID),
        "in_up_c": rows(padded(a("L1_ffn_up_w")), CHUNKS).reshape(CHUNKS, P, HID),
        "in_down_c": padded(a("L1_ffn_down_w").T).reshape(CHUNKS, P, HID),
        "in_scales": np.stack([a("L1_ffn_gate_scale"), a("L1_ffn_up_scale"), a("L1_ffn_down_scale")]),
    }
    return {name: np.ascontiguousarray(v) for name, v in arrays.items()}


def kernel(**inputs):
    import concourse.bacc as bacc
    from concourse.bass_utils import run_bass_kernel_spmd

    nc = bacc.Bacc("TRN2", target_bir_lowering=False, num_devices=1)
    arrays = lay_out(inputs)
    args = [nc.dram_tensor(name, a.shape, mybir.dt.from_np(a.dtype), kind="ExternalInput").ap() for name, a in arrays.items()]
    out = nc.dram_tensor("out", (TOKENS, HID), F32, kind="ExternalOutput").ap()
    build(nc, *args, out)
    result = run_bass_kernel_spmd(nc, [arrays], core_ids=[0])
    return result.results[0]["out"].reshape(BATCH, SEQ, HID)
```
